# Optimizing a Trainium2 kernel written in Bass

```python
import numpy as np
import jax
import jax.numpy as jnp

def _softmax(x, axis=-1):
    return jax.nn.softmax(x, axis=axis)

def _gelu(x):
    return jax.nn.gelu(x, approximate=True)

def _silu(x):
    return jax.nn.silu(x)

def _sigmoid(x):
    return jax.nn.sigmoid(x)

def _layernorm(x, axis=-1, eps=1e-05):
    m = jnp.mean(x, axis=axis, keepdims=True)
    v = jnp.var(x, axis=axis, keepdims=True)
    return (x - m) / jnp.sqrt(v + eps)

def _scatter_add(tgt, idx, src, axis=0):
    return tgt.at[idx].add(src)

def _segment_sum(src, seg, n):
    return jax.ops.segment_sum(src, seg, n)
kernel_name = 'mk_conv_attn_hybrid_d4_conv_nchw512_r4_bdd4ac'

def setup_inputs(seed: int=0):
    np.random.seed(seed)
    _w = jnp.asarray

    def _rec_inputs():
        import jax
        import jax.numpy as jnp
        _gk = jax.random.key(seed)
        x = -0.0002928 + 1 * jax.random.normal(jax.random.fold_in(_gk, 1), (2, 128, 16, 16), jnp.float32)
        return x
    x = _rec_inputs()

    def _L0_conv_setup():
        import jax, jax.numpy as jnp
        import numpy as np
        C = 128
        C8 = C // 8
        key = jax.random.key(seed)
        ks = jax.random.split(key, 7)
        b, c, h, w = (2, C, 16, 16)
        x = jax.random.normal(ks[0], (b, c, h, w), dtype=jnp.float32)

        def conv_init(k, out_c, in_c):
            bound = 1.0 / np.sqrt(in_c)
            kw, kb = jax.random.split(k)
            W = jax.random.uniform(kw, (out_c, in_c), jnp.float32, -bound, bound)
            bvec = jax.random.uniform(kb, (out_c,), jnp.float32, -bound, bound)
            return (W, bvec)
        wq, bq = conv_init(ks[1], C8, c)
        wk, bk = conv_init(ks[2], C8, c)
        wv, bv = conv_init(ks[3], c, c)
        gamma_pos = jnp.full((1,), 0.5, jnp.float32)
        gamma_chan = jnp.full((1,), 0.5, jnp.float32)
        alpha = jnp.full((1,), 0.5, jnp.float32)
        beta = jnp.full((1,), 0.5, jnp.float32)
        return {'x': x, 'wq': wq, 'bq': bq, 'wk': wk, 'bk': bk, 'wv': wv, 'bv': bv, 'gamma_pos': gamma_pos, 'gamma_chan': gamma_chan, 'alpha': alpha, 'beta': beta}
    _L0_conv_all = _L0_conv_setup()
    _L0_conv_in = {k: v for k, v in _L0_conv_all.items() if k in ('wq', 'bq', 'wk', 'bk', 'wv', 'bv', 'gamma_pos', 'gamma_chan', 'alpha', 'beta')}
    del _L0_conv_all

    def _L1_conv_setup():
        import jax, jax.numpy as jnp
        import numpy as np
        from jax import lax

        def _get_mu(x):
            bs, depth, h, w = x.shape
            ix = jnp.arange(1, h + 1, dtype=x.dtype).reshape(1, 1, h, 1)
            iy = jnp.arange(1, w + 1, dtype=x.dtype).reshape(1, 1, 1, w)
            sumX = jnp.maximum(x.sum((2, 3)), 1e-09)
            mu_x = jnp.maximum(jnp.round((ix * x).sum((2, 3)) / sumX), 1.0)
            mu_y = jnp.maximum(jnp.round((iy * x).sum((2, 3)) / sumX), 1.0)
            lin = jnp.linspace(-1.0, 1.0, h, dtype=x.dtype)
            mu_xg = lin[(mu_x - 1.0).astype(jnp.int32)]
            mu_yg = lin[(mu_y - 1.0).astype(jnp.int32)]
            return (mu_xg, mu_yg)

        def _get_mask(x, mask_weight, filt):
            bs, depth, h, w = x.shape
            mu_x, mu_y = _get_mu(x)
            posX = jnp.linspace(-1.0, 1.0, h, dtype=x.dtype).reshape(1, 1, h, 1)
            posY = jnp.linspace(-1.0, 1.0, w, dtype=x.dtype).reshape(1, 1, 1, w)
            m = jnp.abs(posX - mu_x[:, :, None, None]) + jnp.abs(posY - mu_y[:, :, None, None])
            m = 1.0 - m * mask_weight.reshape(1, depth, 1, 1)
            m = jnp.maximum(m, -1.0)
            m = jnp.where(filt.reshape(1, depth, 1, 1) == 1.0, m, 1.0)
            return m
        key = jax.random.key(seed)
        k1, k2, k3, k4 = jax.random.split(key, 4)
        bs, depth, h, w = (32, 128, 28, 28)
        out_c, kh, kw = (128, 3, 3)
        x = jax.random.uniform(k1, (bs, depth, h, w), dtype=jnp.float32)
        weight = jax.random.normal(k2, (out_c, depth, kh, kw), dtype=jnp.float32) * 0.02
        bias = jax.random.normal(k3, (out_c,), dtype=jnp.float32) * 0.02
        mask_weight = jax.random.uniform(k4, (depth,), dtype=jnp.float32)
        filt = jnp.ones((depth, 1), dtype=jnp.float32)
        return {'x': x, 'weight': weight, 'bias': bias, 'mask_weight': mask_weight, 'filter': filt, 'padding': 1}
    _L1_conv_all = _L1_conv_setup()
    _L1_conv_in = {k: v for k, v in _L1_conv_all.items() if k in ('weight', 'bias', 'mask_weight', 'filter')}
    del _L1_conv_all

    def _L2_attn_setup():
        import jax, jax.numpy as jnp
        import numpy as np
        from jax.scipy.special import logsumexp
        D_MODEL = 128
        NHEAD = 8
        BATCH = 2
        SEQ = 256

        def _safe_log_relu(v):
            pos = v > 0
            return jnp.where(pos, jnp.log(jnp.where(pos, v, 1.0)), -jnp.inf)

        def _split_heads(t, h):
            b, l, hd = t.shape
            return t.reshape(b, l, h, hd // h).transpose(0, 2, 1, 3)
        key = jax.random.key(seed)
        ks = jax.random.split(key, 9)
        s = 1.0 / np.sqrt(D_MODEL)
        x = jax.random.normal(ks[0], (BATCH, SEQ, D_MODEL), jnp.float32)
        mk = lambda k: jax.random.normal(k, (D_MODEL, D_MODEL), jnp.float32) * s
        mb = lambda k: jax.random.normal(k, (D_MODEL,), jnp.float32) * 0.02
        return {'x': x, 'W_Q': mk(ks[1]), 'b_Q': mb(ks[2]), 'W_K': mk(ks[3]), 'b_K': mb(ks[4]), 'W_V': mk(ks[5]), 'b_V': mb(ks[6]), 'W_O': mk(ks[7]), 'b_O': mb(ks[8])}
    _L2_attn_all = _L2_attn_setup()
    _L2_attn_in = {k: v for k, v in _L2_attn_all.items() if k in ('W_Q', 'b_Q', 'W_K', 'b_K', 'W_V', 'b_V', 'W_O', 'b_O')}
    del _L2_attn_all

    def _L2_ffn_setup():
        import jax, jax.numpy as jnp
        import numpy as np
        B, S, D, H, E = (4, 512, 128, 256, 8)
        key = jax.random.key(seed)
        ks = jax.random.split(key, 4)
        x = jax.random.normal(ks[0], (B, S, D), jnp.float32)
        Wr = jax.random.normal(ks[1], (E, D), jnp.float32) * 0.02
        br = jnp.zeros((E,), jnp.float32)
        W1 = jax.random.normal(ks[2], (E, D, H), jnp.float32) * 0.02
        b1 = jnp.zeros((E, H), jnp.float32)
        W2 = jax.random.normal(ks[3], (E, H, D), jnp.float32) * 0.02
        b2 = jnp.zeros((E, D), jnp.float32)
        return {'x': x, 'Wr': Wr, 'br': br, 'W1': W1, 'b1': b1, 'W2': W2, 'b2': b2}
    _L2_ffn_all = _L2_ffn_setup()
    _L2_ffn_in = {k: v for k, v in _L2_ffn_all.items() if k in ('Wr', 'br', 'W1', 'b1', 'W2', 'b2')}
    del _L2_ffn_all

    def _L3_attn_setup():
        import jax, jax.numpy as jnp
        import numpy as np
        B, S, E = (8, 256, 128)
        H = 8
        D = E // H
        FFN = 512
        WINDOW = 5
        EPS = 1e-05

        def _mha(x, in_w, in_b, out_w, out_b, mask=None):
            b, s, e = x.shape
            qkv = x @ in_w.T + in_b
            q, k, v = jnp.split(qkv, 3, axis=-1)

            def heads(t):
                return t.reshape(b, s, H, D).transpose(0, 2, 1, 3)
            q, k, v = (heads(q), heads(k), heads(v))
            scores = jnp.einsum('bhsd,bhtd->bhst', q, k) / np.sqrt(D).astype(x.dtype)
            if mask is not None:
                scores = jnp.where(mask[None, None], -jnp.inf, scores)
            attn = jax.nn.softmax(scores, axis=-1)
            out = jnp.einsum('bhst,bhtd->bhsd', attn, v)
            out = out.transpose(0, 2, 1, 3).reshape(b, s, e)
            return out @ out_w.T + out_b

        def _layernorm(x, g, b):
            mu = jnp.mean(x, axis=-1, keepdims=True)
            var = jnp.mean(jnp.square(x - mu), axis=-1, keepdims=True)
            return (x - mu) * jax.lax.rsqrt(var + EPS) * g + b
        key = jax.random.key(seed)
        ks = jax.random.split(key, 8)
        w = 0.02
        return {'x': jax.random.normal(ks[0], (B, S, E), jnp.float32), 'l_in_w': jax.random.normal(ks[1], (3 * E, E), jnp.float32) * w, 'l_in_b': jnp.zeros((3 * E,), jnp.float32), 'l_out_w': jax.random.normal(ks[2], (E, E), jnp.float32) * w, 'l_out_b': jnp.zeros((E,), jnp.float32), 'g_in_w': jax.random.normal(ks[3], (3 * E, E), jnp.float32) * w, 'g_in_b': jnp.zeros((3 * E,), jnp.float32), 'g_out_w': jax.random.normal(ks[4], (E, E), jnp.float32) * w, 'g_out_b': jnp.zeros((E,), jnp.float32), 'ffn_w1': jax.random.normal(ks[5], (FFN, E), jnp.float32) * w, 'ffn_b1': jnp.zeros((FFN,), jnp.float32), 'ffn_w2': jax.random.normal(ks[6], (E, FFN), jnp.float32) * w, 'ffn_b2': jnp.zeros((E,), jnp.float32), 'ln1_g': jnp.ones((E,), jnp.float32), 'ln1_b': jnp.zeros((E,), jnp.float32), 'ln2_g': jnp.ones((E,), jnp.float32), 'ln2_b': jnp.zeros((E,), jnp.float32)}
    _L3_attn_all = _L3_attn_setup()
    _L3_attn_in = {k: v for k, v in _L3_attn_all.items() if k in ('l_in_w', 'l_in_b', 'l_out_w', 'l_out_b', 'g_in_w', 'g_in_b', 'g_out_w', 'g_out_b', 'ffn_w1', 'ffn_b1', 'ffn_w2', 'ffn_b2', 'ln1_g', 'ln1_b', 'ln2_g', 'ln2_b')}
    del _L3_attn_all

    def _L3_ffn_setup():
        import jax, jax.numpy as jnp
        import numpy as np
        E = 16
        K = 4
        NEG = jnp.float32(-1e+20)

        def _swiglu(x, w1, w2, w3):
            a = x @ w1
            return a * jax.nn.sigmoid(a) * (x @ w2) @ w3
        key = jax.random.key(seed)
        ks = jax.random.split(key, 9)
        B, S, D, H = (32, 128, 128, 1365)
        s = 0.02
        return {'x': jax.random.normal(ks[0], (B, S, D), jnp.float32), 'gate_w': jax.random.normal(ks[1], (D, E), jnp.float32) * s, 'routing_bias': jnp.zeros((E,), jnp.float32), 'w1': jax.random.normal(ks[2], (E, D, H), jnp.float32) * s, 'w2': jax.random.normal(ks[3], (E, D, H), jnp.float32) * s, 'w3': jax.random.normal(ks[4], (E, H, D), jnp.float32) * s, 'sw1': jax.random.normal(ks[5], (D, H), jnp.float32) * s, 'sw2': jax.random.normal(ks[6], (D, H), jnp.float32) * s, 'sw3': jax.random.normal(ks[7], (H, D), jnp.float32) * s}
    _L3_ffn_all = _L3_ffn_setup()
    _L3_ffn_in = {k: v for k, v in _L3_ffn_all.items() if k in ('gate_w', 'routing_bias', 'w1', 'w2', 'w3', 'sw1', 'sw2', 'sw3')}
    del _L3_ffn_all
    return {'x': x, 'L0_conv_wq': _L0_conv_in['wq'], 'L0_conv_bq': _L0_conv_in['bq'], 'L0_conv_wk': _L0_conv_in['wk'], 'L0_conv_bk': _L0_conv_in['bk'], 'L0_conv_wv': _L0_conv_in['wv'], 'L0_conv_bv': _L0_conv_in['bv'], 'L0_conv_gamma_pos': _L0_conv_in['gamma_pos'], 'L0_conv_gamma_chan': _L0_conv_in['gamma_chan'], 'L0_conv_alpha': _L0_conv_in['alpha'], 'L0_conv_beta': _L0_conv_in['beta'], 'L1_conv_weight': _L1_conv_in['weight'], 'L1_conv_bias': _L1_conv_in['bias'], 'L1_conv_mask_weight': _L1_conv_in['mask_weight'], 'L1_conv_filter': _L1_conv_in['filter'], 'L2_attn_W_Q': _L2_attn_in['W_Q'], 'L2_attn_b_Q': _L2_attn_in['b_Q'], 'L2_attn_W_K': _L2_attn_in['W_K'], 'L2_attn_b_K': _L2_attn_in['b_K'], 'L2_attn_W_V': _L2_attn_in['W_V'], 'L2_attn_b_V': _L2_attn_in['b_V'], 'L2_attn_W_O': _L2_attn_in['W_O'], 'L2_attn_b_O': _L2_attn_in['b_O'], 'L2_ffn_Wr': _L2_ffn_in['Wr'], 'L2_ffn_br': _L2_ffn_in['br'], 'L2_ffn_W1': _L2_ffn_in['W1'], 'L2_ffn_b1': _L2_ffn_in['b1'], 'L2_ffn_W2': _L2_ffn_in['W2'], 'L2_ffn_b2': _L2_ffn_in['b2'], 'L3_attn_l_in_w': _L3_attn_in['l_in_w'], 'L3_attn_l_in_b': _L3_attn_in['l_in_b'], 'L3_attn_l_out_w': _L3_attn_in['l_out_w'], 'L3_attn_l_out_b': _L3_attn_in['l_out_b'], 'L3_attn_g_in_w': _L3_attn_in['g_in_w'], 'L3_attn_g_in_b': _L3_attn_in['g_in_b'], 'L3_attn_g_out_w': _L3_attn_in['g_out_w'], 'L3_attn_g_out_b': _L3_attn_in['g_out_b'], 'L3_attn_ffn_w1': _L3_attn_in['ffn_w1'], 'L3_attn_ffn_b1': _L3_attn_in['ffn_b1'], 'L3_attn_ffn_w2': _L3_attn_in['ffn_w2'], 'L3_attn_ffn_b2': _L3_attn_in['ffn_b2'], 'L3_attn_ln1_g': _L3_attn_in['ln1_g'], 'L3_attn_ln1_b': _L3_attn_in['ln1_b'], 'L3_attn_ln2_g': _L3_attn_in['ln2_g'], 'L3_attn_ln2_b': _L3_attn_in['ln2_b'], 'L3_ffn_gate_w': _L3_ffn_in['gate_w'], 'L3_ffn_routing_bias': _L3_ffn_in['routing_bias'], 'L3_ffn_w1': _L3_ffn_in['w1'], 'L3_ffn_w2': _L3_ffn_in['w2'], 'L3_ffn_w3': _L3_ffn_in['w3'], 'L3_ffn_sw1': _L3_ffn_in['sw1'], 'L3_ffn_sw2': _L3_ffn_in['sw2'], 'L3_ffn_sw3': _L3_ffn_in['sw3']}

def reference(x, L0_conv_wq, L0_conv_bq, L0_conv_wk, L0_conv_bk, L0_conv_wv, L0_conv_bv, L0_conv_gamma_pos, L0_conv_gamma_chan, L0_conv_alpha, L0_conv_beta, L1_conv_weight, L1_conv_bias, L1_conv_mask_weight, L1_conv_filter, L2_attn_W_Q, L2_attn_b_Q, L2_attn_W_K, L2_attn_b_K, L2_attn_W_V, L2_attn_b_V, L2_attn_W_O, L2_attn_b_O, L2_ffn_Wr, L2_ffn_br, L2_ffn_W1, L2_ffn_b1, L2_ffn_W2, L2_ffn_b2, L3_attn_l_in_w, L3_attn_l_in_b, L3_attn_l_out_w, L3_attn_l_out_b, L3_attn_g_in_w, L3_attn_g_in_b, L3_attn_g_out_w, L3_attn_g_out_b, L3_attn_ffn_w1, L3_attn_ffn_b1, L3_attn_ffn_w2, L3_attn_ffn_b2, L3_attn_ln1_g, L3_attn_ln1_b, L3_attn_ln2_g, L3_attn_ln2_b, L3_ffn_gate_w, L3_ffn_routing_bias, L3_ffn_w1, L3_ffn_w2, L3_ffn_w3, L3_ffn_sw1, L3_ffn_sw2, L3_ffn_sw3):
    import jax
    import jax.numpy as jnp

    def _L0_conv_ref(x, wq, bq, wk, bk, wv, bv, gamma_pos, gamma_chan, alpha, beta):
        import jax, jax.numpy as jnp
        import numpy as np
        C = 128
        C8 = C // 8
        b, c, h, w = x.shape
        n = h * w
        xf = x.reshape(b, c, n)
        q = jnp.einsum('oc,bcn->bon', wq, xf) + bq[None, :, None]
        k = jnp.einsum('oc,bcn->bon', wk, xf) + bk[None, :, None]
        v = jnp.einsum('oc,bcn->bon', wv, xf) + bv[None, :, None]
        energy = jnp.einsum('bdi,bdj->bij', q, k)
        att = jax.nn.softmax(energy, axis=-1)
        pos_out = jnp.einsum('bcj,bij->bci', v, att).reshape(b, c, h, w)
        pos_att = gamma_pos * pos_out + x
        energy_c = jnp.einsum('bin,bjn->bij', xf, xf)
        energy_new = jnp.max(energy_c, axis=-1, keepdims=True) - energy_c
        att_c = jax.nn.softmax(energy_new, axis=-1)
        chan_out = jnp.einsum('bij,bjn->bin', att_c, xf).reshape(b, c, h, w)
        chan_att = gamma_chan * chan_out + x
        return alpha * pos_att + beta * chan_att + x

    def _L1_conv_ref(x, weight, bias, mask_weight, filter, padding):
        import jax, jax.numpy as jnp
        import numpy as np
        from jax import lax

        def _get_mu(x):
            bs, depth, h, w = x.shape
            ix = jnp.arange(1, h + 1, dtype=x.dtype).reshape(1, 1, h, 1)
            iy = jnp.arange(1, w + 1, dtype=x.dtype).reshape(1, 1, 1, w)
            sumX = jnp.maximum(x.sum((2, 3)), 1e-09)
            mu_x = jnp.maximum(jnp.round((ix * x).sum((2, 3)) / sumX), 1.0)
            mu_y = jnp.maximum(jnp.round((iy * x).sum((2, 3)) / sumX), 1.0)
            lin = jnp.linspace(-1.0, 1.0, h, dtype=x.dtype)
            mu_xg = lin[(mu_x - 1.0).astype(jnp.int32)]
            mu_yg = lin[(mu_y - 1.0).astype(jnp.int32)]
            return (mu_xg, mu_yg)

        def _get_mask(x, mask_weight, filt):
            bs, depth, h, w = x.shape
            mu_x, mu_y = _get_mu(x)
            posX = jnp.linspace(-1.0, 1.0, h, dtype=x.dtype).reshape(1, 1, h, 1)
            posY = jnp.linspace(-1.0, 1.0, w, dtype=x.dtype).reshape(1, 1, 1, w)
            m = jnp.abs(posX - mu_x[:, :, None, None]) + jnp.abs(posY - mu_y[:, :, None, None])
            m = 1.0 - m * mask_weight.reshape(1, depth, 1, 1)
            m = jnp.maximum(m, -1.0)
            m = jnp.where(filt.reshape(1, depth, 1, 1) == 1.0, m, 1.0)
            return m
        mask = _get_mask(x, mask_weight, filter)
        x_relu = jnp.maximum(x * mask, 0.0)
        out = lax.conv_general_dilated(x_relu, weight, window_strides=(1, 1), padding=[(padding, padding), (padding, padding)], dimension_numbers=('NCHW', 'OIHW', 'NCHW'))
        return out + bias.reshape(1, -1, 1, 1)

    def _L2_attn_ref(x, W_Q, b_Q, W_K, b_K, W_V, b_V, W_O, b_O):
        import jax, jax.numpy as jnp
        import numpy as np
        from jax.scipy.special import logsumexp
        D_MODEL = 128
        NHEAD = 8
        BATCH = 2
        SEQ = 256

        def _safe_log_relu(v):
            pos = v > 0
            return jnp.where(pos, jnp.log(jnp.where(pos, v, 1.0)), -jnp.inf)

        def _split_heads(t, h):
            b, l, hd = t.shape
            return t.reshape(b, l, h, hd // h).transpose(0, 2, 1, 3)
        Q = _split_heads(x @ W_Q.T + b_Q, NHEAD)
        K = _split_heads(x @ W_K.T + b_K, NHEAD)
        V = _split_heads(x @ W_V.T + b_V, NHEAD)
        log_B = logsumexp(Q + logsumexp(K, axis=-2, keepdims=True), axis=-1)
        log_V_plus = _safe_log_relu(V)[..., None, :]
        log_V_minus = _safe_log_relu(-V)[..., None, :]
        lse_KV_plus = logsumexp(K[..., :, :, None] + log_V_plus, axis=-3)
        lse_KV_minus = logsumexp(K[..., :, :, None] + log_V_minus, axis=-3)
        log_A_plus = logsumexp(Q[..., None] + lse_KV_plus[..., None, :, :], axis=-2)
        log_A_minus = logsumexp(Q[..., None] + lse_KV_minus[..., None, :, :], axis=-2)
        heads = jnp.exp(log_A_plus - log_B[..., None]) - jnp.exp(log_A_minus - log_B[..., None])
        b, h, l, dv = heads.shape
        joined = heads.transpose(0, 2, 1, 3).reshape(b, l, h * dv)
        return joined @ W_O.T + b_O

    def _L2_ffn_ref(x, Wr, br, W1, b1, W2, b2):
        import jax, jax.numpy as jnp
        import numpy as np
        B, S, D, H, E = (4, 512, 128, 256, 8)
        b, s, d = x.shape
        n = b * s
        e = Wr.shape[0]
        xf = x.reshape(n, d)
        logits = xf @ Wr.T + br
        probs = jax.nn.softmax(logits, axis=-1)
        top2_prob, top2_idx = jax.lax.top_k(probs, 2)
        comb = jnp.zeros((n, e), x.dtype).at[jnp.arange(n)[:, None], top2_idx].add(top2_prob)
        h = jax.nn.gelu(jnp.einsum('nd,edh->enh', xf, W1) + b1[:, None, :], approximate=False)
        o = jnp.einsum('enh,ehd->end', h, W2) + b2[:, None, :]
        y = jnp.einsum('ne,end->nd', comb, o)
        return y.reshape(b, s, d)

    def _L3_attn_ref(x, l_in_w, l_in_b, l_out_w, l_out_b, g_in_w, g_in_b, g_out_w, g_out_b, ffn_w1, ffn_b1, ffn_w2, ffn_b2, ln1_g, ln1_b, ln2_g, ln2_b):
        import jax, jax.numpy as jnp
        import numpy as np
        B, S, E = (8, 256, 128)
        H = 8
        D = E // H
        FFN = 512
        WINDOW = 5
        EPS = 1e-05

        def _mha(x, in_w, in_b, out_w, out_b, mask=None):
            b, s, e = x.shape
            qkv = x @ in_w.T + in_b
            q, k, v = jnp.split(qkv, 3, axis=-1)

            def heads(t):
                return t.reshape(b, s, H, D).transpose(0, 2, 1, 3)
            q, k, v = (heads(q), heads(k), heads(v))
            scores = jnp.einsum('bhsd,bhtd->bhst', q, k) / np.sqrt(D).astype(x.dtype)
            if mask is not None:
                scores = jnp.where(mask[None, None], -jnp.inf, scores)
            attn = jax.nn.softmax(scores, axis=-1)
            out = jnp.einsum('bhst,bhtd->bhsd', attn, v)
            out = out.transpose(0, 2, 1, 3).reshape(b, s, e)
            return out @ out_w.T + out_b

        def _layernorm(x, g, b):
            mu = jnp.mean(x, axis=-1, keepdims=True)
            var = jnp.mean(jnp.square(x - mu), axis=-1, keepdims=True)
            return (x - mu) * jax.lax.rsqrt(var + EPS) * g + b
        s = x.shape[1]
        idx = jnp.arange(s)
        local_mask = jnp.abs(idx[:, None] - idx[None, :]) > WINDOW
        local_out = _mha(x, l_in_w, l_in_b, l_out_w, l_out_b, mask=local_mask)
        global_out = _mha(x, g_in_w, g_in_b, g_out_w, g_out_b)
        x = x + local_out + global_out
        x = _layernorm(x, ln1_g, ln1_b)
        ffn = jax.nn.relu(x @ ffn_w1.T + ffn_b1) @ ffn_w2.T + ffn_b2
        x = _layernorm(x + ffn, ln2_g, ln2_b)
        return x

    def _L3_ffn_ref(x, gate_w, routing_bias, w1, w2, w3, sw1, sw2, sw3):
        import jax, jax.numpy as jnp
        import numpy as np
        E = 16
        K = 4
        NEG = jnp.float32(-1e+20)

        def _swiglu(x, w1, w2, w3):
            a = x @ w1
            return a * jax.nn.sigmoid(a) * (x @ w2) @ w3
        gate_out = x @ gate_w + routing_bias
        top_v, top_i = jax.lax.top_k(gate_out, K)
        chosen = jax.nn.one_hot(top_i, E, dtype=x.dtype).sum(axis=-2)
        masked = jnp.where(chosen > 0, gate_out, NEG)
        probs = jax.nn.softmax(masked, axis=-1)
        weights = probs * chosen
        out = _swiglu(x, sw1, sw2, sw3)
        for e in range(E):
            out = out + _swiglu(x, w1[e], w2[e], w3[e]) * weights[..., e:e + 1]
        return out

    def _gn(v, G=32, eps=1e-05):
        B_, C_, H_, W_ = v.shape
        g = v.reshape(B_, G, C_ // G, H_, W_)
        m = jnp.mean(g, axis=(2, 3, 4), keepdims=True)
        s = jnp.var(g, axis=(2, 3, 4), keepdims=True)
        return ((g - m) / jnp.sqrt(s + eps)).reshape(v.shape)

    def _ln_c(v, eps=1e-06):
        m = jnp.mean(v, axis=1, keepdims=True)
        s = jnp.var(v, axis=1, keepdims=True)
        return (v - m) / jnp.sqrt(s + eps)

    def _ln_t(v, eps=1e-05):
        m = jnp.mean(v, axis=-1, keepdims=True)
        s = jnp.var(v, axis=-1, keepdims=True)
        return (v - m) / jnp.sqrt(s + eps)

    def _to_tokens(v):
        B_, C_, H_, W_ = v.shape
        return v.reshape(B_, C_, H_ * W_).transpose(0, 2, 1)

    def _from_tokens(t, like):
        B_, C_, H_, W_ = like.shape
        return t.transpose(0, 2, 1).reshape(B_, C_, H_, W_)
    x = _L0_conv_ref(x, L0_conv_wq, L0_conv_bq, L0_conv_wk, L0_conv_bk, L0_conv_wv, L0_conv_bv, L0_conv_gamma_pos, L0_conv_gamma_chan, L0_conv_alpha, L0_conv_beta)
    x = x + _L1_conv_ref(_gn(x), L1_conv_weight, L1_conv_bias, L1_conv_mask_weight, L1_conv_filter, 1)
    t = _to_tokens(x)
    t = t + _L2_attn_ref(_ln_t(t), L2_attn_W_Q, L2_attn_b_Q, L2_attn_W_K, L2_attn_b_K, L2_attn_W_V, L2_attn_b_V, L2_attn_W_O, L2_attn_b_O)
    t = t + _L2_ffn_ref(_ln_t(t), L2_ffn_Wr, L2_ffn_br, L2_ffn_W1, L2_ffn_b1, L2_ffn_W2, L2_ffn_b2)
    t = t + _L3_attn_ref(_ln_t(t), L3_attn_l_in_w, L3_attn_l_in_b, L3_attn_l_out_w, L3_attn_l_out_b, L3_attn_g_in_w, L3_attn_g_in_b, L3_attn_g_out_w, L3_attn_g_out_b, L3_attn_ffn_w1, L3_attn_ffn_b1, L3_attn_ffn_w2, L3_attn_ffn_b2, L3_attn_ln1_g, L3_attn_ln1_b, L3_attn_ln2_g, L3_attn_ln2_b)
    t = t + _L3_ffn_ref(_ln_t(t), L3_ffn_gate_w, L3_ffn_routing_bias, L3_ffn_w1, L3_ffn_w2, L3_ffn_w3, L3_ffn_sw1, L3_ffn_sw2, L3_ffn_sw3)
    x = _from_tokens(t, x)
    return x

_drawn_inputs = setup_inputs


def setup_inputs(seed=0):
    import zlib

    import numpy as np

    out = dict(_drawn_inputs(seed))
    spreads = {'L1_conv_filter': (1.0, 0.2),
     'L2_ffn_br': (0.0, 0.8),
     'L2_ffn_b1': (0.0, 0.8),
     'L2_ffn_b2': (0.0, 0.672),
     'L3_attn_l_in_b': (0.0, 0.8),
     'L3_attn_l_out_b': (0.0, 0.332),
     'L3_attn_g_in_b': (0.0, 0.8),
     'L3_attn_g_out_b': (0.0, 0.348),
     'L3_attn_ffn_b1': (0.0, 0.724),
     'L3_attn_ffn_b2': (0.0, 0.1),
     'L3_attn_ln1_g': (1.0, 0.2),
     'L3_attn_ln1_b': (0.0, 0.1),
     'L3_attn_ln2_g': (1.0, 0.2),
     'L3_attn_ln2_b': (0.0, 0.1),
     'L3_ffn_routing_bias': (0.0, 0.8)}
    factors = {'L0_conv_wq': 4.291,
     'L0_conv_bq': 8.0,
     'L0_conv_wk': 4.525,
     'L0_conv_bk': 64.0,
     'L0_conv_wv': 4.105,
     'L0_conv_bv': 7.535,
     'L1_conv_bias': 5.375,
     'L2_attn_W_Q': 3.703,
     'L2_attn_b_Q': 8.0,
     'L2_attn_W_K': 2.734,
     'L2_attn_b_K': 8.0,
     'L2_attn_b_V': 5.278,
     'L2_attn_b_O': 5.459,
     'L2_ffn_Wr': 5.289,
     'L2_ffn_W1': 8.0,
     'L2_ffn_W2': 8.0,
     'L3_attn_l_in_w': 8.0,
     'L3_attn_l_out_w': 5.975,
     'L3_attn_g_in_w': 8.0,
     'L3_attn_g_out_w': 6.934,
     'L3_attn_ffn_w1': 2.735,
     'L3_ffn_gate_w': 8.0,
     'L3_ffn_w1': 8.0,
     'L3_ffn_w2': 8.0,
     'L3_ffn_w3': 8.0,
     'L3_ffn_sw1': 8.0,
     'L3_ffn_sw2': 8.0,
     'L3_ffn_sw3': 8.0}
    for name, (base, spread) in spreads.items():
        noise = np.random.default_rng([zlib.crc32(name.encode()), seed]).standard_normal(out[name].shape)
        drawn = base * np.exp(spread * noise) if base else spread * noise
        out[name] = jnp.asarray(drawn.astype(out[name].dtype))
    for name, factor in factors.items():
        out[name] = (out[name] * factor).astype(out[name].dtype)
    return out
```

```python
from contextlib import ExitStack

import concourse.bass as bass
from concourse import mybir

F32 = mybir.dt.float32
BF16 = mybir.dt.bfloat16
ALU = mybir.AluOpType
ACT = mybir.ActivationFunctionType
AX = mybir.AxisListType

C = 128
B = 2
SIDE = 16
PIX = SIDE * SIDE
N = B * PIX
NT = N // 128
C8 = C // 8
GROUP = 4
HEADS, HD = 8, 16
E2, H2 = 8, 256
FF = 512
FT = FF // 128
E3, K3, H3 = 16, 4, 1365
HT = -(-H3 // 128)
H_LAST = H3 - (HT - 1) * 128
H_PAD = HT * 128
SLOTS = 128
MAX_CHUNKS = E3 + (K3 * N - E3) // SLOTS
PAIRS = -(-MAX_CHUNKS // 2)
BLOCKS = N // SLOTS
GROUPS = [(0, 4), (4, 8), (8, HT)]
WINDOW = 5
CREDIT = 2
EPS = 1e-5
MASKED = -1e30
ROUND = 1.5 * 2.0 ** 23

CONV_COLS = [("wq", C8), ("wk", C8), ("wv", C), ("bq", 1), ("bk", 1), ("gamma_pos", 1), ("gamma_chan", 1), ("alpha", 1),
             ("beta", 1), ("conv_bias", 1), ("mask_weight", 1), ("filter", 1)]
ATT_COLS = [("WQ", C), ("WK", C), ("WV", C), ("WO", C), ("bQ", 1), ("bK", 1), ("bV", 1), ("Wr", E2)]
EXPERT2_N = 2 * C + 2 * C + 2
L3_COLS = [("g_in", 3 * C), ("l_in", 3 * C), ("g_out", 2 * C), ("l_out", 2 * C), ("ffn1", FF), ("ffn2", FT * C),
           ("g_bq", 1), ("l_bq", 1), ("g_bk", 1), ("l_bk", 1), ("g_bv", 2), ("l_bv", 2), ("ffn_b1", FT), ("gate", E3)]
ROWS = [("bv", C), ("bO", C), ("br", E2), ("g_out_b", C), ("l_out_b", C), ("ffn_b2", C), ("ln1_g", C), ("ln1_b", C),
        ("ln2_g", C), ("ln2_b", C), ("routing_bias", E3)]


def columns(table):
    at, out = 0, {}
    for name, n in table:
        out[name] = (at, n)
        at += n
    return out, at


CONV_AT, CONV_N = columns(CONV_COLS)
ATT_AT, ATT_N = columns(ATT_COLS)
L3_AT, L3_N = columns(L3_COLS)
ROW_AT, ROW_N = columns(ROWS)

LN_ATT2, LN_FFN2, LN_ATT3, LN_MID3, LN_END3, LN_FFN3 = range(6)

GLOBAL_HEADS, LOCAL_HEADS = 2, 4
WINDOWS = [(0, 0, 128 - WINDOW), (64, 128 - WINDOW, 192 - WINDOW), (128, 192 - WINDOW, PIX)]
UNITS = []
for _b in range(B):
    UNITS += [("g", _b, t, h) for t in range(2) for h in range(0, HEADS, GLOBAL_HEADS)]
    UNITS += [("l", _b, w, h) for w in range(len(WINDOWS)) for h in range(0, HEADS, LOCAL_HEADS)]
UNITS_B = len(UNITS) // B
UNITS_G = 2 * HEADS // GLOBAL_HEADS


def build(nc, x_in, conv_w, taps_w, att_w, experts2_w, b2_w, l3_w, rows_w, sw1_in, sw2_in, sw3_in, w1_in, w2_in, w3_in, out):
    with ExitStack() as ctx:
        sems = {}

        def sem(name):
            if name not in sems:
                sems[name] = ctx.enter_context(nc.semaphore(name))
            return sems[name]

        def sb(name, shape, dt=F32):
            return ctx.enter_context(nc.sbuf_tensor(name, shape, dt))

        ROOM = 13568
        shared_room = sb("shared_room", [128, ROOM])
        used = {}

        def room(phase, shape):
            parts, n = shape[0], 1
            for m in shape[1:]:
                n *= m
            at = used.get(phase, 0)
            used[phase] = at + n
            assert used[phase] <= ROOM
            view = shared_room[0:parts, at:at + n]
            letters = "abcd"[:len(shape) - 1]
            if len(letters) == 1:
                return view
            return view.rearrange(f"p ({' '.join(letters)}) -> p {' '.join(letters)}",
                                  **dict(zip(letters, shape[1:])))

        bank = [ctx.enter_context(nc.psum_tensor(f"bank{i}", [128, 512], F32)) for i in range(8)]

        conv = sb("conv", [128, CONV_N])
        taps = room("early", [128, 9, C])
        att = sb("att", [128, ATT_N])
        b2 = sb("b2", [E2, C])
        l3 = sb("l3", [128, L3_N])
        rows = sb("rows", [128, ROW_N])

        def cc(name):
            a, n = CONV_AT[name]
            return conv[:, a:a + n]

        def ca(name):
            a, n = ATT_AT[name]
            return att[:, a:a + n]

        def c3(name):
            a, n = L3_AT[name]
            return l3[:, a:a + n]

        def row(name, mid=None):
            a, n = ROW_AT[name]
            r = rows[:, a:a + n]
            return r if mid is None else r.unsqueeze(1).broadcast_to([128, mid, n])

        ident = sb("ident", [128, 128])
        ident_bf = sb("ident_bf", [128, 128], BF16)
        band = sb("band", [128, 128], BF16)
        ones = sb("ones", [128, 128])
        group_mean = sb("group_mean", [128, 128])
        head_block = sb("head_block", [128, 128])
        head_mask = sb("head_mask", [128, HEADS])
        den_sel = sb("den_sel", [128, 128])
        ramp = sb("ramp", [128, SIDE])
        pos = sb("pos", [128, SIDE])
        before = sb("before", [128, E3, E3])
        before2 = sb("before2", [128, E2, E2])
        earlier_bf = sb("earlier_bf", [128, 128], BF16)
        ones_bf = sb("ones_bf", [128, 128], BF16)
        slot_no = sb("slot_no", [128, (BLOCKS + 1) * SLOTS])
        chunk_no = sb("chunk_no", [128, 2 * PAIRS + 1])

        x0 = room("early", [128, B, PIX])
        q0 = room("early", [C8, N])
        k0 = room("early", [C8, N])
        v0T = room("early", [128, NT, C])
        x0T = room("early", [128, NT, C])
        p0 = room("early", [128, B, 2, PIX])
        p0T = room("early", [128, B, 2, PIX])
        pc = room("early", [128, B, C])
        pcT = room("early", [128, B, C])
        nmax0 = sb("nmax0", [128, B, 2])
        sum0 = sb("sum0", [128, B, 2])
        minc = sb("minc", [128, B])
        sumc = sb("sumc", [128, B])
        mix = sb("mix", [128, 4])
        x1 = sb("x1", [128, B, PIX])
        gst = sb("gst", [128, B, 6])
        gmv = sb("gmv", [128, B, 2])
        gdev = sb("gdev", [128, B])
        gm = sb("gm", [128, B])
        gvar = sb("gvar", [128, B])
        gr = sb("gr", [128, 4, B])
        gn = room("early", [128, B, SIDE, SIDE])
        sums = sb("sums", [128, 2, B, SIDE])
        weighted = sb("weighted", [128, 2, B, SIDE])
        moment = sb("moment", [128, 2, B])
        total = sb("total", [128, B])
        mu = sb("mu", [128, 2, B])
        mask_w = sb("mask_w", [128, 1])
        dist = sb("dist", [128, 2, B, SIDE])
        mask = room("early", [128, B, SIDE, SIDE])
        pad = room("early", [128, B, SIDE + 2, SIDE + 2])
        x2 = sb("x2", [128, B, PIX])

        t2 = sb("t2", [128, NT, C])
        t3 = sb("t3", [128, NT, C])
        t4 = sb("t4", [128, NT, C])
        u3 = sb("u3", [128, NT, C])
        z3 = sb("z3", [128, NT, C])
        t5 = sb("t5", [128, NT, C])
        y = [None if k == LN_END3 else sb(f"y{k}", [128, NT, C]) for k in range(6)]
        yT = [None if k == LN_END3 else sb(f"yT{k}", [128, N]) for k in range(6)]
        lst = sb("lst", [128, NT, 6])
        lmv = sb("lmv", [128, 6, NT, 2])
        lve = sb("lve", [128, 6, NT])
        lln = sb("lln", [128, 6, NT])
        lr0 = sb("lr0", [128, 6, NT])
        lra = sb("lra", [128, 2, NT])
        lr = sb("lr", [128, 6, NT])

        kmax = sb("kmax", [128, B])
        knmax = sb("knmax", [128, B])
        kq = sb("kq", [128, B])
        kqb = room("early", [128, B, 128])
        ek = room("early", [128, B, PIX])
        sek = sb("sek", [128, B])
        ekT = room("early", [128, NT, C])
        v2 = room("early", [128, NT, C])
        kv = room("early", [128, B, C])
        ksum = room("early", [128, B, C])
        qmax = sb("qmax", [128, NT * HEADS])
        qs = room("early", [128, NT * HEADS, HD])
        eq = room("early", [128, NT, C])
        eqT = room("early", [128, N])
        rden2 = room("early", [128, N])
        heads2 = room("early", [128, N])
        heads2b = room("early", [128, N])

        lg2 = sb("lg2", [128, NT, E2])
        m2 = sb("m2", [128, NT])
        e2 = sb("e2", [128, NT, E2])
        s2 = sb("s2", [128, NT])
        pr2 = sb("pr2", [128, NT, E2])
        cmp2 = sb("cmp2", [128, 2, E2, E2])
        rank2 = sb("rank2", [128, NT, E2])
        comb2 = sb("comb2", [128, NT, E2])
        comb2T = sb("comb2T", [E2, N])
        ew2 = [sb(f"ew2_{p}", [128, EXPERT2_N]) for p in range(2)]
        h2 = sb("h2", [128, 4, N])

        q3 = [room("keys", [128, N]) for s in "gl"]
        k3 = [room("keys", [128, N]) for s in "gl"]
        km3 = [[room("keys", [128, HEADS, PIX]) for b in range(B)] for s in "gl"]
        vg = sb("vg", [128, NT, HEADS, 32])
        vl = sb("vl", [128, B * len(WINDOWS), HEADS, 32])
        nmax3 = sb("nmax3", [128, len(UNITS), 4])
        p3 = sb("p3", [128, 2, 512])
        p3T = room("keys", [128, 2, 512])
        o3 = sb("o3", [128, 2, 512])
        rd3 = sb("rd3", [128, 2, 512])
        on3 = sb("on3", [128, 2, 512])
        ob3 = sb("ob3", [128, B, 2, 2, PIX])
        hf3 = room("keys", [128, FT, N])

        lg3 = sb("lg3", [128, NT, E3])
        m3 = sb("m3", [128, NT])
        e3 = sb("e3", [128, NT, E3])
        s3 = sb("s3", [128, NT])
        cmp3 = sb("cmp3", [128, 2, E3, E3])
        rank3 = sb("rank3", [128, NT, E3])
        chosen = sb("chosen", [128, NT, E3])
        chosen_bf = sb("chosen_bf", [128, NT, E3], BF16)
        weight = sb("weight", [128, NT, E3])
        place = sb("place", [128, NT, E3])
        count = sb("count", [128, E3])
        chunks = sb("chunks", [128, E3])
        first = sb("first", [128, E3])
        reach = room("mixture", [128, 2 * PAIRS + 1, E3])
        plan = sb("plan", [128, 3, 2 * PAIRS + 1])
        plan_int = sb("plan_int", [1, 2, 2 * PAIRS + 1], mybir.dt.int32)
        pairs = sb("pairs", [128, 4])
        pairs_int = sb("pairs_int", [1, 1], mybir.dt.int32)
        w1 = [sb(f"w1_{p}", [128, H_PAD]) for p in range(2)]
        w2 = [sb(f"w2_{p}", [128, H_PAD]) for p in range(2)]
        w3 = [sb(f"w3_{p}", [128, HT, C]) for p in range(2)]
        silu = room("mixture", [128, 2, 512])
        hs = room("mixture", [128, 3, N])
        pick = room("mixture", [128, 2, NT, SLOTS])
        pickw = room("mixture", [128, 2, NT, SLOTS])
        spread = room("mixture", [128, 2, N])
        he = room("mixture", [128, 2, HT, SLOTS])
        xe = room("mixture", [128, 2, SLOTS])
        ye = room("mixture", [128, 2, C])
        outT = room("mixture", [128, B, PIX])

        block = ctx.enter_context(nc.Block())

        @block.sync
        def _(sp):
            sp.dma_start(x0[:], x_in.rearrange("b c n -> c b n")).then_inc(sem("x_in"), 16)
            sp.dma_start(conv[:], conv_w).then_inc(sem("conv_in"), 16)
            sp.dma_start(rows[:], rows_w.partition_broadcast(128)).then_inc(sem("rows_in"), 16)
            sp.dma_start(taps[:], taps_w).then_inc(sem("taps_in"), 16)
            sp.dma_start(att[:], att_w).then_inc(sem("att_in"), 16)
            sp.dma_start(b2[:], b2_w).then_inc(sem("b2_in"), 16)
            sp.dma_start(l3[:], l3_w).then_inc(sem("l3_in"), 16)
            for p in range(2):
                sp.dma_start(ew2[p][:], experts2_w[p, :, :]).then_inc(sem(f"ew2_in{p}"), 16)
            with sp.Fori(0, E2 // 2 - 1) as i:
                for p in range(2):
                    sp.wait_ge(sem("expert2_mm"), CREDIT + 2 * i + p + 1)
                    sp.dma_start(ew2[p][:], experts2_w[2 * i + p + 2, :, :]).then_inc(sem(f"ew2_in{p}"), 16)

            def load(p, a1, a2, a3):
                full = (HT - 1) * 128
                sp.dma_start(w1[p][:, 0:H3], a1).then_inc(sem(f"w1_in{p}"), 16)
                sp.dma_start(w2[p][:, 0:H3], a2).then_inc(sem(f"w2_in{p}"), 16)
                sp.dma_start(w3[p][:, 0:HT - 1, :], a3[0:full, :].rearrange("(t p) d -> p t d", p=128))\
                    .then_inc(sem(f"w3_in{p}"), 16)
                sp.dma_start(w3[p][0:H_LAST, HT - 1, :], a3[full:H3, :]).then_inc(sem(f"w3_in{p}"), 16)

            load(0, sw1_in, sw2_in, sw3_in)
            sp.wait_ge(sem("plan_ready"), 1)
            n_pairs = sp.value_load(pairs_int[0:1, 0:1], min_val=1, max_val=PAIRS)
            with sp.Fori(0, n_pairs) as i:
                for p in (1, 0):
                    e = sp.value_load(plan_int[0:1, 0, bass.ds(2 * i + 1 - p, 1)], min_val=0, max_val=E3 - 1)
                    sp.wait_ge(sem("down_mm"), 2 * i + 1 - p + 1)
                    load(p, w1_in[bass.ds(e, 1), :, :].rearrange("e c h -> c (e h)"),
                         w2_in[bass.ds(e, 1), :, :].rearrange("e c h -> c (e h)"),
                         w3_in[bass.ds(e, 1), :, :].rearrange("e h d -> (e h) d"))
            sp.wait_ge(sem("out_ready"), 1)
            sp.dma_start(out.rearrange("b c n -> c b n"), outT[:]).then_inc(sem("out_stored"), 16)
            sp.wait_ge(sem("out_stored"), 16)

        @block.gpsimd
        def _(pool):
            def select(out, pattern, base, mult, op, fill):
                return nc.gpsimd.affine_select(out=out, in_=out, compare_op=op, fill=fill, base=base, pattern=pattern,
                                               channel_multiplier=mult)

            made = [0]

            def make(ins):
                made[0] += 1
                ins.then_inc(sem("pool_step"), 1)
                pool.wait_ge(sem("pool_step"), made[0])

            make(nc.gpsimd.memset(ident[:], 0.0))
            make(select(ident[:], [[-1, 128]], 0, 1, ALU.not_equal, 1.0))
            nc.gpsimd.memset(ones[:], 1.0).then_inc(sem("ident_made"), 1)
            nc.gpsimd.memset(pad[:], 0.0).then_inc(sem("pad_made"), 1)
            g = group_mean[:].rearrange("p (g c) -> p g c", c=GROUP)
            make(nc.gpsimd.memset(group_mean[:], 1.0 / GROUP))
            make(select(g, [[-GROUP, C // GROUP], [0, GROUP]], 0, 1, ALU.is_ge, 0.0))
            make(select(g, [[GROUP, C // GROUP], [0, GROUP]], GROUP - 1, -1, ALU.is_ge, 0.0))
            nc.gpsimd.iota(ramp[:], pattern=[[1, SIDE]], base=1, channel_multiplier=0,
                           allow_small_or_imprecise_dtypes=True).then_inc(sem("group_made"), 1)
            g = head_block[:].rearrange("p (g c) -> p g c", c=HD)
            make(nc.gpsimd.memset(head_block[:], 1.0))
            make(select(g, [[-HD, HEADS], [0, HD]], 0, 1, ALU.is_ge, 0.0))
            make(select(g, [[HD, HEADS], [0, HD]], HD - 1, -1, ALU.is_ge, 0.0))
            make(nc.gpsimd.memset(head_mask[:], 1.0))
            make(select(head_mask[:], [[-HD, HEADS]], 0, 1, ALU.is_ge, 0.0))
            make(select(head_mask[:], [[HD, HEADS]], HD - 1, -1, ALU.is_ge, 0.0))
            make(nc.gpsimd.memset(before2[:], 1.0))
            make(select(before2[:], [[1, E2], [-1, E2]], -1, 0, ALU.is_ge, 0.0))
            make(nc.gpsimd.memset(before[:], 1.0))
            make(select(before[:], [[1, E3], [-1, E3]], -1, 0, ALU.is_ge, 0.0))
            g = den_sel[:].rearrange("p (j c) -> p j c", c=32)
            make(nc.gpsimd.memset(den_sel[:], 0.0))
            make(select(g, [[-32, 4], [0, 32]], -HD, 1, ALU.not_equal, 1.0))
            make(nc.gpsimd.memset(band[:], 0.0))
            make(select(band[:], [[-1, 128]], WINDOW, 1, ALU.is_ge, MASKED))
            make(select(band[:], [[1, 128]], WINDOW, -1, ALU.is_ge, MASKED))
            make(nc.gpsimd.tensor_copy(ident_bf[:], ident[:]))
            make(nc.gpsimd.memset(ones_bf[:], 1.0))
            make(nc.gpsimd.memset(earlier_bf[:], 1.0))
            make(select(earlier_bf[:], [[1, 128]], -1, -1, ALU.is_ge, 0.0))
            make(nc.gpsimd.iota(slot_no[:], pattern=[[1, (BLOCKS + 1) * SLOTS]], base=0, channel_multiplier=0,
                                allow_small_or_imprecise_dtypes=True))
            make(nc.gpsimd.iota(chunk_no[:], pattern=[[1, 2 * PAIRS + 1]], base=0, channel_multiplier=0,
                                allow_small_or_imprecise_dtypes=True))
            for p in range(2):
                make(nc.gpsimd.memset(w1[p][:, H3:H_PAD], 0.0))
                make(nc.gpsimd.memset(w2[p][:, H3:H_PAD], 0.0))
            make(nc.gpsimd.memset(vg[:], 0.0))
            make(nc.gpsimd.memset(vl[:], 0.0))
            make(nc.gpsimd.memset(vg[:, :, :, HD:HD + 1], 1.0))
            nc.gpsimd.memset(vl[:, :, :, HD:HD + 1], 1.0).then_inc(sem("masks_made"), 1)
            for s in range(2):
                pool.wait_ge(sem("k3_ready"), s + 1)
                for h in range(HEADS):
                    last = nc.gpsimd.tensor_scalar(km3[s][1][:, h, :], k3[s][:, PIX:N], head_mask[:, h:h + 1], None,
                                                   ALU.mult)
                last.then_inc(sem("km3_image1"), 1)

        @block.tensor
        def _(pe):
            mm = nc.tensor.matmul
            tr = nc.tensor.transpose

            pe.sem_inc(sem("expert2_mm"), CREDIT)
            pe.sem_inc(sem("down_mm"), 1)
            pe.sem_inc(sem("scatter_mm"), 1)
            pe.sem_inc(sem("spread_mm"), 1)
            pe.wait_ge(sem("x_in"), 16)
            pe.wait_ge(sem("conv_in"), 16)
            pe.wait_ge(sem("ident_made"), 1)
            xf = x0[:].rearrange("p b n -> p (b n)")
            mm(bank[0][0:C8, :], cc("wq"), xf, start=True, stop=True).then_inc(sem("q0_mm"), 1)
            mm(bank[1][0:C8, :], cc("wk"), xf, start=True, stop=True).then_inc(sem("k0_mm"), 1)
            for t in range(NT):
                last = tr(bank[3][:, 128 * t:128 * t + 128], xf[:, 128 * t:128 * t + 128], ident[:])
            last.then_inc(sem("x0T_mm"), 1)
            for t in range(NT):
                last = mm(bank[2][:, 128 * t:128 * t + 128], xf[:, 128 * t:128 * t + 128], cc("wv"),
                          start=True, stop=True)
            last.then_inc(sem("v0_mm"), 1)
            pe.wait_ge(sem("q0_ready"), 1)
            pe.wait_ge(sem("k0_ready"), 1)
            for b in range(B):
                for t in range(2):
                    last = mm(bank[4 + b][:, PIX * t:PIX * t + PIX], q0[:, b * PIX + 128 * t:b * PIX + 128 * t + 128],
                              k0[:, b * PIX:b * PIX + PIX], start=True, stop=True)
                last.then_inc(sem("energy_mm"), 1)
            pe.wait_ge(sem("x0T_ready"), 1)
            for b in range(B):
                for t in range(2):
                    last = mm(bank[6][:, C * b:C * b + C], x0T[:, 2 * b + t, :], x0T[:, 2 * b + t, :],
                              start=(t == 0), stop=(t == 1))
            last.then_inc(sem("energyc_mm"), 1)
            pe.wait_ge(sem("v0_ready"), 1)
            for b in range(B):
                pe.wait_ge(sem("p0_ready"), 4 * b + 4)
                for j in range(2):
                    for t in range(2):
                        last = tr(bank[b][:, j * PIX + 128 * t:j * PIX + 128 * t + 128],
                                  p0[:, b, t, 128 * j:128 * j + 128], ident[:])
                last.then_inc(sem("p0T_mm"), 1)
            pe.wait_ge(sem("pc_ready"), B)
            for b in range(B):
                last = tr(bank[2][:, C * b:C * b + C], pc[:, b, :], ident[:])
            last.then_inc(sem("pcT_mm"), 1)
            pe.wait_ge(sem("pcT_ready"), 1)
            for b in range(B):
                pe.wait_ge(sem("p0T_ready"), b + 1)
                for j in range(2):
                    mm(bank[7 - 4 * b][:, 0:PIX], v0T[:, 2 * b + j, :], p0T[:, b, j, :],
                       start=(j == 0), stop=False)
                mm(bank[7 - 4 * b][:, 0:PIX], pcT[:, b, :], x0[:, b, :], start=False, stop=True)\
                    .then_inc(sem("layer0_mm"), 1)
            pe.wait_ge(sem("group_made"), 1)
            pe.wait_ge(sem("gmv_ready"), 1)
            mm(bank[0][:, 0:B], group_mean[:], gmv[:, :, 0], start=True, stop=True).then_inc(sem("gmean_mm"), 1)
            pe.wait_ge(sem("gdev_ready"), 1)
            mm(bank[1][:, 0:B], group_mean[:], gdev[:], start=True, stop=True).then_inc(sem("gvar_mm"), 1)
            pe.wait_ge(sem("taps_in"), 16)
            pe.wait_ge(sem("pad_ready"), 1)
            for k in range(9):
                i, j = k // 3, k % 3
                last = mm(bank[2][:, :], taps[:, k, :], pad[:, :, i:i + SIDE, j:j + SIDE], start=(k == 0), stop=(k == 8))
            last.then_inc(sem("conv_mm"), 1)
            pe.wait_ge(sem("x2_ready"), 1)
            x2f = x2[:].rearrange("p b n -> p (b n)")
            for t in range(NT):
                last = tr(bank[3][:, 128 * t:128 * t + 128], x2f[:, 128 * t:128 * t + 128], ident[:])
            last.then_inc(sem("t2_mm"), 1)

            def ln_transpose(k, b):
                for t in range(NT):
                    pe.wait_ge(sem(f"y{k}_ready"), t + 1)
                    tr(bank[b + t // 2][:, 128 * (t % 2):128 * (t % 2) + 128], y[k][:, t, :], ident[:]).then_inc(sem(f"y{k}T_mm"), 1)

            ln_transpose(LN_ATT2, 4)
            pe.wait_ge(sem("att_in"), 16)
            pe.wait_ge(sem(f"yT{LN_ATT2}_ready"), 2)
            yt = yT[LN_ATT2]
            mm(bank[0][:, :], ca("WK"), yt[:], start=True, stop=True).then_inc(sem("k2_mm"), 1)
            for t in range(NT):
                mm(bank[1][:, 128 * t:128 * t + 128], yt[:, 128 * t:128 * t + 128], ca("WQ"), start=(t == 0),
                   stop=False, skip_group_check=True)
            for t in range(NT):
                last = mm(bank[2][:, 128 * t:128 * t + 128], yt[:, 128 * t:128 * t + 128], ca("WV"),
                          start=True, stop=True)
            last.then_inc(sem("v2_mm"), 1)
            for t in range(NT):
                pe.wait_ge(sem("kqb_ready"), t // 2 + 1)
                last = mm(bank[1][:, 128 * t:128 * t + 128], kqb[:, t // 2, :], ident[:], start=False,
                          stop=(t == NT - 1), skip_group_check=True)
            last.then_inc(sem("q2_mm"), 1)
            pe.wait_ge(sem("t2_ready"), 1)
            for b in range(B):
                pe.wait_ge(sem("ek_ready"), b + 1)
                for t in range(2):
                    last = tr(bank[3][:, (2 * b + t) * 128:(2 * b + t) * 128 + 128], ek[:, b, 128 * t:128 * t + 128],
                              ident[:])
            last.then_inc(sem("ekT_mm"), 1)
            pe.wait_ge(sem("ekT_ready"), 1)
            pe.wait_ge(sem("v2_ready"), 1)
            for b in range(B):
                for t in range(2):
                    last = mm(bank[5][:, C * b:C * b + C], ekT[:, 2 * b + t, :], v2[:, 2 * b + t, :],
                              start=(t == 0), stop=(t == 1))
            last.then_inc(sem("kv_mm"), 1)
            pe.wait_ge(sem("eq_ready"), 1)
            pe.wait_ge(sem("ekT_ready"), 1)
            for t in range(NT):
                last = tr(bank[3][:, 128 * t:128 * t + 128], eq[:, t, :], ident[:])
            last.then_inc(sem("eqT_mm"), 1)
            pe.wait_ge(sem("eqT_ready"), 1)
            pe.wait_ge(sem("kv_ready"), 2)
            for b in range(B):
                last = mm(bank[7][:, PIX * b:PIX * b + PIX], ksum[:, b, :], eqT[:, PIX * b:PIX * b + PIX],
                          start=True, stop=True)
            last.then_inc(sem("den2_mm"), 1)
            for b in range(B):
                last = mm(bank[6][:, PIX * b:PIX * b + PIX], kv[:, b, :], eqT[:, PIX * b:PIX * b + PIX],
                          start=True, stop=True)
            last.then_inc(sem("num2_mm"), 1)
            pe.wait_ge(sem("heads2_ready"), 1)
            for t in range(NT):
                last = mm(bank[0][:, 128 * t:128 * t + 128], heads2b[:, 128 * t:128 * t + 128], ca("WO"),
                          start=True, stop=True)
            last.then_inc(sem("att2_mm"), 1)

            ln_transpose(LN_FFN2, 4)
            pe.wait_ge(sem(f"yT{LN_FFN2}_ready"), 2)
            yt = yT[LN_FFN2]
            for t in range(NT):
                last = mm(bank[1][:, E2 * t:E2 * t + E2], yt[:, 128 * t:128 * t + 128], ca("Wr"), start=True, stop=True)
            last.then_inc(sem("route2_mm"), 1)
            pe.wait_ge(sem("heads2_ready"), 1)
            pe.wait_ge(sem(f"yT{LN_FFN2}_ready"), 2)
            pe.wait_ge(sem("kv_ready"), 2)
            pe.wait_ge(sem("eqT_ready"), 1)
            with pe.Fori(0, E2 // 2) as i:
                for p in range(2):
                    pe.wait_ge(sem(f"ew2_in{p}"), 16 * i + 16)
                    pe.wait_ge(sem("h2_ready"), 4 * i + 2 * p + 2)
                    for half in range(2):
                        mm(bank[4 + 2 * p + half][:, :], ew2[p][:, C * half:C * half + C], yt[:],
                           start=True, stop=True).then_inc(sem("hidden2_mm"), 1)
                for p in range(2):
                    pe.wait_ge(sem("y2_added"), 2 * i + p + 1)
                    for half in range(2):
                        pe.wait_ge(sem("h2_ready"), 2 * CREDIT + 4 * i + 2 * p + half + 1)
                        for t in range(NT):
                            last = mm(bank[2 + p][:, 128 * t:128 * t + 128], h2[:, 2 * p + half, 128 * t:128 * t + 128],
                                      ew2[p][:, 2 * C + C * half:3 * C + C * half],
                                      start=(half == 0 and t == 0), stop=(half == 1 and t == NT - 1),
                                      skip_group_check=True)
                    last.then_inc(sem("expert2_mm"), 1)
            pe.wait_ge(sem("comb2_ready"), 1)
            for t in range(NT):
                last = tr(bank[0][0:E2, 128 * t:128 * t + 128], comb2[:, t, :], ident[:])
            last.then_inc(sem("comb2T_mm"), 1)
            pe.wait_ge(sem("comb2T_ready"), 1)
            pe.wait_ge(sem("b2_in"), 16)
            for t in range(NT):
                last = mm(bank[1][:, 128 * t:128 * t + 128], comb2T[:, 128 * t:128 * t + 128], b2[:],
                          start=True, stop=True)
            last.then_inc(sem("bias2_mm"), 1)

            ln_transpose(LN_ATT3, 2)
            pe.wait_ge(sem("l3_in"), 16)
            pe.wait_ge(sem(f"yT{LN_ATT3}_ready"), 2)
            yt = yT[LN_ATT3]
            for s, name in enumerate(("g_in", "l_in")):
                w = c3(name)
                mm(bank[4 + 2 * s][:, :], w[:, 0:C], yt[:], start=True, stop=True).then_inc(sem("q3_mm"), 1)
                mm(bank[5 + 2 * s][:, :], w[:, C:2 * C], yt[:], start=True, stop=True).then_inc(sem("k3_mm"), 1)
            for t in range(NT):
                last = mm(bank[2][:, 128 * t:128 * t + 128], yt[:, 128 * t:128 * t + 128], c3("g_in")[:, 2 * C:3 * C],
                          start=True, stop=True)
            last.then_inc(sem("vg_mm"), 1)
            for b in range(B):
                for w, (start, _, _) in enumerate(WINDOWS):
                    last = mm(bank[b][:, 128 * w:128 * w + 128], yt[:, b * PIX + start:b * PIX + start + 128],
                              c3("l_in")[:, 2 * C:3 * C], start=True, stop=True)
            last.then_inc(sem("vl_mm"), 1)

            def scores(u):
                kind, b, t, h = UNITS[u]
                if u >= 2:
                    pe.wait_ge(sem("exp3"), u - 1)
                if kind == "g":
                    pe.wait_ge(sem("km3_image1" if b else "km3_image0"), 1)
                    mm(bank[u % 2][:, :], q3[0][:, b * PIX + 128 * t:b * PIX + 128 * t + 128],
                       km3[0][b][:, h:h + GLOBAL_HEADS, :], start=True, stop=True).then_inc(sem("score3_mm"), 1)
                else:
                    start = WINDOWS[t][0]
                    pe.wait_ge(sem("km3_image1" if b else "km3_image0"), 2)
                    mm(bank[u % 2][:, :], q3[1][:, b * PIX + start:b * PIX + start + 128],
                       km3[1][b][:, h:h + LOCAL_HEADS, start:start + 128], start=True, stop=False)
                    mm(bank[u % 2][:, :], ident_bf[:], band[:].unsqueeze(1).broadcast_to([128, LOCAL_HEADS, 128]),
                       start=False, stop=True).then_inc(sem("score3_mm"), 1)

            def turn(u):
                pe.wait_ge(sem("exp3"), u + 1)
                if u >= 2:
                    pe.wait_ge(sem("p3T_ready"), u - 1)
                for n in range(4):
                    last = tr(bank[2 + u % 2][:, 128 * n:128 * n + 128], p3[:, u % 2, 128 * n:128 * n + 128], ident[:])
                last.then_inc(sem("p3T_mm"), 1)

            def attend(u):
                kind, b, t, h0 = UNITS[u]
                if u % UNITS_B == 0 and b:
                    pe.wait_ge(sem("o3_copied"), 1)
                if u % UNITS_B == UNITS_G and b:
                    pe.wait_ge(sem("o3_copied"), 2)
                pe.wait_ge(sem("p3T_ready"), u + 1)
                if kind == "g":
                    for n in range(GLOBAL_HEADS):
                        h = h0 + n
                        r = 32 * (h % 4)
                        for j in range(2):
                            last = mm(bank[4][r:r + 32, h // 4 * PIX + 128 * t:h // 4 * PIX + 128 * t + 128],
                                      vg[:, 2 * b + j, h, :], p3T[:, u % 2, (2 * n + j) * 128:(2 * n + j) * 128 + 128],
                                      start=(j == 0), stop=(j == 1), tile_position=(0, r))
                else:
                    start, first, end = WINDOWS[t]
                    for n in range(LOCAL_HEADS):
                        h = h0 + n
                        r = 32 * (h % 4)
                        last = mm(bank[5][r:r + 32, h // 4 * PIX + first:h // 4 * PIX + end],
                                  vl[:, b * len(WINDOWS) + t, h, :],
                                  p3T[:, u % 2, 128 * n + first - start:128 * n + end - start],
                                  start=True, stop=True, tile_position=(0, r))
                last.then_inc(sem("attend3"), 1)

            def denominators(n):
                pe.wait_ge(sem("o3_copied"), n + 1)
                if n:
                    pe.wait_ge(sem("rd3_ready"), n)
                mm(bank[6][:, :], den_sel[:], o3[:, n % 2, :], start=True, stop=True).then_inc(sem("den3_mm"), 1)

            def project(b):
                pe.wait_ge(sem("ob3_ready"), 2 * b + 2)
                for t in range(2):
                    for s, name in enumerate(("g_out", "l_out")):
                        for half in range(2):
                            last = mm(bank[7][:, (2 * b + t) * 128:(2 * b + t) * 128 + 128],
                                      ob3[:, b, s, half, 128 * t:128 * t + 128], c3(name)[:, C * half:C * half + C],
                                      start=(s == 0 and half == 0), stop=(s == 1 and half == 1))
                last.then_inc(sem("att3_mm"), 1)

            pe.wait_ge(sem("masks_made"), 1)
            pe.wait_ge(sem("q3_ready"), 2)
            pe.wait_ge(sem("k3_ready"), 2)
            pe.wait_ge(sem("v3_ready"), 2)
            for u in range(len(UNITS) + 2):
                if u < len(UNITS):
                    scores(u)
                if 1 <= u <= len(UNITS):
                    turn(u - 1)
                if u >= 2:
                    attend(u - 2)
                for n, end in enumerate((UNITS_G, UNITS_B, UNITS_B + UNITS_G)):
                    if u == end + 3:
                        denominators(n)
            denominators(3)
            project(0)
            project(1)

            ln_transpose(LN_MID3, 0)
            pe.wait_ge(sem(f"yT{LN_MID3}_ready"), 2)
            for f in range(FT):
                mm(bank[1 + f][:, :], c3("ffn1")[:, 128 * f:128 * f + 128], yT[LN_MID3][:], start=True, stop=True)\
                    .then_inc(sem("ff3_mm"), 1)
            for f in range(FT):
                pe.wait_ge(sem("hf3_ready"), f + 1)
                for t in range(NT):
                    last = mm(bank[6][:, 128 * t:128 * t + 128], hf3[:, f, 128 * t:128 * t + 128],
                              c3("ffn2")[:, C * f:C * f + C], start=(f == 0 and t == 0),
                              stop=(f == FT - 1 and t == NT - 1), skip_group_check=True)
            last.then_inc(sem("ffn3_mm"), 1)

            ln_transpose(LN_FFN3, 5)
            pe.wait_ge(sem(f"yT{LN_FFN3}_ready"), 2)
            yt = yT[LN_FFN3]
            for t in range(NT):
                last = mm(bank[4][:, E3 * t:E3 * t + E3], yt[:, 128 * t:128 * t + 128], c3("gate"), start=True, stop=True)
            last.then_inc(sem("route3_mm"), 1)

            def shared_up(t):
                if t >= 2:
                    pe.wait_ge(sem("hs_ready"), t - 1)
                if t == 0:
                    pe.wait_ge(sem("w1_in0"), 16)
                    pe.wait_ge(sem("w2_in0"), 16)
                mm(bank[t % 2][:, :], w1[0][:, 128 * t:128 * t + 128], yt[:], start=True, stop=True)\
                    .then_inc(sem("sa_mm"), 1)
                mm(bank[2 + t % 2][:, :], w2[0][:, 128 * t:128 * t + 128], yt[:], start=True, stop=True)\
                    .then_inc(sem("sb_mm"), 1)

            def shared_down(t):
                m = 128 if t < HT - 1 else H_LAST
                if t == 0:
                    pe.wait_ge(sem("w3_in0"), 32)
                pe.wait_ge(sem("hs_ready"), t + 1)
                return mm(bank[7][:, :], w3[0][0:m, t, :], hs[0:m, t % 3, :], start=(t == 0), stop=False,
                          skip_group_check=True)

            def places():
                pe.wait_ge(sem("chosen_ready"), 1)
                flat = chosen_bf[:].rearrange("p t e -> p (t e)")
                mm(bank[6][:, 0:NT * E3], earlier_bf[:], flat, start=True, stop=False, skip_group_check=True)
                for t in range(NT - 1):
                    mm(bank[6][:, E3 * (t + 1):E3 * NT].rearrange("p (t e) -> p t e", e=E3), ones_bf[:],
                       chosen_bf[:, t, :].unsqueeze(1).broadcast_to([128, NT - 1 - t, E3]),
                       start=False, stop=False, skip_group_check=True)
                for t in range(NT):
                    last = mm(bank[6][:, E3 * NT:E3 * NT + E3], ones_bf[:], chosen_bf[:, t, :],
                              start=False, stop=(t == NT - 1), skip_group_check=True)
                last.then_inc(sem("places_mm"), 1)

            for t in range(HT):
                shared_up(t)
                if t >= 1:
                    shared_down(t - 1).then_inc(sem("shared_down"), 1)
                if t == 3:
                    places()
            for t in range(NT):
                mm(bank[7][:, 128 * t:128 * t + 128], t5[:, t, :], ident[:], start=False, stop=False,
                   skip_group_check=True)
            shared_down(HT - 1).then_inc(sem("down_mm"), 1)

            def gather(p, k, first=False):
                pe.wait_ge(sem("pick_ready"), k + 1)
                if not first:
                    pe.wait_ge(sem("xe_ready"), k)
                for t in range(NT):
                    last = mm(bank[4][:, 0:SLOTS], y[LN_FFN3][:, t, :], pick[:, p, t, :],
                              start=(t == 0), stop=(t == NT - 1))
                last.then_inc(sem("xe_mm"), 1)
                if not first:
                    pe.wait_ge(sem("spread_ready"), k + 1)
                for t in range(NT):
                    last = tr(bank[6][:, 128 * t:128 * t + 128], pickw[:, p, t, :], ident[:])
                last.then_inc(sem("spread_mm"), 1)

            def scatter(p):
                return mm(bank[7][:, :], ye[:, p, :], spread[:, p, :], start=False, stop=False, skip_group_check=True)

            pe.wait_ge(sem("hs_ready"), HT)
            pe.wait_ge(sem("plan_ready"), 1)
            gather(1, 0, first=True)
            n_pairs = pe.value_load(pairs_int[0:1, 0:1], min_val=1, max_val=PAIRS)
            with pe.Fori(0, n_pairs) as i:
                for p in (1, 0):
                    k = 2 * i + 1 - p
                    uses = i + 1 if p == 1 else i + 2
                    pe.wait_ge(sem(f"w1_in{p}"), 16 * uses)
                    pe.wait_ge(sem(f"w2_in{p}"), 16 * uses)
                    pe.wait_ge(sem("xe_ready"), k + 1)
                    for g, (t0, t1) in enumerate(GROUPS):
                        slot = (3 * (1 - p) + g) % 2
                        pe.wait_ge(sem("he_ready"), 3 * k + g + 1)
                        for w, b, name in ((w1, slot, "a3_mm"), (w2, 2 + slot, "b3_mm")):
                            for t in range(t0, t1):
                                last = mm(bank[b][:, 128 * (t - t0):128 * (t - t0) + 128],
                                          w[p][:, 128 * t:128 * t + 128], xe[:, p, :], start=True, stop=True)
                            last.then_inc(sem(name), 1)
                        if g == 0:
                            pe.wait_ge(sem("ye_ready"), k + 1)
                            pe.wait_ge(sem("spread_ready"), k + 1)
                            scatter(1 - p).then_inc(sem("scatter_mm"), 1)
                    gather(1 - p, k + 1)
                    pe.wait_ge(sem(f"w3_in{p}"), 32 * uses)
                    pe.wait_ge(sem("he_ready"), CREDIT + 3 * k + 3)
                    for t in range(HT):
                        m = 128 if t < HT - 1 else H_LAST
                        last = mm(bank[5][:, 0:C], he[0:m, p, t, :], w3[p][0:m, t, :], start=(t == 0), stop=(t == HT - 1))
                    last.then_inc(sem("down_mm"), 1)
            pe.wait_ge(sem("ye_ready"), 2 * n_pairs + 1)
            scatter(0).then_inc(sem("out_mm"), 1)

        @block.scalar
        def _(act):
            act.sem_inc(sem("h2_ready"), 2 * CREDIT)
            act.sem_inc(sem("ye_ready"), 1)
            act.sem_inc(sem("spread_ready"), 1)

            def copy(dst, src):
                return nc.scalar.activation(dst, src, ACT.Copy)

            act.wait_ge(sem("conv_in"), 16)
            act.wait_ge(sem("q0_mm"), 1)
            nc.scalar.activation(q0[:], bank[0][0:C8, :], ACT.Identity, bias=cc("bq")[0:C8, :]).then_inc(sem("q0_ready"), 1)
            act.wait_ge(sem("x0T_mm"), 1)
            copy(x0T[:].rearrange("p t c -> p (t c)"), bank[3][:, :]).then_inc(sem("x0T_ready"), 1)
            for b in range(B):
                act.wait_ge(sem("nmax0_ready"), b + 1)
                for t in range(2):
                    nc.scalar.activation(p0[:, b, t, :], bank[4 + b][:, PIX * t:PIX * t + PIX], ACT.Exp,
                                         bias=nmax0[:, b, t:t + 1], accum_out=sum0[:, b, t:t + 1])\
                        .then_inc(sem("exp0"), 1)
            act.wait_ge(sem("minc_ready"), 1)
            for b in range(B):
                nc.scalar.activation(pc[:, b, :], bank[6][:, C * b:C * b + C], ACT.Exp, bias=minc[:, b:b + 1], scale=-1.0,
                                     accum_out=sumc[:, b:b + 1]).then_inc(sem("expc"), 1)
            for b in range(B):
                act.wait_ge(sem("p0T_mm"), b + 1)
                copy(p0T[:, b, :, :].rearrange("p t n -> p (t n)"), bank[b][:, :]).then_inc(sem("p0T_ready"), 1)
            act.wait_ge(sem("gvar_ready"), 1)
            nc.scalar.activation(gr[:, 0, :], gvar[:], ACT.Ln).then_inc(sem("gln"), 1)
            act.wait_ge(sem("gln"), 1)
            nc.scalar.activation(gr[:, 1, :], gr[:, 0, :], ACT.Exp, scale=-0.5).then_inc(sem("gr_first"), 1)
            act.wait_ge(sem("t2_mm"), 1)
            copy(t2[:].rearrange("p t c -> p (t c)"), bank[3][:, :]).then_inc(sem("t2_ready"), 1)

            def ln_first(k):
                act.wait_ge(sem("lve_ready"), k + 1)
                nc.scalar.activation(lln[:, k, :], lve[:, k, :], ACT.Ln).then_inc(sem("lln"), 1)
                act.wait_ge(sem("lln"), k + 1)
                nc.scalar.activation(lr0[:, k, :], lln[:, k, :], ACT.Exp, scale=-0.5).then_inc(sem("lr_first"), 1)

            def ln_copy(k, b):
                for half in range(2):
                    act.wait_ge(sem(f"y{k}T_mm"), 2 * half + 2)
                    copy(yT[k][:, PIX * half:PIX * half + PIX], bank[b + half][:, 0:PIX])\
                        .then_inc(sem(f"yT{k}_ready"), 1)

            ln_first(LN_ATT2)
            ln_copy(LN_ATT2, 4)
            for b in range(B):
                act.wait_ge(sem("knmax_ready"), 1)
                nc.scalar.activation(ek[:, b, :], bank[0][:, PIX * b:PIX * b + PIX], ACT.Exp, bias=knmax[:, b:b + 1],
                                     accum_out=sek[:, b:b + 1]).then_inc(sem("ek_ready"), 1)
            act.wait_ge(sem("v2_mm"), 1)
            copy(v2[:].rearrange("p t c -> p (t c)"), bank[2][:, :]).then_inc(sem("v2_ready"), 1)
            act.wait_ge(sem("ekT_mm"), 1)
            copy(ekT[:].rearrange("p t c -> p (t c)"), bank[3][:, :]).then_inc(sem("ekT_ready"), 1)
            act.wait_ge(sem("qs_ready"), 1)
            nc.scalar.activation(eq[:].rearrange("p t c -> p (t c)"), qs[:].rearrange("p g c -> p (g c)"), ACT.Exp)\
                .then_inc(sem("eq_ready"), 1)
            act.wait_ge(sem("eqT_mm"), 1)
            copy(eqT[:], bank[3][:, :]).then_inc(sem("eqT_ready"), 1)
            act.wait_ge(sem("heads2_divided"), 1)
            nc.scalar.activation(heads2b[:], heads2[:], ACT.Identity, bias=ca("bV")).then_inc(sem("heads2_ready"), 1)

            ln_first(LN_FFN2)
            ln_copy(LN_FFN2, 4)
            act.wait_ge(sem("lg2_ready"), 1)
            nc.scalar.activation(e2[:], lg2[:], ACT.Exp).then_inc(sem("e2_ready"), 1)
            with act.Fori(0, E2 // 2) as i:
                for p in range(2):
                    act.wait_ge(sem(f"ew2_in{p}"), 16 * i + 16)
                    act.wait_ge(sem("expert2_mm"), 2 * i + p + 1)
                    for half in range(2):
                        act.wait_ge(sem("hidden2_mm"), 4 * i + 2 * p + half + 1)
                        nc.scalar.activation(h2[:, 2 * p + half, :], bank[4 + 2 * p + half][:, :], ACT.Gelu,
                                             bias=ew2[p][:, 4 * C + half:4 * C + half + 1]).then_inc(sem("h2_ready"), 1)
            act.wait_ge(sem("comb2T_mm"), 1)
            copy(comb2T[:], bank[0][0:E2, :]).then_inc(sem("comb2T_ready"), 1)

            ln_first(LN_ATT3)
            ln_copy(LN_ATT3, 2)
            for s, side in enumerate("gl"):
                act.wait_ge(sem("q3_mm"), s + 1)
                nc.scalar.activation(q3[s][:], bank[4 + 2 * s][:, :], ACT.Identity, bias=c3(side + "_bq"))\
                    .then_inc(sem("q3_ready"), 1)
            act.wait_ge(sem("masks_made"), 1)
            act.wait_ge(sem("vg_mm"), 1)
            copy(vg[:, :, :, 0:HD], bank[2][:, :].rearrange("p (t h c) -> p t h c", t=NT, h=HEADS))\
                .then_inc(sem("v3_ready"), 1)
            act.wait_ge(sem("vl_mm"), 1)
            nw = len(WINDOWS)
            for b in range(B):
                last = copy(vl[:, nw * b:nw * b + nw, :, 0:HD],
                            bank[b][:, 0:nw * C].rearrange("p (t h c) -> p t h c", t=nw, h=HEADS))
            last.then_inc(sem("v3_ready"), 1)

            def exps(u):
                kind = UNITS[u][0]
                n = GLOBAL_HEADS if kind == "g" else LOCAL_HEADS
                m = 512 // n
                act.wait_ge(sem("nmax3_ready"), u + 1)
                if u >= 2:
                    act.wait_ge(sem("p3T_mm"), u - 1)
                for h in range(n):
                    last = nc.scalar.activation(p3[:, u % 2, m * h:m * h + m], bank[u % 2][:, m * h:m * h + m], ACT.Exp,
                                                bias=nmax3[:, u, h:h + 1], scale=HD ** -0.5)
                last.then_inc(sem("exp3"), 1)

            def copy_out(n):
                act.wait_ge(sem("attend3"), (n // 2) * UNITS_B + (UNITS_B if n % 2 else UNITS_G))
                if n >= 2:
                    act.wait_ge(sem("on3_ready"), n - 1)
                copy(o3[:, n % 2, :], bank[4 + n % 2][:, :]).then_inc(sem("o3_copied"), 1)

            def add_bias(n):
                act.wait_ge(sem("on3_ready"), n + 1)
                bias = c3("gl"[n % 2] + "_bv")
                for half in range(2):
                    last = nc.scalar.activation(ob3[:, n // 2, n % 2, half, :], on3[:, n % 2, PIX * half:PIX * half + PIX],
                                                ACT.Identity, bias=bias[:, half:half + 1])
                last.then_inc(sem("ob3_ready"), 1)

            for u in range(len(UNITS)):
                exps(u)
                for n, end in enumerate((UNITS_G, UNITS_B, UNITS_B + UNITS_G)):
                    if u == end + 2:
                        copy_out(n)
                    if u == end + 4:
                        add_bias(n)
            copy_out(3)
            add_bias(3)

            ln_first(LN_MID3)
            ln_copy(LN_MID3, 0)
            for f in range(FT):
                act.wait_ge(sem("ff3_mm"), f + 1)
                nc.scalar.activation(hf3[:, f, :], bank[1 + f][:, :], ACT.Relu, bias=c3("ffn_b1")[:, f:f + 1])\
                    .then_inc(sem("hf3_ready"), 1)
            ln_first(LN_END3)

            ln_first(LN_FFN3)
            ln_copy(LN_FFN3, 5)
            act.wait_ge(sem("lg3_ready"), 1)
            nc.scalar.activation(e3[:], lg3[:], ACT.Exp).then_inc(sem("e3_ready"), 1)
            for t in range(HT):
                act.wait_ge(sem("sa_mm"), t + 1)
                if t >= 2:
                    act.wait_ge(sem("hs_ready"), t - 1)
                nc.scalar.activation(silu[:, t % 2, :], bank[t % 2][:, :], ACT.Silu).then_inc(sem("s_silu"), 1)

            def turn_weights(p, k):
                act.wait_ge(sem("scatter_mm"), k + 1)
                act.wait_ge(sem("spread_mm"), k + 2)
                copy(spread[:, p, :], bank[6][:, :]).then_inc(sem("spread_ready"), 1)

            act.wait_ge(sem("plan_ready"), 1)
            act.wait_ge(sem("hs_ready"), HT)
            turn_weights(1, 0)
            n_pairs = act.value_load(pairs_int[0:1, 0:1], min_val=1, max_val=PAIRS)
            with act.Fori(0, n_pairs) as i:
                for p in (1, 0):
                    k = 2 * i + 1 - p
                    for g, (t0, t1) in enumerate(GROUPS):
                        slot = (3 * (1 - p) + g) % 2
                        n = 128 * (t1 - t0)
                        act.wait_ge(sem("a3_mm"), 3 * k + g + 1)
                        act.wait_ge(sem("he_ready"), 3 * k + g + 1)
                        nc.scalar.activation(silu[:, slot, 0:n], bank[slot][:, 0:n], ACT.Silu)\
                            .then_inc(sem("silu_ready"), 1)
                    turn_weights(1 - p, k + 1)
                    act.wait_ge(sem("down_mm"), k + 3)
                    copy(ye[:, p, :], bank[5][:, 0:C]).then_inc(sem("ye_ready"), 1)

        @block.vector
        def _(dve):
            tt = nc.vector.tensor_tensor
            ts = nc.vector.tensor_scalar
            stt = nc.vector.scalar_tensor_tensor
            done = [0]

            def note(ins):
                done[0] += 1
                ins.then_inc(sem("dve_step"), 1)

            def settle(ins=None):
                if ins is not None:
                    note(ins)
                dve.wait_ge(sem("dve_step"), done[0])

            def flat(x):
                return x.rearrange("p a b -> p (a b)")

            dve.sem_inc(sem("y2_added"), CREDIT)
            dve.sem_inc(sem("he_ready"), CREDIT)
            dve.wait_ge(sem("conv_in"), 16)
            dve.wait_ge(sem("rows_in"), 16)
            note(tt(mix[:, 0:1], cc("alpha"), cc("gamma_pos"), ALU.mult))
            note(tt(mix[:, 1:2], cc("beta"), cc("gamma_chan"), ALU.mult))
            note(stt(mix[:, 2:3], cc("alpha"), 1.0, cc("beta"), ALU.add, ALU.add))
            note(stt(mask_w[:], cc("filter"), 1.0, cc("mask_weight"), ALU.is_equal, ALU.mult))
            dve.wait_ge(sem("k0_mm"), 1)
            ts(k0[:], bank[1][0:C8, :], cc("bk")[0:C8, :], None, ALU.add).then_inc(sem("k0_ready"), 1)
            dve.wait_ge(sem("v0_mm"), 1)
            tt(v0T[:], bank[2][:, :].rearrange("p (t c) -> p t c", t=NT), row("bv", NT), ALU.add)\
                .then_inc(sem("v0_ready"), 1)
            for b in range(B):
                dve.wait_ge(sem("energy_mm"), b + 1)
                nc.vector.tensor_reduce(nmax0[:, b, :], bank[4 + b][:, :].rearrange("p (t n) -> p t n", t=2), AX.X,
                                        ALU.max, negate=True).then_inc(sem("nmax0_ready"), 1)
            dve.wait_ge(sem("energyc_mm"), 1)
            nc.vector.tensor_reduce(minc[:], bank[6][:, 0:B * C].rearrange("p (b n) -> p b n", b=B), AX.X, ALU.min)\
                .then_inc(sem("minc_ready"), 1)
            for b in range(B):
                dve.wait_ge(sem("exp0"), 2 * b + 2)
                settle(nc.vector.reciprocal(sum0[:, b, :], sum0[:, b, :]))
                settle(ts(sum0[:, b, :], sum0[:, b, :], mix[:, 0:1], None, ALU.mult))
                for t in range(2):
                    ts(p0[:, b, t, :], p0[:, b, t, :], sum0[:, b, t:t + 1], None, ALU.mult).then_inc(sem("p0_ready"), 2)
            dve.wait_ge(sem("expc"), B)
            settle(nc.vector.reciprocal(sumc[:], sumc[:]))
            settle(ts(sumc[:], sumc[:], mix[:, 1:2], None, ALU.mult))
            for b in range(B):
                ts(pc[:, b, :], pc[:, b, :], sumc[:, b:b + 1], None, ALU.mult).then_inc(sem("pc_ready"), 1)
            dve.wait_ge(sem("pcT_mm"), 1)
            nc.vector.tensor_copy(flat(pcT[:]), bank[2][:, 0:B * C]).then_inc(sem("pcT_ready"), 1)
            for b in range(B):
                dve.wait_ge(sem("layer0_mm"), b + 1)
                settle(stt(x1[:, b, :], x0[:, b, :], mix[:, 2:3], bank[7 - 4 * b][:, 0:PIX], ALU.mult, ALU.add))
                settle(nc.vector.bn_stats(gst[:, b, :], x1[:, b, :]))
                note(nc.vector.bn_aggr(gmv[:, b, :], gst[:, b, :]))
            settle()
            dve.sem_inc(sem("gmv_ready"), 1)
            dve.wait_ge(sem("gmean_mm"), 1)
            settle(nc.vector.tensor_copy(gm[:], bank[0][:, 0:B]))
            settle(tt(gdev[:], gmv[:, :, 0], gm[:], ALU.subtract))
            settle(tt(gdev[:], gdev[:], gdev[:], ALU.mult))
            tt(gdev[:], gdev[:], gmv[:, :, 1], ALU.add).then_inc(sem("gdev_ready"), 1)
            dve.wait_ge(sem("gvar_mm"), 1)
            ts(gvar[:], bank[1][:, 0:B], EPS, None, ALU.add).then_inc(sem("gvar_ready"), 1)
            dve.wait_ge(sem("gr_first"), 1)

            def newton(r, r0, v, tmp):
                settle(tt(tmp, r0, r0, ALU.mult))
                settle(tt(tmp, tmp, v, ALU.mult))
                settle(ts(tmp, tmp, -0.5, 1.5, ALU.mult, ALU.add))
                settle(tt(r, r0, tmp, ALU.mult))

            dve.wait_ge(sem("gvar_ready"), 1)
            newton(gr[:, 2, :], gr[:, 1, :], gvar[:], gr[:, 3, :])
            for b in range(B):
                note(ts(gn[:, b, :, :].rearrange("p h w -> p (h w)"), x1[:, b, :], gm[:, b:b + 1], gr[:, 2, b:b + 1],
                        ALU.subtract, ALU.mult))
            settle()
            note(nc.vector.tensor_reduce(sums[:, 0, :, :], gn[:], AX.X, ALU.add))
            note(nc.vector.tensor_reduce(sums[:, 1, :, :], gn[:].rearrange("p b h w -> p b w h"), AX.X, ALU.add))
            settle()
            dve.wait_ge(sem("group_made"), 1)
            note(nc.vector.tensor_reduce(total[:], sums[:, 0, :, :], AX.X, ALU.add))
            note(tt(weighted[:].rearrange("p k b h -> p (k b) h"), sums[:].rearrange("p k b h -> p (k b) h"),
                    ramp[:].unsqueeze(1).broadcast_to([128, 2 * B, SIDE]), ALU.mult))
            settle(ts(pos[:], ramp[:], -1.0, 2.0 / (SIDE - 1), ALU.add, ALU.mult))
            note(ts(pos[:], pos[:], -1.0, None, ALU.add))
            note(nc.vector.tensor_reduce(moment[:], weighted[:], AX.X, ALU.add))
            settle(ts(total[:], total[:], 1e-9, None, ALU.max))
            settle(nc.vector.reciprocal(total[:], total[:]))
            settle(tt(mu[:], moment[:], total[:].unsqueeze(1).broadcast_to([128, 2, B]), ALU.mult))
            settle(ts(mu[:], mu[:], 1.0, float(SIDE), ALU.max, ALU.min))
            settle(ts(mu[:], mu[:], ROUND, ROUND, ALU.add, ALU.subtract))
            settle(ts(mu[:], mu[:], -1.0, 2.0 / (SIDE - 1), ALU.add, ALU.mult))
            settle(ts(mu[:], mu[:], -1.0, None, ALU.add))
            d = dist[:].rearrange("p k b h -> p (k b) h")
            settle(tt(d, pos[:].unsqueeze(1).broadcast_to([128, 2 * B, SIDE]),
                      mu[:].rearrange("p k b -> p (k b)").unsqueeze(2).broadcast_to([128, 2 * B, SIDE]), ALU.subtract))
            settle(stt(d, d, -1.0, d, ALU.mult, ALU.max))
            m = mask[:].rearrange("p b h w -> p (b h w)")
            for b in range(B):
                note(tt(mask[:, b, :, :], dist[:, 0, b, :].unsqueeze(2).broadcast_to([128, SIDE, SIDE]),
                        dist[:, 1, b, :].unsqueeze(1).broadcast_to([128, SIDE, SIDE]), ALU.add))
            settle()
            settle(ts(mask_w[:], mask_w[:], -1.0, None, ALU.mult))
            settle(ts(m, m, mask_w[:], 1.0, ALU.mult, ALU.add))
            settle(stt(m, m, -1.0, gn[:].rearrange("p b h w -> p (b h w)"), ALU.max, ALU.mult))
            dve.wait_ge(sem("pad_made"), 1)
            ts(pad[:, :, 1:1 + SIDE, 1:1 + SIDE], mask[:], 0.0, None, ALU.max).then_inc(sem("pad_ready"), 1)
            dve.wait_ge(sem("conv_mm"), 1)
            stt(flat(x2[:]), bank[2][:, :], cc("conv_bias"), flat(x1[:]), ALU.add, ALU.add).then_inc(sem("x2_ready"), 1)

            def normalise(k, src, out=None):
                for t in range(NT):
                    note(nc.vector.bn_stats(lst[:, t, :], src[:, t, :]))
                settle()
                for t in range(NT):
                    note(nc.vector.bn_aggr(lmv[:, k, t, :], lst[:, t, :]))
                settle()
                ts(lve[:, k, :], lmv[:, k, :, 1], EPS, None, ALU.add).then_inc(sem("lve_ready"), 1)
                dve.wait_ge(sem("lve_ready"), k + 1)
                dve.wait_ge(sem("lr_first"), k + 1)
                newton(lr[:, k, :], lr0[:, k, :], lve[:, k, :], lra[:, k % 2, :])
                for t in range(NT):
                    ins = ts((y[k] if out is None else out)[:, t, :], src[:, t, :], lmv[:, k, t, 0:1], lr[:, k, t:t + 1],
                             ALU.subtract, ALU.mult)
                    if out is None:
                        ins.then_inc(sem(f"y{k}_ready"), 1)
                    else:
                        note(ins)
                if out is not None:
                    settle()

            dve.wait_ge(sem("t2_ready"), 1)
            normalise(LN_ATT2, t2)
            dve.wait_ge(sem("att_in"), 16)
            dve.wait_ge(sem(f"y{LN_ATT2}_ready"), NT)
            note(tt(t2[:], t2[:], row("bO", NT), ALU.add))
            dve.wait_ge(sem("k2_mm"), 1)
            settle(nc.vector.tensor_reduce(kmax[:], bank[0][:, :].rearrange("p (b n) -> p b n", b=B), AX.X, ALU.max))
            ts(knmax[:], kmax[:], -1.0, None, ALU.mult).then_inc(sem("knmax_ready"), 1)
            settle(ts(kq[:], kmax[:], ca("bK"), ca("bQ"), ALU.add, ALU.add))
            dve.wait_ge(sem("ident_made"), 1)
            for b in range(B):
                ts(kqb[:, b, :], ones[:], kq[:, b:b + 1], None, ALU.mult).then_inc(sem("kqb_ready"), 1)
            dve.wait_ge(sem("q2_mm"), 1)
            settle(nc.vector.tensor_reduce(qmax[:], bank[1][:, :].rearrange("p (g c) -> p g c", c=HD), AX.X, ALU.max))
            tt(qs[:], bank[1][:, :].rearrange("p (g c) -> p g c", c=HD),
               qmax[:].unsqueeze(2).broadcast_to([128, NT * HEADS, HD]), ALU.subtract).then_inc(sem("qs_ready"), 1)
            dve.wait_ge(sem("masks_made"), 1)
            dve.wait_ge(sem("ek_ready"), B)
            for b in range(B):
                last = ts(ksum[:, b, :], head_block[:], sek[:, b:b + 1], None, ALU.mult)
            last.then_inc(sem("kv_ready"), 1)
            dve.wait_ge(sem("kv_mm"), 1)
            tt(kv[:], bank[5][:, 0:B * C].rearrange("p (b c) -> p b c", b=B),
               head_block[:].unsqueeze(1).broadcast_to([128, B, C]), ALU.mult).then_inc(sem("kv_ready"), 1)
            dve.wait_ge(sem("den2_mm"), 1)
            settle(nc.vector.reciprocal(rden2[:], bank[7][:, :]))
            dve.wait_ge(sem("num2_mm"), 1)
            tt(heads2[:], bank[6][:, :], rden2[:], ALU.mult).then_inc(sem("heads2_divided"), 1)
            dve.wait_ge(sem("att2_mm"), 1)
            settle(tt(flat(t3[:]), bank[0][:, :], flat(t2[:]), ALU.add))

            normalise(LN_FFN2, t3)

            def logits(lg, b, n, bias, m):
                settle(tt(lg[:], bank[b][:, 0:NT * n].rearrange("p (t e) -> p t e", e=n), row(bias, NT), ALU.add))
                settle(nc.vector.tensor_reduce(m[:], lg[:], AX.X, ALU.max))
                return tt(lg[:], lg[:], m[:].unsqueeze(2).broadcast_to([128, NT, n]), ALU.subtract)

            def rank(out, x, cmp, earlier, n):
                for t in range(NT):
                    other = x[:, t, :].unsqueeze(1).broadcast_to([128, n, n])
                    own = x[:, t, :].unsqueeze(2).broadcast_to([128, n, n])
                    note(tt(cmp[:, 0, :, :], other, own, ALU.is_gt))
                    settle(tt(cmp[:, 1, :, :], other, own, ALU.is_equal))
                    settle(tt(cmp[:, 1, :, :], cmp[:, 1, :, :], earlier[:], ALU.mult))
                    settle(tt(cmp[:, 0, :, :], cmp[:, 0, :, :], cmp[:, 1, :, :], ALU.add))
                    settle(nc.vector.tensor_reduce(out[:, t, :], cmp[:, 0, :, :], AX.X, ALU.add))

            dve.wait_ge(sem("route2_mm"), 1)
            logits(lg2, 1, E2, "br", m2).then_inc(sem("lg2_ready"), 1)
            dve.wait_ge(sem("e2_ready"), 1)
            settle(nc.vector.tensor_reduce(s2[:], e2[:], AX.X, ALU.add))
            settle(nc.vector.reciprocal(s2[:], s2[:]))
            settle(tt(pr2[:], e2[:], s2[:].unsqueeze(2).broadcast_to([128, NT, E2]), ALU.mult))
            rank(rank2, pr2, cmp2, before2, E2)
            stt(comb2[:], rank2[:], 2.0, pr2[:], ALU.is_lt, ALU.mult).then_inc(sem("comb2_ready"), 1)
            dve.wait_ge(sem("comb2_ready"), 1)
            nc.vector.tensor_copy(t4[:], t3[:]).then_inc(sem("t4_added"), 1)
            with dve.Fori(0, E2 // 2) as i:
                for p in range(2):
                    dve.wait_ge(sem("expert2_mm"), CREDIT + 2 * i + p + 1)
                    dve.wait_ge(sem("t4_added"), 2 * i + p + 1)
                    for t in range(NT):
                        last = stt(t4[:, t, :], bank[2 + p][:, 128 * t:128 * t + 128],
                                   comb2[:, t, bass.ds(2 * i + p, 1)], t4[:, t, :], ALU.mult, ALU.add)
                    last.then_inc(sem("t4_added"), 1)
                    dve.wait_ge(sem("t4_added"), 2 * i + p + 2)
                    dve.sem_inc(sem("y2_added"), 1)
            dve.wait_ge(sem("bias2_mm"), 1)
            settle(tt(flat(t4[:]), bank[1][:, :], flat(t4[:]), ALU.add))

            normalise(LN_ATT3, t4)
            dve.wait_ge(sem(f"y{LN_ATT3}_ready"), NT)
            settle(tt(u3[:], y[LN_ATT3][:], row("g_out_b", NT), ALU.add))
            note(tt(u3[:], u3[:], row("l_out_b", NT), ALU.add))
            dve.wait_ge(sem("l3_in"), 16)
            for s, side in enumerate("gl"):
                dve.wait_ge(sem("k3_mm"), s + 1)
                ts(k3[s][:], bank[5 + 2 * s][:, :], c3(side + "_bk"), None, ALU.add).then_inc(sem("k3_ready"), 1)
                dve.wait_ge(sem("k3_ready"), s + 1)
                for h in range(HEADS):
                    last = ts(km3[s][0][:, h, :], k3[s][:, 0:PIX], head_mask[:, h:h + 1], None, ALU.mult)
                last.then_inc(sem("km3_image0"), 1)

            def largest(u):
                kind = UNITS[u][0]
                n = GLOBAL_HEADS if kind == "g" else LOCAL_HEADS
                dve.wait_ge(sem("score3_mm"), u + 1)
                settle(nc.vector.tensor_reduce(nmax3[:, u, 0:n], bank[u % 2][:, :].rearrange("p (h n) -> p h n", h=n),
                                               AX.X, ALU.max))
                ts(nmax3[:, u, 0:n], nmax3[:, u, 0:n], -HD ** -0.5, None, ALU.mult).then_inc(sem("nmax3_ready"), 1)

            def copy_turned(u):
                dve.wait_ge(sem("p3T_mm"), u + 1)
                if u >= 2:
                    dve.wait_ge(sem("attend3"), u - 1)
                nc.vector.tensor_copy(p3T[:, u % 2, :], bank[2 + u % 2][:, :]).then_inc(sem("p3T_ready"), 1)

            def divide(n):
                dve.wait_ge(sem("den3_mm"), n + 1)
                nc.vector.reciprocal(rd3[:, n % 2, :], bank[6][:, :]).then_inc(sem("rd3_ready"), 1)
                dve.wait_ge(sem("rd3_ready"), n + 1)
                dve.wait_ge(sem("o3_copied"), n + 1)
                if n >= 2:
                    dve.wait_ge(sem("ob3_ready"), n - 1)
                tt(on3[:, n % 2, :], o3[:, n % 2, :], rd3[:, n % 2, :], ALU.mult).then_inc(sem("on3_ready"), 1)

            for u in range(len(UNITS) + 1):
                if u < len(UNITS):
                    largest(u)
                if u >= 1:
                    copy_turned(u - 1)
                for n, end in enumerate((UNITS_G, UNITS_B, UNITS_B + UNITS_G)):
                    if u == end + 3:
                        divide(n)
            divide(3)
            dve.wait_ge(sem("att3_mm"), B)
            settle(tt(flat(u3[:]), bank[7][:, :], flat(u3[:]), ALU.add))

            normalise(LN_MID3, u3, out=z3)
            settle(tt(z3[:], z3[:], row("ln1_g", NT), ALU.mult))
            for t in range(NT):
                tt(y[LN_MID3][:, t, :], z3[:, t, :], row("ln1_b"), ALU.add).then_inc(sem(f"y{LN_MID3}_ready"), 1)
            dve.wait_ge(sem(f"y{LN_MID3}_ready"), NT)
            settle(tt(u3[:], y[LN_MID3][:], row("ffn_b2", NT), ALU.add))
            dve.wait_ge(sem("ffn3_mm"), 1)
            settle(tt(flat(u3[:]), bank[6][:, :], flat(u3[:]), ALU.add))
            normalise(LN_END3, u3, out=z3)
            settle(tt(z3[:], z3[:], row("ln2_g", NT), ALU.mult))
            settle(tt(z3[:], z3[:], row("ln2_b", NT), ALU.add))
            settle(tt(t5[:], z3[:], t4[:], ALU.add))

            normalise(LN_FFN3, t5)
            dve.wait_ge(sem("route3_mm"), 1)
            logits(lg3, 4, E3, "routing_bias", m3).then_inc(sem("lg3_ready"), 1)
            dve.wait_ge(sem("lg3_ready"), 1)
            rank(rank3, lg3, cmp3, before, E3)
            settle(ts(chosen[:], rank3[:], float(K3), None, ALU.is_lt))
            nc.vector.tensor_copy(chosen_bf[:], chosen[:]).then_inc(sem("chosen_ready"), 1)
            dve.wait_ge(sem("e3_ready"), 1)
            settle(tt(weight[:], e3[:], chosen[:], ALU.mult))
            settle(nc.vector.tensor_reduce(s3[:], weight[:], AX.X, ALU.add))
            settle(nc.vector.reciprocal(s3[:], s3[:]))
            settle(tt(weight[:], weight[:], s3[:].unsqueeze(2).broadcast_to([128, NT, E3]), ALU.mult))

            def shared(t):
                dve.wait_ge(sem("sb_mm"), t + 1)
                dve.wait_ge(sem("s_silu"), t + 1)
                if t >= 3:
                    dve.wait_ge(sem("shared_down"), t - 2)
                tt(hs[:, t % 3, :], bank[2 + t % 2][:, :], silu[:, t % 2, :], ALU.mult).then_inc(sem("hs_ready"), 1)

            def make_plan():
                dve.wait_ge(sem("places_mm"), 1)
                settle(stt(place[:], bank[6][:, 0:NT * E3].rearrange("p (t e) -> p t e", e=E3), 1.0, chosen[:],
                           ALU.add, ALU.mult))
                note(ts(place[:], place[:], -1.0, None, ALU.add))
                settle(nc.vector.tensor_copy(count[:], bank[6][:, E3 * NT:E3 * NT + E3]))
                settle(ts(chunks[:], count[:], 0.0, None, ALU.is_gt))
                for n in range(1, BLOCKS):
                    settle(stt(chunks[:], count[:], float(n * SLOTS), chunks[:], ALU.is_gt, ALU.add))
                settle(tt(cmp3[:, 0, :, :], before[:], chunks[:].unsqueeze(1).broadcast_to([128, E3, E3]), ALU.mult))
                settle(nc.vector.tensor_reduce(first[:], cmp3[:, 0, :, :], AX.X, ALU.add))
                nk = 2 * PAIRS + 1
                settle(tt(reach[:], chunk_no[:].unsqueeze(2).broadcast_to([128, nk, E3]),
                          first[:].unsqueeze(1).broadcast_to([128, nk, E3]), ALU.is_ge))
                settle(nc.vector.tensor_reduce(plan[:, 0, :], reach[:], AX.X, ALU.add))
                note(ts(plan[:, 0, :], plan[:, 0, :], -1.0, None, ALU.add))
                settle(tt(reach[:], reach[:], first[:].unsqueeze(1).broadcast_to([128, nk, E3]), ALU.mult))
                settle(nc.vector.tensor_reduce(plan[:, 2, :], reach[:], AX.X, ALU.max))
                settle(tt(plan[:, 1, :], chunk_no[:], plan[:, 2, :], ALU.subtract))
                settle(ts(plan[:, 1, :], plan[:, 1, :], float(BLOCKS), float(SLOTS), ALU.min, ALU.mult))
                note(nc.vector.tensor_copy(plan_int[:], plan[0:1, 0:2, :]))
                settle(tt(pairs[:, 0:1], first[:, E3 - 1:E3], chunks[:, E3 - 1:E3], ALU.add))
                settle(ts(pairs[:, 1:2], pairs[:, 0:1], 0.5, 0.25, ALU.mult, ALU.add))
                settle(ts(pairs[:, 2:3], pairs[:, 1:2], ROUND, ROUND, ALU.add, ALU.subtract))
                settle(nc.vector.tensor_copy(pairs_int[:], pairs[0:1, 2:3]))
                dve.sem_inc(sem("plan_ready"), 1)

            def choose(p, k):
                e = dve.value_load(plan_int[0:1, 0, bass.ds(k, 1)], min_val=0, max_val=E3 - 1)
                at = dve.value_load(plan_int[0:1, 1, bass.ds(k, 1)], min_val=0, max_val=BLOCKS * SLOTS)
                slots = slot_no[:, bass.ds(at, SLOTS)]
                for t in range(NT):
                    ts(pick[:, p, t, :], slots, place[:, t, bass.ds(e, 1)], None, ALU.is_equal)
                    last = ts(pickw[:, p, t, :], slots, place[:, t, bass.ds(e, 1)], weight[:, t, bass.ds(e, 1)],
                              ALU.is_equal, ALU.mult)
                last.then_inc(sem("pick_ready"), 1)

            def copy_tokens(p, k):
                dve.wait_ge(sem("xe_mm"), k + 1)
                nc.vector.tensor_copy(xe[:, p, :], bank[4][:, 0:SLOTS]).then_inc(sem("xe_ready"), 1)

            note(nc.vector.memset(spread[:, 0, :], 0.0))
            note(nc.vector.memset(ye[:, 0, :], 0.0))
            for t in range(HT):
                shared(t)
                if t == 4:
                    make_plan()
                    choose(1, 0)
            copy_tokens(1, 0)
            n_pairs = dve.value_load(pairs_int[0:1, 0:1], min_val=1, max_val=PAIRS)
            with dve.Fori(0, n_pairs) as i:
                for p in (1, 0):
                    k = 2 * i + 1 - p
                    dve.wait_ge(sem("spread_mm"), k + 1)
                    choose(1 - p, k + 1)
                    dve.wait_ge(sem("down_mm"), k + 1)
                    for g, (t0, t1) in enumerate(GROUPS):
                        slot = (3 * (1 - p) + g) % 2
                        n = 128 * (t1 - t0)
                        dve.wait_ge(sem("b3_mm"), 3 * k + g + 1)
                        dve.wait_ge(sem("silu_ready"), 3 * k + g + 1)
                        tt(he[:, p, t0:t1, :].rearrange("p t s -> p (t s)"), bank[2 + slot][:, 0:n], silu[:, slot, 0:n],
                           ALU.mult).then_inc(sem("he_ready"), 1)
                    copy_tokens(1 - p, k + 1)
            dve.wait_ge(sem("out_mm"), 1)
            nc.vector.tensor_copy(flat(outT[:]), bank[7][:, :]).then_inc(sem("out_ready"), 1)


def launch_arrays(inputs):
    import numpy as np

    a = {k: np.asarray(v) for k, v in inputs.items()}

    def pack(at, n, parts):
        out = np.zeros((128, n), np.float32)
        for name, (first, count) in at.items():
            v = parts[name]
            out[0:v.shape[0], first:first + count] = v
        return out

    def col(v, n=1):
        return v.reshape(n, -1).T

    def scalar(v):
        return np.broadcast_to(v.reshape(1, 1), (128, 1))

    conv = pack(CONV_AT, CONV_N, {
        "wq": a["L0_conv_wq"].T, "wk": a["L0_conv_wk"].T, "wv": a["L0_conv_wv"].T,
        "bq": col(a["L0_conv_bq"]), "bk": col(a["L0_conv_bk"]),
        "gamma_pos": scalar(a["L0_conv_gamma_pos"]), "gamma_chan": scalar(a["L0_conv_gamma_chan"]),
        "alpha": scalar(a["L0_conv_alpha"]), "beta": scalar(a["L0_conv_beta"]),
        "conv_bias": col(a["L1_conv_bias"]), "mask_weight": col(a["L1_conv_mask_weight"]),
        "filter": a["L1_conv_filter"].reshape(C, 1)})
    att = pack(ATT_AT, ATT_N, {
        "WQ": a["L2_attn_W_Q"].T, "WK": a["L2_attn_W_K"].T, "WV": a["L2_attn_W_V"].T, "WO": a["L2_attn_W_O"].T,
        "bQ": col(a["L2_attn_b_Q"]), "bK": col(a["L2_attn_b_K"]), "bV": col(a["L2_attn_b_V"]), "Wr": a["L2_ffn_Wr"].T})
    experts2 = np.concatenate([
        a["L2_ffn_W1"], a["L2_ffn_W2"].reshape(E2, 2, 128, C).transpose(0, 2, 1, 3).reshape(E2, 128, 2 * C),
        a["L2_ffn_b1"].reshape(E2, 2, 128).transpose(0, 2, 1)], axis=2)

    def spread_heads(v):
        out = np.zeros((2, 4, 32, v.shape[1]), np.float32)
        out[:, :, 0:HD, :] = v.reshape(2, 4, HD, v.shape[1])
        return out.reshape(2, 128, v.shape[1]).transpose(1, 0, 2).reshape(128, 2 * v.shape[1])

    parts = {"ffn1": a["L3_attn_ffn_w1"].T,
             "ffn2": a["L3_attn_ffn_w2"].T.reshape(FT, 128, C).transpose(1, 0, 2).reshape(128, FT * C),
             "ffn_b1": col(a["L3_attn_ffn_b1"], FT), "gate": a["L3_ffn_gate_w"]}
    for s in "gl":
        w, b = a[f"L3_attn_{s}_in_w"], a[f"L3_attn_{s}_in_b"]
        parts |= {f"{s}_in": w.T, f"{s}_out": spread_heads(a[f"L3_attn_{s}_out_w"].T), f"{s}_bq": col(b[0:C]),
                  f"{s}_bk": col(b[C:2 * C]), f"{s}_bv": spread_heads(col(b[2 * C:]))}
    l3 = pack(L3_AT, L3_N, parts)
    rows = {"bv": "L0_conv_bv", "bO": "L2_attn_b_O", "br": "L2_ffn_br", "g_out_b": "L3_attn_g_out_b",
            "l_out_b": "L3_attn_l_out_b", "ffn_b2": "L3_attn_ffn_b2", "ln1_g": "L3_attn_ln1_g",
            "ln1_b": "L3_attn_ln1_b", "ln2_g": "L3_attn_ln2_g", "ln2_b": "L3_attn_ln2_b",
            "routing_bias": "L3_ffn_routing_bias"}
    return {
        "x": a["x"].reshape(B, C, PIX),
        "conv": conv,
        "taps": a["L1_conv_weight"].transpose(1, 2, 3, 0).reshape(C, 9, C),
        "att": att,
        "experts2": experts2,
        "b2": a["L2_ffn_b2"],
        "l3": l3,
        "rows": np.concatenate([a[rows[name]] for name, _ in ROWS]),
        "sw1": a["L3_ffn_sw1"], "sw2": a["L3_ffn_sw2"], "sw3": a["L3_ffn_sw3"],
        "w1": a["L3_ffn_w1"], "w2": a["L3_ffn_w2"], "w3": a["L3_ffn_w3"],
    }


def kernel(**inputs):
    import numpy as np
    import concourse.bacc as bacc
    from concourse.bass_utils import run_bass_kernel_spmd

    nc = bacc.Bacc("TRN2", target_bir_lowering=False, num_devices=1)
    arrays = {f"in_{k}": np.ascontiguousarray(v) for k, v in launch_arrays(inputs).items()}
    args = [nc.dram_tensor(k, v.shape, mybir.dt.from_np(v.dtype), kind="ExternalInput").ap() for k, v in arrays.items()]
    out = nc.dram_tensor("out", (B, C, PIX), F32, kind="ExternalOutput").ap()
    build(nc, *args, out)
    got = run_bass_kernel_spmd(nc, [arrays], core_ids=[0])
    return got.results[0]["out"].reshape(B, C, SIDE, SIDE)
```

```python
from contextlib import ExitStack

import concourse.bass as bass
from concourse import mybir

F32 = mybir.dt.float32
BF16 = mybir.dt.bfloat16
F32R = mybir.dt.float32r
ALU = mybir.AluOpType
ACT = mybir.ActivationFunctionType
AX = mybir.AxisListType

C = 128
B = 2
SIDE = 16
PIX = SIDE * SIDE
N = B * PIX
NT = N // 128
C8 = C // 8
GROUP = 4
HEADS, HD = 8, 16
E2, H2 = 8, 256
FF = 512
FT = FF // 128
E3, K3, H3 = 16, 4, 1365
HT = -(-H3 // 128)
H_LAST = H3 - (HT - 1) * 128
H_PAD = HT * 128
SLOTS = 128
MAX_CHUNKS = E3 + (K3 * N - E3) // SLOTS
MIN_CHUNKS = -(-K3 * N // SLOTS)
PAIRS = MAX_CHUNKS // 2
BLOCKS = -(-N // SLOTS)
GROUPS = [(0, 4), (4, 8), (8, HT)]
WINDOW = 5
CREDIT = 2
EPS = 1e-5
MASKED = -1e30
ROUND = 1.5 * 2.0 ** 23

CONV_COLS = [("wq", C8), ("wk", C8), ("wv", C), ("bq", 1), ("bk", 1), ("gamma_pos", 1), ("gamma_chan", 1), ("alpha", 1),
             ("beta", 1), ("conv_bias", 1), ("mask_weight", 1), ("filter", 1)]
ATT_COLS = [("WQ", C), ("WK", C), ("WV", C), ("WO", C), ("bQ", 1), ("bK", 1), ("Wr", E2)]
EXPERT2_N = 2 * C + 2 * C + 2
L3_COLS = [("g_in", 3 * C), ("l_in", 3 * C), ("g_out", 2 * C), ("l_out", 2 * C), ("ffn1", FF), ("ffn2", FT * C),
           ("g_bq", 1), ("l_bq", 1), ("g_bk", 1), ("l_bk", 1), ("ffn_b1", FT), ("gate", E3)]
ROWS = [("bv", C), ("bV", C), ("bO", C), ("br", E2), ("g_bv", C), ("l_bv", C), ("g_out_b", C), ("l_out_b", C), ("ffn_b2", C), ("ln1_g", C), ("ln1_b", C),
        ("ln2_g", C), ("ln2_b", C), ("routing_bias", E3)]


def columns(table):
    at, out = 0, {}
    for name, n in table:
        out[name] = (at, n)
        at += n
    return out, at


CONV_AT, CONV_N = columns(CONV_COLS)
ATT_AT, ATT_N = columns(ATT_COLS)
L3_AT, L3_N = columns(L3_COLS)
ROW_AT, ROW_N = columns(ROWS)

LN_ATT2, LN_FFN2, LN_ATT3, LN_MID3, LN_END3, LN_FFN3 = range(6)



def turn_of(k):
    return k - (k > LN_END3)


GLOBAL_HEADS, LOCAL_HEADS = 2, 4
WINDOWS = [(0, 0, 128 - WINDOW), (64, 128 - WINDOW, 192 - WINDOW), (128, 192 - WINDOW, PIX)]
UNITS = []
for _b in range(B):
    UNITS += [("g", _b, t, h) for t in range(2) for h in range(0, HEADS, GLOBAL_HEADS)]
    UNITS += [("l", _b, w, h) for w in range(len(WINDOWS)) for h in range(0, HEADS, LOCAL_HEADS)]
UNITS_B = len(UNITS) // B
UNITS_G = 2 * HEADS // GLOBAL_HEADS


def build(nc, x_in, conv_w, taps_w, att_w, experts2_w, b2_w, l3_w, rows_w, sw1_in, sw2_in, sw3_in, w1_in, w2_in, w3_in, out):
    with ExitStack() as ctx:
        sems = {}

        def sem(name):
            if name not in sems:
                sems[name] = ctx.enter_context(nc.semaphore(name))
            return sems[name]

        def sb(name, shape, dt=F32):
            return ctx.enter_context(nc.sbuf_tensor(name, shape, dt))

        ROOM = 13312
        shared_room = sb("shared_room", [128, ROOM])
        used = {}

        def room(phase, shape):
            parts, n = shape[0], 1
            for m in shape[1:]:
                n *= m
            at = used.get(phase, 0)
            used[phase] = at + n
            assert used[phase] <= ROOM, used
            view = shared_room[0:parts, at:at + n]
            letters = "abcd"[:len(shape) - 1]
            if len(letters) == 1:
                return view
            return view.rearrange(f"p ({' '.join(letters)}) -> p {' '.join(letters)}",
                                  **dict(zip(letters, shape[1:])))

        bank = [ctx.enter_context(nc.psum_tensor(f"bank{i}", [128, 512], F32)) for i in range(8)]

        conv = sb("conv", [128, CONV_N])
        taps = room("layers01", [128, 9, C])
        att = sb("att", [128, ATT_N])
        b2 = sb("b2", [E2, C])
        l3 = sb("l3", [128, L3_N])
        rows = sb("rows", [128, ROW_N])

        def cc(name):
            a, n = CONV_AT[name]
            return conv[:, a:a + n]

        def ca(name):
            a, n = ATT_AT[name]
            return att[:, a:a + n]

        def c3(name):
            a, n = L3_AT[name]
            return l3[:, a:a + n]

        def row(name, mid=None):
            a, n = ROW_AT[name]
            r = rows[:, a:a + n]
            return r if mid is None else r.unsqueeze(1).broadcast_to([128, mid, n])

        ident = sb("ident", [128, 128])
        ident_bf = sb("ident_bf", [128, 128], BF16)
        band = sb("band", [128, 128], BF16)
        ones = sb("ones", [128, 128])
        group_mean = sb("group_mean", [128, 128])
        head_block = sb("head_block", [128, 128])
        head_mask = sb("head_mask", [128, HEADS])
        den_row = sb("den_row", [128, 4])
        ramp = sb("ramp", [128, SIDE])
        pos = sb("pos", [128, SIDE])
        before = sb("before", [128, E3, E3])
        before2 = sb("before2", [128, E2, E2])
        earlier_bf = sb("earlier_bf", [128, 128], BF16)
        ones_bf = sb("ones_bf", [128, 128], BF16)
        slot_no = sb("slot_no", [128, (BLOCKS + 1) * SLOTS])
        chunk_no = sb("chunk_no", [128, 2 * PAIRS + 2])
        chunk_odd = sb("chunk_odd", [128, PAIRS + 1, 2])
        chunk_half = sb("chunk_half", [128, PAIRS + 1, 2])

        x0 = room("layers01", [128, B, PIX])
        q0 = room("layers01", [C8, N])
        k0 = room("layers01", [C8, N])
        v0T = room("layers01", [128, NT, C])
        x0T = room("layers01", [128, NT, C])
        p0 = room("layers01", [128, B, 2, PIX])
        p0T = room("layers01", [128, B, 2, PIX])
        pc = room("layers01", [128, B, C])
        pcT = room("layers01", [128, B, C])
        nmax0 = sb("nmax0", [128, B, 2])
        sum0 = sb("sum0", [128, B, 2])
        minc = sb("minc", [128, B])
        sumc = sb("sumc", [128, B])
        mix = sb("mix", [128, 4])
        x1 = sb("x1", [128, B, PIX])
        gst = sb("gst", [128, B, 6])
        gmv = sb("gmv", [128, B, 2])
        gdev = sb("gdev", [128, B])
        gm = sb("gm", [128, B])
        gvar = sb("gvar", [128, B])
        gr = sb("gr", [128, 4, B])
        gn = room("layers01", [128, B, SIDE, SIDE])
        sums = sb("sums", [128, 2, B, SIDE])
        weighted = sb("weighted", [128, 2, B, SIDE])
        moment = sb("moment", [128, 2, B])
        total = sb("total", [128, B])
        mu = sb("mu", [128, 2, B])
        mask_w = sb("mask_w", [128, 1])
        dist = sb("dist", [128, 2, B, SIDE])
        mask = room("layers01", [128, B, SIDE, SIDE])
        pad = room("layers01", [128, B, SIDE + 2, SIDE + 2])
        x2 = sb("x2", [128, B, PIX])

        t2 = room("layer2", [128, NT, C])
        t3 = sb("t3", [128, NT, C])
        t4 = sb("t4", [128, NT, C])
        u3 = sb("u3", [128, NT, C])
        z3 = sb("z3", [128, NT, C])
        t5 = sb("t5", [128, NT, C])
        y = [None if k == LN_END3 else sb(f"y{k}", [128, NT, C]) for k in range(6)]
        yT = [None if k == LN_END3 else sb(f"yT{k}", [128, N]) for k in range(6)]
        lst = sb("lst", [128, NT, 6])
        lmv = sb("lmv", [128, 6, NT, 2])
        lve = sb("lve", [128, 6, NT])
        lsd = sb("lsd", [128, 6, NT])
        lr0 = sb("lr0", [128, 6, NT])
        nothing = sb("nothing", [1, 1])
        lra = sb("lra", [128, 2, NT])
        lr = sb("lr", [128, 6, NT])

        kmax = sb("kmax", [128, B])
        knmax = sb("knmax", [128, B])
        kq = sb("kq", [128, B])
        kqb = room("layer2", [128, B, 128])
        ek = room("layer2", [128, B, PIX])
        sek = sb("sek", [128, B])
        ekT = room("layer2", [128, NT, C])
        v2 = room("layer2", [128, NT, C])
        kv = room("layer2", [128, B, C])
        ksum = room("layer2", [128, B, HEADS])
        qmax = sb("qmax", [128, NT * HEADS])
        qs = room("layer2", [128, NT * HEADS, HD])
        eq = room("layer2", [128, NT, C])
        eqT = room("layer2", [128, N])
        rd2 = sb("rd2", [128, NT * HEADS])
        rden2 = room("layer2", [128, NT, HEADS, HD])
        num2 = room("layer2", [128, N])
        heads2 = room("layer2", [128, N])

        lg2 = sb("lg2", [128, NT, E2])
        m2 = sb("m2", [128, NT])
        e2 = sb("e2", [128, NT, E2])
        s2 = sb("s2", [128, NT])
        pr2 = sb("pr2", [128, NT, E2])
        cmp2 = room("route2", [128, 2, NT * E2, E2])
        rank2 = sb("rank2", [128, NT, E2])
        comb2 = sb("comb2", [128, NT, E2])
        comb2T = sb("comb2T", [E2, N])
        ew2 = [sb(f"ew2_{p}", [128, EXPERT2_N]) for p in range(2)]
        h2 = sb("h2", [128, 4, N])

        q3 = [room("keys", [128, N]) for s in "gl"]
        k3 = [room("keys", [128, N]) for s in "gl"]
        km3 = [[room("keys", [128, HEADS, PIX]) for b in range(B)] for s in "gl"]
        vg = sb("vg", [128, NT, HEADS, 32])
        vl = sb("vl", [128, B * len(WINDOWS), HEADS, 32])
        nmax3 = sb("nmax3", [128, len(UNITS), 4])
        p3 = sb("p3", [128, 2, 512])
        p3T = room("keys", [128, 2, 512])
        o3 = sb("o3", [128, 2, 512])
        rd3 = sb("rd3", [128, 16])
        rd3_wide = sb("rd3_wide", [128, 4, 4, 32])
        ob3 = sb("ob3", [128, B, 2, 2, PIX])
        hf3 = room("keys", [128, FT, N])

        lg3 = sb("lg3", [128, NT, E3])
        m3 = sb("m3", [128, NT])
        e3 = sb("e3", [128, NT, E3])
        s3 = sb("s3", [128, NT])
        cmp3 = room("mixture", [128, 2, NT * E3, E3])
        rank3 = sb("rank3", [128, NT, E3])
        chosen = sb("chosen", [128, NT, E3])
        chosen_bf = sb("chosen_bf", [128, NT, E3], BF16)
        weight = sb("weight", [128, NT, E3])
        left = sb("left", [128, NT, E3])
        place = sb("place", [128, NT, E3])
        count = sb("count", [128, E3])
        chunks = sb("chunks", [128, E3])
        first = sb("first", [128, E3])
        reach = room("mixture", [128, 2 * PAIRS + 2, E3])
        NK = 2 * PAIRS + 2
        plan = sb("plan", [128, 5, NK])
        plan_int = sb("plan_int", [1, 3, NK], mybir.dt.int32)
        pairs = sb("pairs", [128, 6])
        pairs_int = sb("pairs_int", [1, 2], mybir.dt.int32)
        w1 = [sb(f"w1_{p}", [128, H_PAD]) for p in range(2)]
        w2 = [sb(f"w2_{p}", [128, H_PAD]) for p in range(2)]
        w3 = [sb(f"w3_{p}", [128, HT, C]) for p in range(2)]
        tokens_left = room("mixture", [128, NT, C])
        silu = room("mixture", [128, 2, 512])
        hs = room("mixture", [128, 3, N])
        he = room("mixture", [128, 2, HT, SLOTS])
        xe = room("mixture", [128, 2, SLOTS])
        outT = room("mixture", [128, B, PIX])

        pick_bf = sb("pick_bf", [128, 2, NT, SLOTS], BF16)
        y_bf = sb("y_bf", [128, NT, 3, C], BF16)
        spread = sb("spread", [128, 2, N], F32R)
        ye_hi = sb("ye_hi", [128, 2, C], F32R)
        ye_lo = sb("ye_lo", [128, 2, C], F32R)
        slot_weight = sb("slot_weight", [128, 2])
        weight_bf = sb("weight_bf", [128, NT, E3, 3], BF16)

        block = ctx.enter_context(nc.Block())

        @block.sync
        def _(sp):
            sp.dma_start(x0[:], x_in.rearrange("b c n -> c b n")).then_inc(sem("x_in"), 16)
            sp.dma_start(conv[:], conv_w).then_inc(sem("conv_in"), 16)
            sp.dma_start(rows[:], rows_w.partition_broadcast(128)).then_inc(sem("rows_in"), 16)
            sp.dma_start(taps[:], taps_w).then_inc(sem("taps_in"), 16)
            sp.dma_start(att[:], att_w).then_inc(sem("att_in"), 16)
            sp.dma_start(b2[:], b2_w).then_inc(sem("b2_in"), 16)
            sp.dma_start(l3[:], l3_w).then_inc(sem("l3_in"), 16)
            for p in range(2):
                sp.dma_start(ew2[p][:], experts2_w[p, :, :]).then_inc(sem(f"ew2_in{p}"), 16)
            with sp.Fori(0, E2 // 2 - 1) as i:
                for p in range(2):
                    sp.wait_ge(sem("expert2_mm"), CREDIT + 2 * i + p + 1)
                    sp.dma_start(ew2[p][:], experts2_w[2 * i + p + 2, :, :]).then_inc(sem(f"ew2_in{p}"), 16)

            def load(p, a1, a2, a3):
                full = (HT - 1) * 128
                sp.dma_start(w1[p][:, 0:H3], a1).then_inc(sem(f"w1_in{p}"), 16)
                sp.dma_start(w2[p][:, 0:H3], a2).then_inc(sem(f"w2_in{p}"), 16)
                sp.dma_start(w3[p][:, 0:HT - 1, :], a3[0:full, :].rearrange("(t p) d -> p t d", p=128))\
                    .then_inc(sem(f"w3_in{p}"), 16)
                sp.dma_start(w3[p][0:H_LAST, HT - 1, :], a3[full:H3, :]).then_inc(sem(f"w3_in{p}"), 16)

            load(0, sw1_in, sw2_in, sw3_in)
            sp.wait_ge(sem("plan_ready"), 1)
            n_pairs = sp.value_load(pairs_int[0:1, 0:1], min_val=MIN_CHUNKS // 2, max_val=PAIRS)

            def load_chunk(p, k, always=False):
                sp.wait_ge(sem("down_mm"), k + 1)
                e = sp.value_load(plan_int[0:1, 0, bass.ds(k, 1)], min_val=0, max_val=E3 - 1)
                weights = (w1_in[bass.ds(e, 1), :, :].rearrange("e c h -> c (e h)"),
                           w2_in[bass.ds(e, 1), :, :].rearrange("e c h -> c (e h)"),
                           w3_in[bass.ds(e, 1), :, :].rearrange("e h d -> (e h) d"))
                if always:
                    load(p, *weights)
                    return
                other = sp.value_load(plan_int[0:1, 2, bass.ds(k, 1)], min_val=0, max_val=1)
                with sp.If(other > 0):
                    load(p, *weights)
                with sp.If(other < 1):
                    sp.sem_inc(sem(f"w1_in{p}"), 16)
                    sp.sem_inc(sem(f"w2_in{p}"), 16)
                    sp.sem_inc(sem(f"w3_in{p}"), 32)

            load_chunk(1, 0, always=True)
            load_chunk(0, 1, always=True)
            with sp.Fori(1, n_pairs) as i:
                load_chunk(1, 2 * i)
                load_chunk(0, 2 * i + 1)
            single = sp.value_load(pairs_int[0:1, 1:2], min_val=0, max_val=1)
            with sp.If(single > 0):
                load_chunk(1, 2 * n_pairs)
            sp.wait_ge(sem("out_ready"), 1)
            sp.dma_start(out.rearrange("b c n -> c b n"), outT[:]).then_inc(sem("out_stored"), 16)
            sp.wait_ge(sem("out_stored"), 16)

        @block.gpsimd
        def _(pool):
            def select(out, pattern, base, mult, op, fill):
                return nc.gpsimd.affine_select(out=out, in_=out, compare_op=op, fill=fill, base=base, pattern=pattern,
                                               channel_multiplier=mult)

            made = [0]

            def make(ins):
                made[0] += 1
                ins.then_inc(sem("pool_step"), 1)
                pool.wait_ge(sem("pool_step"), made[0])

            make(nc.gpsimd.memset(ident[:], 0.0))
            make(select(ident[:], [[-1, 128]], 0, 1, ALU.not_equal, 1.0))
            nc.gpsimd.memset(ones[:], 1.0).then_inc(sem("ident_made"), 1)
            nc.gpsimd.memset(pad[:], 0.0).then_inc(sem("pad_made"), 1)
            g = group_mean[:].rearrange("p (g c) -> p g c", c=GROUP)
            make(nc.gpsimd.memset(group_mean[:], 1.0 / GROUP))
            make(select(g, [[-GROUP, C // GROUP], [0, GROUP]], 0, 1, ALU.is_ge, 0.0))
            make(select(g, [[GROUP, C // GROUP], [0, GROUP]], GROUP - 1, -1, ALU.is_ge, 0.0))
            nc.gpsimd.iota(ramp[:], pattern=[[1, SIDE]], base=1, channel_multiplier=0,
                           allow_small_or_imprecise_dtypes=True).then_inc(sem("group_made"), 1)
            g = head_block[:].rearrange("p (g c) -> p g c", c=HD)
            make(nc.gpsimd.memset(head_block[:], 1.0))
            make(select(g, [[-HD, HEADS], [0, HD]], 0, 1, ALU.is_ge, 0.0))
            make(select(g, [[HD, HEADS], [0, HD]], HD - 1, -1, ALU.is_ge, 0.0))
            make(nc.gpsimd.memset(head_mask[:], 1.0))
            make(select(head_mask[:], [[-HD, HEADS]], 0, 1, ALU.is_ge, 0.0))
            make(select(head_mask[:], [[HD, HEADS]], HD - 1, -1, ALU.is_ge, 0.0))
            make(nc.gpsimd.memset(before2[:], 1.0))
            make(select(before2[:], [[1, E2], [-1, E2]], -1, 0, ALU.is_ge, 0.0))
            make(nc.gpsimd.memset(before[:], 1.0))
            make(select(before[:], [[1, E3], [-1, E3]], -1, 0, ALU.is_ge, 0.0))
            make(nc.gpsimd.memset(den_row[:], 0.0))
            make(select(den_row[:], [[-32, 4]], -HD, 1, ALU.not_equal, 1.0))
            make(nc.gpsimd.memset(band[:], 0.0))
            make(select(band[:], [[-1, 128]], WINDOW, 1, ALU.is_ge, MASKED))
            make(select(band[:], [[1, 128]], WINDOW, -1, ALU.is_ge, MASKED))
            make(nc.gpsimd.tensor_copy(ident_bf[:], ident[:]))
            make(nc.gpsimd.memset(ones_bf[:], 1.0))
            make(nc.gpsimd.memset(earlier_bf[:], 1.0))
            make(select(earlier_bf[:], [[1, 128]], -1, -1, ALU.is_ge, 0.0))
            make(nc.gpsimd.iota(slot_no[:], pattern=[[1, (BLOCKS + 1) * SLOTS]], base=0, channel_multiplier=0,
                                allow_small_or_imprecise_dtypes=True))
            for numbers, pattern in ((chunk_no, [[1, 2 * PAIRS + 2]]), (chunk_odd, [[0, PAIRS + 1], [1, 2]]),
                                     (chunk_half, [[1, PAIRS + 1], [0, 2]])):
                make(nc.gpsimd.iota(numbers[:], pattern=pattern, base=0, channel_multiplier=0,
                                    allow_small_or_imprecise_dtypes=True))
            for p in range(2):
                make(nc.gpsimd.memset(w1[p][:, H3:H_PAD], 0.0))
                make(nc.gpsimd.memset(w2[p][:, H3:H_PAD], 0.0))
            make(nc.gpsimd.memset(vg[:], 0.0))
            make(nc.gpsimd.memset(vl[:], 0.0))
            make(nc.gpsimd.memset(vg[:, :, :, HD:HD + 1], 1.0))
            nc.gpsimd.memset(vl[:, :, :, HD:HD + 1], 1.0).then_inc(sem("masks_made"), 1)
            for s in range(2):
                pool.wait_ge(sem("k3_ready"), s + 1)
                for h in range(HEADS):
                    last = nc.gpsimd.tensor_scalar(km3[s][1][:, h, :], k3[s][:, PIX:N], head_mask[:, h:h + 1], 0.0,
                                                   ALU.mult, ALU.add)
                last.then_inc(sem("km3_image1"), 1)

        @block.tensor
        def _(pe):
            mm = nc.tensor.matmul
            tr = nc.tensor.transpose

            pe.sem_inc(sem("expert2_mm"), CREDIT)
            pe.sem_inc(sem("down_mm"), 1)
            pe.sem_inc(sem("scatter_mm"), 1)
            pe.sem_inc(sem("spread_mm"), 1)
            pe.wait_ge(sem("x_in"), 16)
            pe.wait_ge(sem("conv_in"), 16)
            pe.wait_ge(sem("ident_made"), 1)
            xf = x0[:].rearrange("p b n -> p (b n)")
            mm(bank[0][0:C8, :], cc("wq"), xf, start=True, stop=True).then_inc(sem("q0_mm"), 1)
            mm(bank[1][0:C8, :], cc("wk"), xf, start=True, stop=True).then_inc(sem("k0_mm"), 1)
            for t in range(NT):
                last = tr(bank[3][:, 128 * t:128 * t + 128], xf[:, 128 * t:128 * t + 128], ident[:])
            last.then_inc(sem("x0T_mm"), 1)
            for t in range(NT):
                last = mm(bank[2][:, 128 * t:128 * t + 128], xf[:, 128 * t:128 * t + 128], cc("wv"),
                          start=True, stop=True)
            last.then_inc(sem("v0_mm"), 1)
            pe.wait_ge(sem("q0_ready"), 1)
            pe.wait_ge(sem("k0_ready"), 1)
            for b in range(B):
                for t in range(2):
                    last = mm(bank[4 + b][:, PIX * t:PIX * t + PIX], q0[:, b * PIX + 128 * t:b * PIX + 128 * t + 128],
                              k0[:, b * PIX:b * PIX + PIX], start=True, stop=True)
                last.then_inc(sem("energy_mm"), 1)
            pe.wait_ge(sem("x0T_ready"), 1)
            for b in range(B):
                for t in range(2):
                    last = mm(bank[6][:, C * b:C * b + C], x0T[:, 2 * b + t, :], x0T[:, 2 * b + t, :],
                              start=(t == 0), stop=(t == 1))
            last.then_inc(sem("energyc_mm"), 1)
            pe.wait_ge(sem("v0_ready"), 1)
            for b in range(B):
                pe.wait_ge(sem("p0_ready"), 4 * b + 4)
                for j in range(2):
                    for t in range(2):
                        last = tr(bank[b][:, j * PIX + 128 * t:j * PIX + 128 * t + 128],
                                  p0[:, b, t, 128 * j:128 * j + 128], ident[:])
                last.then_inc(sem("p0T_mm"), 1)
            pe.wait_ge(sem("pc_ready"), B)
            for b in range(B):
                last = tr(bank[2][:, C * b:C * b + C], pc[:, b, :], ident[:])
            last.then_inc(sem("pcT_mm"), 1)
            pe.wait_ge(sem("pcT_ready"), 1)
            for b in range(B):
                pe.wait_ge(sem("p0T_ready"), b + 1)
                for j in range(2):
                    mm(bank[7 - 4 * b][:, 0:PIX], v0T[:, 2 * b + j, :], p0T[:, b, j, :],
                       start=(j == 0), stop=False)
                mm(bank[7 - 4 * b][:, 0:PIX], pcT[:, b, :], x0[:, b, :], start=False, stop=True)\
                    .then_inc(sem("layer0_mm"), 1)
            pe.wait_ge(sem("group_made"), 1)
            pe.wait_ge(sem("gmv_ready"), 1)
            mm(bank[0][:, 0:B], group_mean[:], gmv[:, :, 0], start=True, stop=True).then_inc(sem("gmean_mm"), 1)
            pe.wait_ge(sem("gdev_ready"), 1)
            mm(bank[1][:, 0:B], group_mean[:], gdev[:], start=True, stop=True).then_inc(sem("gvar_mm"), 1)
            pe.wait_ge(sem("taps_in"), 16)
            pe.wait_ge(sem("pad_ready"), 1)
            for k in range(9):
                i, j = k // 3, k % 3
                last = mm(bank[2][:, :], taps[:, k, :], pad[:, :, i:i + SIDE, j:j + SIDE], start=(k == 0), stop=(k == 8))
            last.then_inc(sem("conv_mm"), 1)
            pe.wait_ge(sem("x2_ready"), 1)
            x2f = x2[:].rearrange("p b n -> p (b n)")
            for t in range(NT):
                last = tr(bank[3][:, 128 * t:128 * t + 128], x2f[:, 128 * t:128 * t + 128], ident[:])
            last.then_inc(sem("t2_mm"), 1)

            def ln_transpose(k, b):
                for t in range(NT):
                    pe.wait_ge(sem("y_ready"), NT * turn_of(k) + t + 1)
                    tr(bank[b + t // 2][:, 128 * (t % 2):128 * (t % 2) + 128], y[k][:, t, :], ident[:]).then_inc(sem("yT_mm"), 1)

            ln_transpose(LN_ATT2, 4)
            pe.wait_ge(sem("att_in"), 16)
            pe.wait_ge(sem("yT_ready"), 2 * turn_of(LN_ATT2) + 2)
            yt = yT[LN_ATT2]
            mm(bank[0][:, :], ca("WK"), yt[:], start=True, stop=True).then_inc(sem("k2_mm"), 1)
            for t in range(NT):
                mm(bank[1][:, 128 * t:128 * t + 128], yt[:, 128 * t:128 * t + 128], ca("WQ"), start=(t == 0),
                   stop=False, skip_group_check=True)
            for t in range(NT):
                last = mm(bank[2][:, 128 * t:128 * t + 128], yt[:, 128 * t:128 * t + 128], ca("WV"),
                          start=True, stop=True)
            last.then_inc(sem("v2_mm"), 1)
            for t in range(NT):
                pe.wait_ge(sem("kqb_ready"), t // 2 + 1)
                last = mm(bank[1][:, 128 * t:128 * t + 128], kqb[:, t // 2, :], ident[:], start=False,
                          stop=(t == NT - 1), skip_group_check=True)
            last.then_inc(sem("q2_mm"), 1)
            pe.wait_ge(sem("t2_ready"), 1)
            for b in range(B):
                pe.wait_ge(sem("ek_ready"), b + 1)
                for t in range(2):
                    last = tr(bank[3][:, (2 * b + t) * 128:(2 * b + t) * 128 + 128], ek[:, b, 128 * t:128 * t + 128],
                              ident[:])
            last.then_inc(sem("ekT_mm"), 1)
            pe.wait_ge(sem("ekT_ready"), 1)
            pe.wait_ge(sem("v2_ready"), 1)
            for b in range(B):
                for t in range(2):
                    last = mm(bank[5][:, C * b:C * b + C], ekT[:, 2 * b + t, :], v2[:, 2 * b + t, :],
                              start=(t == 0), stop=(t == 1))
            last.then_inc(sem("kv_mm"), 1)
            pe.wait_ge(sem("eq_ready"), 1)
            pe.wait_ge(sem("ekT_ready"), 1)
            for t in range(NT):
                last = tr(bank[3][:, 128 * t:128 * t + 128], eq[:, t, :], ident[:])
            last.then_inc(sem("eqT_mm"), 1)
            pe.wait_ge(sem("eqT_ready"), 1)
            pe.wait_ge(sem("kv_ready"), 2)
            for t in range(NT):
                last = mm(bank[4][:, HEADS * t:HEADS * t + HEADS], eqT[:, 128 * t:128 * t + 128], ksum[:, t // 2, :],
                          start=True, stop=True)
            last.then_inc(sem("den2_mm"), 1)
            for b in range(B):
                last = mm(bank[6][:, PIX * b:PIX * b + PIX], kv[:, b, :], eqT[:, PIX * b:PIX * b + PIX],
                          start=True, stop=True)
            last.then_inc(sem("num2_mm"), 1)
            pe.wait_ge(sem("rden2_ready"), 1)
            for t in range(NT):
                last = mm(bank[7][:, 128 * t:128 * t + 128],
                          rden2[:, t, :, :].rearrange("p h c -> p (h c)"), ident[:],
                          start=True, stop=True)
            last.then_inc(sem("spread2_mm"), 1)
            pe.wait_ge(sem("heads2_ready"), 1)
            for t in range(NT):
                last = mm(bank[0][:, 128 * t:128 * t + 128], heads2[:, 128 * t:128 * t + 128], ca("WO"),
                          start=True, stop=True)
            last.then_inc(sem("att2_mm"), 1)

            ln_transpose(LN_FFN2, 4)
            pe.wait_ge(sem("yT_ready"), 2 * turn_of(LN_FFN2) + 2)
            yt = yT[LN_FFN2]
            for t in range(NT):
                last = mm(bank[1][:, E2 * t:E2 * t + E2], yt[:, 128 * t:128 * t + 128], ca("Wr"), start=True, stop=True)
            last.then_inc(sem("route2_mm"), 1)
            pe.wait_ge(sem("heads2_ready"), 1)
            pe.wait_ge(sem("yT_ready"), 2 * turn_of(LN_FFN2) + 2)
            pe.wait_ge(sem("kv_ready"), 2)
            pe.wait_ge(sem("eqT_ready"), 1)
            with pe.Fori(0, E2 // 2) as i:
                for p in range(2):
                    pe.wait_ge(sem(f"ew2_in{p}"), 16 * i + 16)
                    pe.wait_ge(sem("h2_ready"), 4 * i + 2 * p + 2)
                    for half in range(2):
                        mm(bank[4 + 2 * p + half][:, :], ew2[p][:, C * half:C * half + C], yt[:],
                           start=True, stop=True).then_inc(sem("hidden2_mm"), 1)
                for p in range(2):
                    pe.wait_ge(sem("y2_added"), 2 * i + p + 1)
                    for half in range(2):
                        pe.wait_ge(sem("h2_ready"), 2 * CREDIT + 4 * i + 2 * p + half + 1)
                        for t in range(NT):
                            last = mm(bank[2 + p][:, 128 * t:128 * t + 128], h2[:, 2 * p + half, 128 * t:128 * t + 128],
                                      ew2[p][:, 2 * C + C * half:3 * C + C * half],
                                      start=(half == 0 and t == 0), stop=(half == 1 and t == NT - 1),
                                      skip_group_check=True)
                    last.then_inc(sem("expert2_mm"), 1)
            pe.wait_ge(sem("comb2_ready"), 1)
            for t in range(NT):
                last = tr(bank[0][0:E2, 128 * t:128 * t + 128], comb2[:, t, :], ident[:])
            last.then_inc(sem("comb2T_mm"), 1)
            pe.wait_ge(sem("comb2T_ready"), 1)
            pe.wait_ge(sem("b2_in"), 16)
            for t in range(NT):
                last = mm(bank[1][:, 128 * t:128 * t + 128], comb2T[:, 128 * t:128 * t + 128], b2[:],
                          start=True, stop=True)
            last.then_inc(sem("bias2_mm"), 1)

            ln_transpose(LN_ATT3, 2)
            pe.wait_ge(sem("l3_in"), 16)
            pe.wait_ge(sem("yT_ready"), 2 * turn_of(LN_ATT3) + 2)
            yt = yT[LN_ATT3]
            for s, name in enumerate(("g_in", "l_in")):
                w = c3(name)
                mm(bank[4 + 2 * s][:, :], w[:, 0:C], yt[:], start=True, stop=True).then_inc(sem("q3_mm"), 1)
                mm(bank[5 + 2 * s][:, :], w[:, C:2 * C], yt[:], start=True, stop=True).then_inc(sem("k3_mm"), 1)
            for t in range(NT):
                last = mm(bank[2][:, 128 * t:128 * t + 128], yt[:, 128 * t:128 * t + 128], c3("g_in")[:, 2 * C:3 * C],
                          start=True, stop=True)
            last.then_inc(sem("vg_mm"), 1)
            for b in range(B):
                for w, (start, _, _) in enumerate(WINDOWS):
                    last = mm(bank[b][:, 128 * w:128 * w + 128], yt[:, b * PIX + start:b * PIX + start + 128],
                              c3("l_in")[:, 2 * C:3 * C], start=True, stop=True)
            last.then_inc(sem("vl_mm"), 1)

            def scores(u):
                kind, b, t, h = UNITS[u]
                if u >= 2:
                    pe.wait_ge(sem("exp3"), u - 1)
                if kind == "g":
                    pe.wait_ge(sem("km3_image1" if b else "km3_global0"), 1)
                    mm(bank[u % 2][:, :], q3[0][:, b * PIX + 128 * t:b * PIX + 128 * t + 128],
                       km3[0][b][:, h:h + GLOBAL_HEADS, :], start=True, stop=True).then_inc(sem("score3_mm"), 1)
                else:
                    start = WINDOWS[t][0]
                    if b == 0:
                        pe.wait_ge(sem("km3_local0"), 1)
                    else:
                        pe.wait_ge(sem("km3_image1"), 2)
                    mm(bank[u % 2][:, :], q3[1][:, b * PIX + start:b * PIX + start + 128],
                       km3[1][b][:, h:h + LOCAL_HEADS, start:start + 128], start=True, stop=False)
                    mm(bank[u % 2][:, :], ident_bf[:], band[:].unsqueeze(1).broadcast_to([128, LOCAL_HEADS, 128]),
                       start=False, stop=True).then_inc(sem("score3_mm"), 1)

            def turn(u):
                pe.wait_ge(sem("exp3"), u + 1)
                if u >= 2:
                    pe.wait_ge(sem("p3T_ready"), u - 1)
                for n in range(4):
                    last = tr(bank[2 + u % 2][:, 128 * n:128 * n + 128], p3[:, u % 2, 128 * n:128 * n + 128], ident[:])
                last.then_inc(sem("p3T_mm"), 1)

            def attend(u):
                kind, b, t, h0 = UNITS[u]
                if u % UNITS_B == 0 and b:
                    pe.wait_ge(sem("o3_copied"), 1)
                if u % UNITS_B == UNITS_G and b:
                    pe.wait_ge(sem("o3_copied"), 2)
                pe.wait_ge(sem("p3T_ready"), u + 1)
                if kind == "g":
                    for n in range(GLOBAL_HEADS):
                        h = h0 + n
                        r = 32 * (h % 4)
                        for j in range(2):
                            last = mm(bank[4][r:r + 32, h // 4 * PIX + 128 * t:h // 4 * PIX + 128 * t + 128],
                                      vg[:, 2 * b + j, h, :], p3T[:, u % 2, (2 * n + j) * 128:(2 * n + j) * 128 + 128],
                                      start=(j == 0), stop=(j == 1), tile_position=(0, r))
                else:
                    start, first, end = WINDOWS[t]
                    for n in range(LOCAL_HEADS):
                        h = h0 + n
                        r = 32 * (h % 4)
                        last = mm(bank[5][r:r + 32, h // 4 * PIX + first:h // 4 * PIX + end],
                                  vl[:, b * len(WINDOWS) + t, h, :],
                                  p3T[:, u % 2, 128 * n + first - start:128 * n + end - start],
                                  start=True, stop=True, tile_position=(0, r))
                last.then_inc(sem("attend3"), 1)

            def denominators(n):
                pe.wait_ge(sem("o3_copied"), n + 1)
                if n:
                    pe.wait_ge(sem("ob3_ready"), n)
                for q in range(4):
                    last = mm(bank[6][:, 4 * q:4 * q + 4], o3[:, n % 2, 128 * q:128 * q + 128], den_row[:],
                              start=True, stop=True)
                last.then_inc(sem("den3_mm"), 1)

            def spread_quotients(n):
                pe.wait_ge(sem("rd3_ready"), n + 1)
                for q in range(4):
                    last = mm(bank[6][:, 128 * q:128 * q + 128],
                              rd3_wide[:, q, :, :].rearrange("p j c -> p (j c)"), ident[:],
                              start=True, stop=True)
                last.then_inc(sem("spread3_mm"), 1)

            def project(b):
                pe.wait_ge(sem("ob3_ready"), 2 * b + 2)
                for t in range(2):
                    for s, name in enumerate(("g_out", "l_out")):
                        for half in range(2):
                            last = mm(bank[7][:, (2 * b + t) * 128:(2 * b + t) * 128 + 128],
                                      ob3[:, b, s, half, 128 * t:128 * t + 128], c3(name)[:, C * half:C * half + C],
                                      start=(s == 0 and half == 0), stop=(s == 1 and half == 1))
                last.then_inc(sem("att3_mm"), 1)

            pe.wait_ge(sem("masks_made"), 1)
            pe.wait_ge(sem("q3_ready"), 2)
            pe.wait_ge(sem("k3_ready"), 2)
            pe.wait_ge(sem("v3_ready"), 2)
            for u in range(len(UNITS) + 2):
                if u < len(UNITS):
                    scores(u)
                if 1 <= u <= len(UNITS):
                    turn(u - 1)
                if u >= 2:
                    attend(u - 2)
                for n, end in enumerate((UNITS_G, UNITS_B, UNITS_B + UNITS_G)):
                    if u == end + 3:
                        denominators(n)
                    if u == end + 4:
                        spread_quotients(n)
                if u == UNITS_B + 7:
                    project(0)
            denominators(3)
            spread_quotients(3)
            project(1)

            ln_transpose(LN_MID3, 0)
            pe.wait_ge(sem("yT_ready"), 2 * turn_of(LN_MID3) + 2)
            for f in range(FT):
                mm(bank[1 + f][:, :], c3("ffn1")[:, 128 * f:128 * f + 128], yT[LN_MID3][:], start=True, stop=True)\
                    .then_inc(sem("ff3_mm"), 1)
            for f in range(FT):
                pe.wait_ge(sem("hf3_ready"), f + 1)
                for t in range(NT):
                    last = mm(bank[6][:, 128 * t:128 * t + 128], hf3[:, f, 128 * t:128 * t + 128],
                              c3("ffn2")[:, C * f:C * f + C], start=(f == 0 and t == 0),
                              stop=(f == FT - 1 and t == NT - 1), skip_group_check=True)
            last.then_inc(sem("ffn3_mm"), 1)

            ln_transpose(LN_FFN3, 5)
            pe.wait_ge(sem("yT_ready"), 2 * turn_of(LN_FFN3) + 2)
            yt = yT[LN_FFN3]
            for t in range(NT):
                last = mm(bank[4][:, E3 * t:E3 * t + E3], yt[:, 128 * t:128 * t + 128], c3("gate"), start=True, stop=True)
            last.then_inc(sem("route3_mm"), 1)

            def shared_up(t):
                if t >= 2:
                    pe.wait_ge(sem("hs_ready"), t - 1)
                if t == 0:
                    pe.wait_ge(sem("w1_in0"), 16)
                    pe.wait_ge(sem("w2_in0"), 16)
                mm(bank[t % 2][:, :], w1[0][:, 128 * t:128 * t + 128], yt[:], start=True, stop=True)\
                    .then_inc(sem("sa_mm"), 1)
                mm(bank[2 + t % 2][:, :], w2[0][:, 128 * t:128 * t + 128], yt[:], start=True, stop=True)\
                    .then_inc(sem("sb_mm"), 1)

            def shared_down(t):
                m = 128 if t < HT - 1 else H_LAST
                if t == 0:
                    pe.wait_ge(sem("w3_in0"), 32)
                pe.wait_ge(sem("hs_ready"), t + 1)
                return mm(bank[7][:, :], w3[0][0:m, t, :], hs[0:m, t % 3, :], start=(t == 0), stop=False,
                          skip_group_check=True)

            def places():
                pe.wait_ge(sem("chosen_ready"), 1)
                flat = chosen_bf[:].rearrange("p t e -> p (t e)")
                mm(bank[6][:, 0:NT * E3], earlier_bf[:], flat, start=True, stop=False, skip_group_check=True)
                for t in range(NT - 1):
                    mm(bank[6][:, E3 * (t + 1):E3 * NT].rearrange("p (t e) -> p t e", e=E3), ones_bf[:],
                       chosen_bf[:, t, :].unsqueeze(1).broadcast_to([128, NT - 1 - t, E3]),
                       start=False, stop=False, skip_group_check=True)
                for t in range(NT):
                    last = mm(bank[6][:, E3 * NT:E3 * NT + E3], ones_bf[:], chosen_bf[:, t, :],
                              start=False, stop=(t == NT - 1), skip_group_check=True)
                last.then_inc(sem("places_mm"), 1)

            def gather(p, k, first=False):
                e = pe.value_load(plan_int[0:1, 0, bass.ds(k, 1)], min_val=0, max_val=E3 - 1)
                pe.wait_ge(sem("pick_ready"), k + 1)
                if not first:
                    pe.wait_ge(sem("xe_ready"), k)
                for t in range(NT):
                    for part in range(3):
                        mm(bank[4][:, 0:SLOTS], y_bf[:, t, part, :], pick_bf[:, p, t, :],
                           start=(t == 0 and part == 0), stop=(t == NT - 1 and part == 2))
                for t in range(NT):
                    last = mm(bank[4][:, SLOTS:SLOTS + 3], pick_bf[:, p, t, :],
                              weight_bf[:, t, bass.ds(e, 1), :].rearrange("p e w -> p (e w)"),
                              start=(t == 0), stop=(t == NT - 1))
                last.then_inc(sem("xe_mm"), 1)
                if not first:
                    pe.wait_ge(sem("spread_ready"), k + 1)
                for t in range(NT):
                    last = mm(bank[6][:, 128 * t:128 * t + 128], pick_bf[:, p, t, :], ident_bf[:], start=True, stop=True)
                last.then_inc(sem("spread_mm"), 1)

            def scatter(p):
                mm(bank[7][:, :], ye_hi[:, p, :], spread[:, p, :], start=False, stop=False, skip_group_check=True)
                return mm(bank[7][:, :], ye_lo[:, p, :], spread[:, p, :], start=False, stop=False, skip_group_check=True)

            for t in range(HT):
                shared_up(t)
                if t >= 1:
                    shared_down(t - 1).then_inc(sem("shared_down"), 1)
                if t == 2:
                    places()
            gather(1, 0, first=True)
            for t in range(NT):
                mm(bank[7][:, 128 * t:128 * t + 128], t5[:, t, :], ident[:], start=False, stop=False,
                   skip_group_check=True)
            shared_down(HT - 1).then_inc(sem("down_mm"), 1)

            def compute(p, k, uses):
                pe.wait_ge(sem(f"w1_in{p}"), 16 * uses)
                pe.wait_ge(sem(f"w2_in{p}"), 16 * uses)
                pe.wait_ge(sem("xe_ready"), k + 1)
                for g, (t0, t1) in enumerate(GROUPS):
                    slot = (3 * (1 - p) + g) % 2
                    pe.wait_ge(sem("he_ready"), 3 * k + g + 1)
                    for w, b, name in ((w1, slot, "a3_mm"), (w2, 2 + slot, "b3_mm")):
                        for t in range(t0, t1):
                            last = mm(bank[b][:, SLOTS * (t - t0):SLOTS * (t - t0 + 1)],
                                      w[p][:, 128 * t:128 * t + 128], xe[:, p, :], start=True, stop=True)
                        last.then_inc(sem(name), 1)
                    if g == 0:
                        pe.wait_ge(sem("ye_ready"), k + 1)
                        pe.wait_ge(sem("spread_ready"), k + 1)
                        scatter(1 - p).then_inc(sem("scatter_mm"), 1)
                gather(1 - p, k + 1)
                pe.wait_ge(sem(f"w3_in{p}"), 32 * uses)
                for t in range(HT):
                    for g, (t0, _) in enumerate(GROUPS):
                        if t == t0:
                            pe.wait_ge(sem("he_ready"), CREDIT + 3 * k + g + 1)
                    m = 128 if t < HT - 1 else H_LAST
                    last = mm(bank[5][:, 0:C], he[0:m, p, t, :], w3[p][0:m, t, :], start=(t == 0), stop=(t == HT - 1))
                last.then_inc(sem("down_mm"), 1)

            n_pairs = pe.value_load(pairs_int[0:1, 0:1], min_val=MIN_CHUNKS // 2, max_val=PAIRS)
            with pe.Fori(0, n_pairs) as i:
                compute(1, 2 * i, i + 1)
                compute(0, 2 * i + 1, i + 2)
            single = pe.value_load(pairs_int[0:1, 1:2], min_val=0, max_val=1)
            with pe.If(single > 0):
                compute(1, 2 * n_pairs, n_pairs + 1)
                pe.wait_ge(sem("ye_ready"), 2 * n_pairs + 2)
                scatter(1).then_inc(sem("out_mm"), 1)
            with pe.If(single < 1):
                pe.wait_ge(sem("ye_ready"), 2 * n_pairs + 1)
                scatter(0).then_inc(sem("out_mm"), 1)

        @block.scalar
        def _(act):
            act.sem_inc(sem("h2_ready"), 2 * CREDIT)
            act.sem_inc(sem("spread_ready"), 1)

            def copy(dst, src):
                return nc.scalar.activation(dst, src, ACT.Copy)

            act.wait_ge(sem("conv_in"), 16)
            act.wait_ge(sem("q0_mm"), 1)
            nc.scalar.activation(q0[:], bank[0][0:C8, :], ACT.Identity, bias=cc("bq")[0:C8, :]).then_inc(sem("q0_ready"), 1)
            act.wait_ge(sem("x0T_mm"), 1)
            copy(x0T[:].rearrange("p t c -> p (t c)"), bank[3][:, :]).then_inc(sem("x0T_ready"), 1)
            for b in range(B):
                act.wait_ge(sem("nmax0_ready"), b + 1)
                for t in range(2):
                    nc.scalar.activation(p0[:, b, t, :], bank[4 + b][:, PIX * t:PIX * t + PIX], ACT.Exp,
                                         bias=nmax0[:, b, t:t + 1], accum_out=sum0[:, b, t:t + 1])\
                        .then_inc(sem("exp0"), 1)
            act.wait_ge(sem("minc_ready"), 1)
            for b in range(B):
                nc.scalar.activation(pc[:, b, :], bank[6][:, C * b:C * b + C], ACT.Exp, bias=minc[:, b:b + 1], scale=-1.0,
                                     accum_out=sumc[:, b:b + 1]).then_inc(sem("expc"), 1)
            for b in range(B):
                act.wait_ge(sem("p0T_mm"), b + 1)
                copy(p0T[:, b, :, :].rearrange("p t n -> p (t n)"), bank[b][:, :]).then_inc(sem("p0T_ready"), 1)
            nc.scalar.activation(nothing[:], ones[0:1, 0:1], ACT.Sqrt).then_inc(sem("act_prepared0"), 1)
            act.wait_ge(sem("act_prepared0"), 1)
            act.wait_ge(sem("gvar_ready"), 1)
            nc.scalar.activation(gr[:, 0, :], gvar[:], ACT.Sqrt).then_inc(sem("gsd_ready"), 1)
            act.wait_ge(sem("t2_mm"), 1)
            copy(t2[:].rearrange("p t c -> p (t c)"), bank[3][:, :]).then_inc(sem("t2_ready"), 1)

            def prepare(func):
                nc.scalar.activation(nothing[:], ones[0:1, 0:1], func).then_inc(sem("act_prepared"), 1)
                prepared[0] += 1
                act.wait_ge(sem("act_prepared"), prepared[0])

            prepared = [0]

            def deviation(k):
                prepare(ACT.Sqrt)
                act.wait_ge(sem("lve_ready"), k + 1)
                nc.scalar.activation(lsd[:, k, :], lve[:, k, :], ACT.Sqrt).then_inc(sem("lsd_ready"), 1)

            def ln_copy(k, b):
                for half in range(2):
                    act.wait_ge(sem("yT_mm"), NT * turn_of(k) + 2 * half + 2)
                    copy(yT[k][:, PIX * half:PIX * half + PIX], bank[b + half][:, 0:PIX])\
                        .then_inc(sem("yT_ready"), 1)

            deviation(LN_ATT2)
            ln_copy(LN_ATT2, 4)
            for b in range(B):
                act.wait_ge(sem("knmax_ready"), 1)
                nc.scalar.activation(ek[:, b, :], bank[0][:, PIX * b:PIX * b + PIX], ACT.Exp, bias=knmax[:, b:b + 1],
                                     accum_out=sek[:, b:b + 1]).then_inc(sem("ek_ready"), 1)
            act.wait_ge(sem("ekT_mm"), 1)
            copy(ekT[:].rearrange("p t c -> p (t c)"), bank[3][:, :]).then_inc(sem("ekT_ready"), 1)
            act.wait_ge(sem("qs_ready"), 1)
            nc.scalar.activation(eq[:].rearrange("p t c -> p (t c)"), qs[:].rearrange("p g c -> p (g c)"), ACT.Exp)\
                .then_inc(sem("eq_ready"), 1)
            act.wait_ge(sem("eqT_mm"), 1)
            copy(eqT[:], bank[3][:, :]).then_inc(sem("eqT_ready"), 1)
            act.wait_ge(sem("num2_mm"), 1)
            copy(num2[:], bank[6][:, :]).then_inc(sem("num2_ready"), 1)

            deviation(LN_FFN2)
            ln_copy(LN_FFN2, 4)
            act.wait_ge(sem("lg2_ready"), 1)
            nc.scalar.activation(e2[:], lg2[:], ACT.Exp).then_inc(sem("e2_ready"), 1)
            prepare(ACT.Gelu)
            with act.Fori(0, E2 // 2) as i:
                for p in range(2):
                    act.wait_ge(sem(f"ew2_in{p}"), 16 * i + 16)
                    act.wait_ge(sem("expert2_mm"), 2 * i + p + 1)
                    for half in range(2):
                        act.wait_ge(sem("hidden2_mm"), 4 * i + 2 * p + half + 1)
                        nc.scalar.activation(h2[:, 2 * p + half, :], bank[4 + 2 * p + half][:, :], ACT.Gelu,
                                             bias=ew2[p][:, 4 * C + half:4 * C + half + 1]).then_inc(sem("h2_ready"), 1)
            act.wait_ge(sem("comb2T_mm"), 1)
            copy(comb2T[:], bank[0][0:E2, :]).then_inc(sem("comb2T_ready"), 1)

            deviation(LN_ATT3)
            ln_copy(LN_ATT3, 2)
            for s, side in enumerate("gl"):
                act.wait_ge(sem("q3_mm"), s + 1)
                nc.scalar.activation(q3[s][:], bank[4 + 2 * s][:, :], ACT.Identity, bias=c3(side + "_bq"))\
                    .then_inc(sem("q3_ready"), 1)
            act.wait_ge(sem("masks_made"), 1)
            act.wait_ge(sem("k3_ready"), 2)
            for h in range(HEADS):
                last = nc.scalar.activation(km3[1][0][:, h, :], k3[1][:, 0:PIX], ACT.Copy, scale=head_mask[:, h:h + 1])
            last.then_inc(sem("km3_local0"), 1)

            def exps(u):
                kind = UNITS[u][0]
                n = GLOBAL_HEADS if kind == "g" else LOCAL_HEADS
                m = 512 // n
                act.wait_ge(sem("nmax3_ready"), u + 1)
                if u >= 2:
                    act.wait_ge(sem("p3T_mm"), u - 1)
                for h in range(n):
                    last = nc.scalar.activation(p3[:, u % 2, m * h:m * h + m], bank[u % 2][:, m * h:m * h + m], ACT.Exp,
                                                bias=nmax3[:, u, h:h + 1], scale=HD ** -0.5)
                last.then_inc(sem("exp3"), 1)

            def copy_out(n):
                act.wait_ge(sem("attend3"), (n // 2) * UNITS_B + (UNITS_B if n % 2 else UNITS_G))
                if n >= 2:
                    act.wait_ge(sem("ob3_ready"), n - 1)
                copy(o3[:, n % 2, :], bank[4 + n % 2][:, :]).then_inc(sem("o3_copied"), 1)

            for u in range(len(UNITS)):
                exps(u)
                for n, end in enumerate((UNITS_G, UNITS_B, UNITS_B + UNITS_G)):
                    if u == end + 2:
                        copy_out(n)
            copy_out(3)

            deviation(LN_MID3)
            ln_copy(LN_MID3, 0)
            for f in range(FT):
                act.wait_ge(sem("ff3_mm"), f + 1)
                nc.scalar.activation(hf3[:, f, :], bank[1 + f][:, :], ACT.Relu, bias=c3("ffn_b1")[:, f:f + 1])\
                    .then_inc(sem("hf3_ready"), 1)
            deviation(LN_END3)

            deviation(LN_FFN3)
            ln_copy(LN_FFN3, 5)
            act.wait_ge(sem("lg3_ready"), 1)
            nc.scalar.activation(e3[:], lg3[:], ACT.Exp).then_inc(sem("e3_ready"), 1)
            for t in range(HT):
                act.wait_ge(sem("sa_mm"), t + 1)
                if t >= 2:
                    act.wait_ge(sem("hs_ready"), t - 1)
                nc.scalar.activation(silu[:, t % 2, :], bank[t % 2][:, :], ACT.Silu).then_inc(sem("s_silu"), 1)

            def copy_turned_choice(p, k):
                act.wait_ge(sem("scatter_mm"), k + 1)
                act.wait_ge(sem("spread_mm"), k + 2)
                copy(spread[:, p, :], bank[6][:, :]).then_inc(sem("spread_ready"), 1)

            def activate(p, k):
                for g, (t0, t1) in enumerate(GROUPS):
                    slot = (3 * (1 - p) + g) % 2
                    n = SLOTS * (t1 - t0)
                    act.wait_ge(sem("a3_mm"), 3 * k + g + 1)
                    act.wait_ge(sem("he_ready"), 3 * k + g + 1)
                    nc.scalar.activation(silu[:, slot, 0:n], bank[slot][:, 0:n], ACT.Silu)\
                        .then_inc(sem("silu_ready"), 1)
                copy_turned_choice(1 - p, k + 1)
                act.wait_ge(sem("xe_ready"), k + 1)
                act.wait_ge(sem("down_mm"), k + 3)
                nc.scalar.activation(ye_hi[:, p, :], bank[5][:, 0:C], ACT.Copy, scale=slot_weight[:, p:p + 1])\
                    .then_inc(sem("ye_hi_ready"), 1)

            act.wait_ge(sem("plan_ready"), 1)
            copy_turned_choice(1, 0)
            n_pairs = act.value_load(pairs_int[0:1, 0:1], min_val=MIN_CHUNKS // 2, max_val=PAIRS)
            with act.Fori(0, n_pairs) as i:
                activate(1, 2 * i)
                activate(0, 2 * i + 1)
            single = act.value_load(pairs_int[0:1, 1:2], min_val=0, max_val=1)
            with act.If(single > 0):
                activate(1, 2 * n_pairs)

        @block.vector
        def _(dve):
            tt = nc.vector.tensor_tensor
            ts = nc.vector.tensor_scalar
            stt = nc.vector.scalar_tensor_tensor
            done = [0]

            def note(ins):
                done[0] += 1
                ins.then_inc(sem("dve_step"), 1)

            def settle(ins=None):
                if ins is not None:
                    note(ins)
                dve.wait_ge(sem("dve_step"), done[0])

            def flat(x):
                return x.rearrange("p a b -> p (a b)")

            dve.sem_inc(sem("y2_added"), CREDIT)
            dve.sem_inc(sem("he_ready"), CREDIT)
            dve.sem_inc(sem("ye_ready"), 1)
            dve.wait_ge(sem("conv_in"), 16)
            dve.wait_ge(sem("rows_in"), 16)
            note(tt(mix[:, 0:1], cc("alpha"), cc("gamma_pos"), ALU.mult))
            note(tt(mix[:, 1:2], cc("beta"), cc("gamma_chan"), ALU.mult))
            note(stt(mix[:, 2:3], cc("alpha"), 1.0, cc("beta"), ALU.add, ALU.add))
            note(stt(mask_w[:], cc("filter"), 1.0, cc("mask_weight"), ALU.is_equal, ALU.mult))
            dve.wait_ge(sem("k0_mm"), 1)
            ts(k0[:], bank[1][0:C8, :], cc("bk")[0:C8, :], None, ALU.add).then_inc(sem("k0_ready"), 1)
            dve.wait_ge(sem("v0_mm"), 1)
            tt(v0T[:], bank[2][:, :].rearrange("p (t c) -> p t c", t=NT), row("bv", NT), ALU.add)\
                .then_inc(sem("v0_ready"), 1)
            for b in range(B):
                dve.wait_ge(sem("energy_mm"), b + 1)
                nc.vector.tensor_reduce(nmax0[:, b, :], bank[4 + b][:, :].rearrange("p (t n) -> p t n", t=2), AX.X,
                                        ALU.max, negate=True).then_inc(sem("nmax0_ready"), 1)
            dve.wait_ge(sem("energyc_mm"), 1)
            nc.vector.tensor_reduce(minc[:], bank[6][:, 0:B * C].rearrange("p (b n) -> p b n", b=B), AX.X, ALU.min)\
                .then_inc(sem("minc_ready"), 1)
            for b in range(B):
                dve.wait_ge(sem("exp0"), 2 * b + 2)
                settle(nc.vector.reciprocal(sum0[:, b, :], sum0[:, b, :]))
                settle(ts(sum0[:, b, :], sum0[:, b, :], mix[:, 0:1], None, ALU.mult))
                for t in range(2):
                    ts(p0[:, b, t, :], p0[:, b, t, :], sum0[:, b, t:t + 1], None, ALU.mult).then_inc(sem("p0_ready"), 2)
            dve.wait_ge(sem("expc"), B)
            settle(nc.vector.reciprocal(sumc[:], sumc[:]))
            settle(ts(sumc[:], sumc[:], mix[:, 1:2], None, ALU.mult))
            for b in range(B):
                ts(pc[:, b, :], pc[:, b, :], sumc[:, b:b + 1], None, ALU.mult).then_inc(sem("pc_ready"), 1)
            dve.wait_ge(sem("pcT_mm"), 1)
            nc.vector.tensor_copy(flat(pcT[:]), bank[2][:, 0:B * C]).then_inc(sem("pcT_ready"), 1)
            for b in range(B):
                dve.wait_ge(sem("layer0_mm"), b + 1)
                settle(stt(x1[:, b, :], x0[:, b, :], mix[:, 2:3], bank[7 - 4 * b][:, 0:PIX], ALU.mult, ALU.add))
                settle(nc.vector.bn_stats(gst[:, b, :], x1[:, b, :]))
                note(nc.vector.bn_aggr(gmv[:, b, :], gst[:, b, :]))
            settle()
            dve.sem_inc(sem("gmv_ready"), 1)
            dve.wait_ge(sem("gmean_mm"), 1)
            settle(nc.vector.tensor_copy(gm[:], bank[0][:, 0:B]))
            settle(tt(gdev[:], gmv[:, :, 0], gm[:], ALU.subtract))
            settle(tt(gdev[:], gdev[:], gdev[:], ALU.mult))
            tt(gdev[:], gdev[:], gmv[:, :, 1], ALU.add).then_inc(sem("gdev_ready"), 1)
            dve.wait_ge(sem("gvar_mm"), 1)
            ts(gvar[:], bank[1][:, 0:B], EPS, None, ALU.add).then_inc(sem("gvar_ready"), 1)
            dve.wait_ge(sem("gsd_ready"), 1)

            def newton(r, r0, sd, v, tmp):
                settle(nc.vector.reciprocal(r0, sd))
                settle(tt(tmp, r0, r0, ALU.mult))
                settle(stt(tmp, tmp, -0.5, v, ALU.mult, ALU.mult))
                settle(stt(r, tmp, 1.5, r0, ALU.add, ALU.mult))

            dve.wait_ge(sem("gvar_ready"), 1)
            newton(gr[:, 2, :], gr[:, 1, :], gr[:, 0, :], gvar[:], gr[:, 3, :])
            for b in range(B):
                note(ts(gn[:, b, :, :].rearrange("p h w -> p (h w)"), x1[:, b, :], gm[:, b:b + 1], gr[:, 2, b:b + 1],
                        ALU.subtract, ALU.mult))
            settle()
            note(nc.vector.tensor_reduce(sums[:, 0, :, :], gn[:], AX.X, ALU.add))
            note(nc.vector.tensor_reduce(sums[:, 1, :, :], gn[:].rearrange("p b h w -> p b w h"), AX.X, ALU.add))
            settle()
            dve.wait_ge(sem("group_made"), 1)
            note(nc.vector.tensor_reduce(total[:], sums[:, 0, :, :], AX.X, ALU.add))
            note(tt(weighted[:].rearrange("p k b h -> p (k b) h"), sums[:].rearrange("p k b h -> p (k b) h"),
                    ramp[:].unsqueeze(1).broadcast_to([128, 2 * B, SIDE]), ALU.mult))
            settle(ts(pos[:], ramp[:], -1.0, 2.0 / (SIDE - 1), ALU.add, ALU.mult))
            note(ts(pos[:], pos[:], -1.0, None, ALU.add))
            note(nc.vector.tensor_reduce(moment[:], weighted[:], AX.X, ALU.add))
            settle(ts(total[:], total[:], 1e-9, None, ALU.max))
            settle(nc.vector.reciprocal(total[:], total[:]))
            settle(tt(mu[:], moment[:], total[:].unsqueeze(1).broadcast_to([128, 2, B]), ALU.mult))
            settle(ts(mu[:], mu[:], 1.0, float(SIDE), ALU.max, ALU.min))
            settle(ts(mu[:], mu[:], ROUND, ROUND, ALU.add, ALU.subtract))
            settle(ts(mu[:], mu[:], -1.0, 2.0 / (SIDE - 1), ALU.add, ALU.mult))
            settle(ts(mu[:], mu[:], -1.0, None, ALU.add))
            d = dist[:].rearrange("p k b h -> p (k b) h")
            settle(tt(d, pos[:].unsqueeze(1).broadcast_to([128, 2 * B, SIDE]),
                      mu[:].rearrange("p k b -> p (k b)").unsqueeze(2).broadcast_to([128, 2 * B, SIDE]), ALU.subtract))
            settle(stt(d, d, -1.0, d, ALU.mult, ALU.max))
            m = mask[:].rearrange("p b h w -> p (b h w)")
            for b in range(B):
                note(tt(mask[:, b, :, :], dist[:, 0, b, :].unsqueeze(2).broadcast_to([128, SIDE, SIDE]),
                        dist[:, 1, b, :].unsqueeze(1).broadcast_to([128, SIDE, SIDE]), ALU.add))
            settle()
            settle(ts(mask_w[:], mask_w[:], -1.0, None, ALU.mult))
            settle(ts(m, m, mask_w[:], 1.0, ALU.mult, ALU.add))
            settle(stt(m, m, -1.0, gn[:].rearrange("p b h w -> p (b h w)"), ALU.max, ALU.mult))
            dve.wait_ge(sem("pad_made"), 1)
            ts(pad[:, :, 1:1 + SIDE, 1:1 + SIDE], mask[:], 0.0, None, ALU.max).then_inc(sem("pad_ready"), 1)
            dve.wait_ge(sem("conv_mm"), 1)
            stt(flat(x2[:]), bank[2][:, :], cc("conv_bias"), flat(x1[:]), ALU.add, ALU.add).then_inc(sem("x2_ready"), 1)

            def normalise(k, src, gain=None, shift=None, out=None):
                for t in range(NT):
                    note(nc.vector.bn_stats(lst[:, t, :], src[:, t, :]))
                settle()
                for t in range(NT):
                    note(nc.vector.bn_aggr(lmv[:, k, t, :], lst[:, t, :]))
                settle()
                ts(lve[:, k, :], lmv[:, k, :, 1], EPS, None, ALU.add).then_inc(sem("lve_ready"), 1)
                if gain is not None:
                    for t in range(NT):
                        note(stt(z3[:, t, :], src[:, t, :], lmv[:, k, t, 0:1], gain, ALU.subtract, ALU.mult))
                dve.wait_ge(sem("lve_ready"), k + 1)
                dve.wait_ge(sem("lsd_ready"), k + 1)
                newton(lr[:, k, :], lr0[:, k, :], lsd[:, k, :], lve[:, k, :], lra[:, k % 2, :])
                for t in range(NT):
                    if gain is None:
                        ins = ts(y[k][:, t, :], src[:, t, :], lmv[:, k, t, 0:1], lr[:, k, t:t + 1], ALU.subtract, ALU.mult)
                    else:
                        ins = stt((y[k] if out is None else out)[:, t, :], z3[:, t, :], lr[:, k, t:t + 1], shift(t),
                                  ALU.mult, ALU.add)
                    if out is None:
                        ins.then_inc(sem("y_ready"), 1)
                    else:
                        note(ins)
                if out is not None:
                    settle()

            dve.wait_ge(sem("t2_ready"), 1)
            normalise(LN_ATT2, t2)
            dve.wait_ge(sem("att_in"), 16)
            dve.wait_ge(sem("y_ready"), NT * turn_of(LN_ATT2) + NT)
            note(tt(t2[:], t2[:], row("bO", NT), ALU.add))
            dve.wait_ge(sem("k2_mm"), 1)
            settle(nc.vector.tensor_reduce(kmax[:], bank[0][:, :].rearrange("p (b n) -> p b n", b=B), AX.X, ALU.max))
            ts(knmax[:], kmax[:], -1.0, None, ALU.mult).then_inc(sem("knmax_ready"), 1)
            settle(ts(kq[:], kmax[:], ca("bK"), ca("bQ"), ALU.add, ALU.add))
            dve.wait_ge(sem("ident_made"), 1)
            for b in range(B):
                ts(kqb[:, b, :], ones[:], kq[:, b:b + 1], None, ALU.mult).then_inc(sem("kqb_ready"), 1)
            dve.wait_ge(sem("v2_mm"), 1)
            tt(v2[:], bank[2][:, :].rearrange("p (t c) -> p t c", t=NT), row("bV", NT), ALU.add).then_inc(sem("v2_ready"), 1)
            dve.wait_ge(sem("q2_mm"), 1)
            settle(nc.vector.tensor_reduce(qmax[:], bank[1][:, :].rearrange("p (g c) -> p g c", c=HD), AX.X, ALU.max))
            tt(qs[:], bank[1][:, :].rearrange("p (g c) -> p g c", c=HD),
               qmax[:].unsqueeze(2).broadcast_to([128, NT * HEADS, HD]), ALU.subtract).then_inc(sem("qs_ready"), 1)
            dve.wait_ge(sem("masks_made"), 1)
            dve.wait_ge(sem("ek_ready"), B)
            for b in range(B):
                last = ts(ksum[:, b, :], head_mask[:], sek[:, b:b + 1], None, ALU.mult)
            last.then_inc(sem("kv_ready"), 1)
            dve.wait_ge(sem("kv_mm"), 1)
            tt(kv[:], bank[5][:, 0:B * C].rearrange("p (b c) -> p b c", b=B),
               head_block[:].unsqueeze(1).broadcast_to([128, B, C]), ALU.mult).then_inc(sem("kv_ready"), 1)
            dve.wait_ge(sem("den2_mm"), 1)
            settle(nc.vector.reciprocal(rd2[:], bank[4][:, 0:NT * HEADS]))
            nc.vector.tensor_copy(rden2[:].rearrange("p t h c -> p (t h) c"),
                                  rd2[:].unsqueeze(2).broadcast_to([128, NT * HEADS, HD])).then_inc(sem("rden2_ready"), 1)
            dve.wait_ge(sem("spread2_mm"), 1)
            dve.wait_ge(sem("num2_ready"), 1)
            tt(heads2[:], bank[7][:, :], num2[:], ALU.mult).then_inc(sem("heads2_ready"), 1)
            dve.wait_ge(sem("att2_mm"), 1)
            settle(tt(flat(t3[:]), bank[0][:, :], flat(t2[:]), ALU.add))

            normalise(LN_FFN2, t3)

            def logits(lg, b, n, bias, m):
                settle(tt(lg[:], bank[b][:, 0:NT * n].rearrange("p (t e) -> p t e", e=n), row(bias, NT), ALU.add))
                settle(nc.vector.tensor_reduce(m[:], lg[:], AX.X, ALU.max))
                return tt(lg[:], lg[:], m[:].unsqueeze(2).broadcast_to([128, NT, n]), ALU.subtract)

            def tiles(x, n):
                return x.rearrange("p (t e) f -> p t e f", t=NT)

            def compare(x, cmp, n):
                other = x[:].unsqueeze(2).broadcast_to([128, NT, n, n])
                own = x[:].unsqueeze(3).broadcast_to([128, NT, n, n])
                note(tt(tiles(cmp[:, 0, :, :], n), other, own, ALU.is_gt))
                settle(tt(tiles(cmp[:, 1, :, :], n), other, own, ALU.is_equal))

            def rank(out, cmp, earlier, n):
                settle(tt(tiles(cmp[:, 1, :, :], n), tiles(cmp[:, 1, :, :], n),
                          earlier[:].unsqueeze(1).broadcast_to([128, NT, n, n]), ALU.mult))
                settle(tt(cmp[:, 0, :, :], cmp[:, 0, :, :], cmp[:, 1, :, :], ALU.add))
                settle(nc.vector.tensor_reduce(out[:].rearrange("p t e -> p (t e)"), cmp[:, 0, :, :], AX.X, ALU.add))

            dve.wait_ge(sem("route2_mm"), 1)
            logits(lg2, 1, E2, "br", m2).then_inc(sem("lg2_ready"), 1)
            dve.wait_ge(sem("e2_ready"), 1)
            settle(nc.vector.tensor_reduce(s2[:], e2[:], AX.X, ALU.add))
            settle(nc.vector.reciprocal(s2[:], s2[:]))
            settle(tt(pr2[:], e2[:], s2[:].unsqueeze(2).broadcast_to([128, NT, E2]), ALU.mult))
            compare(pr2, cmp2, E2)
            rank(rank2, cmp2, before2, E2)
            stt(comb2[:], rank2[:], 2.0, pr2[:], ALU.is_lt, ALU.mult).then_inc(sem("comb2_ready"), 1)
            dve.wait_ge(sem("comb2_ready"), 1)
            nc.vector.tensor_copy(t4[:], t3[:]).then_inc(sem("t4_added"), 1)
            with dve.Fori(0, E2 // 2) as i:
                for p in range(2):
                    dve.wait_ge(sem("expert2_mm"), CREDIT + 2 * i + p + 1)
                    dve.wait_ge(sem("t4_added"), 2 * i + p + 1)
                    for t in range(NT):
                        last = stt(t4[:, t, :], bank[2 + p][:, 128 * t:128 * t + 128],
                                   comb2[:, t, bass.ds(2 * i + p, 1)], t4[:, t, :], ALU.mult, ALU.add)
                    last.then_inc(sem("t4_added"), 1)
                    dve.wait_ge(sem("t4_added"), 2 * i + p + 2)
                    dve.sem_inc(sem("y2_added"), 1)
            dve.wait_ge(sem("bias2_mm"), 1)
            settle(tt(flat(t4[:]), bank[1][:, :], flat(t4[:]), ALU.add))

            normalise(LN_ATT3, t4)
            dve.wait_ge(sem("y_ready"), NT * turn_of(LN_ATT3) + NT)
            settle(tt(u3[:], y[LN_ATT3][:], row("g_out_b", NT), ALU.add))
            note(tt(u3[:], u3[:], row("l_out_b", NT), ALU.add))
            dve.wait_ge(sem("l3_in"), 16)
            for s, side in enumerate("gl"):
                dve.wait_ge(sem("k3_mm"), s + 1)
                ts(k3[s][:], bank[5 + 2 * s][:, :], c3(side + "_bk"), None, ALU.add).then_inc(sem("k3_ready"), 1)
                if s == 0:
                    dve.wait_ge(sem("k3_ready"), 1)
                    for h in range(HEADS):
                        last = ts(km3[0][0][:, h, :], k3[0][:, 0:PIX], head_mask[:, h:h + 1], None, ALU.mult)
                    last.then_inc(sem("km3_global0"), 1)

            def values(dst, src, side, n):
                bias = row(side + "_bv").rearrange("p (h c) -> p h c", h=HEADS)
                return tt(dst, src.rearrange("p (t h c) -> p t h c", t=n, h=HEADS),
                          bias.unsqueeze(1).broadcast_to([128, n, HEADS, HD]), ALU.add)

            dve.wait_ge(sem("vg_mm"), 1)
            values(vg[:, :, :, 0:HD], bank[2][:, :], "g", NT).then_inc(sem("v3_ready"), 1)
            dve.wait_ge(sem("vl_mm"), 1)
            nw = len(WINDOWS)
            for b in range(B):
                last = values(vl[:, nw * b:nw * b + nw, :, 0:HD], bank[b][:, 0:nw * C], "l", nw)
            last.then_inc(sem("v3_ready"), 1)

            def largest(u):
                kind = UNITS[u][0]
                n = GLOBAL_HEADS if kind == "g" else LOCAL_HEADS
                dve.wait_ge(sem("score3_mm"), u + 1)
                settle(nc.vector.tensor_reduce(nmax3[:, u, 0:n], bank[u % 2][:, :].rearrange("p (h n) -> p h n", h=n),
                                               AX.X, ALU.max))
                ts(nmax3[:, u, 0:n], nmax3[:, u, 0:n], -HD ** -0.5, None, ALU.mult).then_inc(sem("nmax3_ready"), 1)

            def copy_turned(u):
                dve.wait_ge(sem("p3T_mm"), u + 1)
                if u >= 2:
                    dve.wait_ge(sem("attend3"), u - 1)
                nc.vector.tensor_copy(p3T[:, u % 2, :], bank[2 + u % 2][:, :]).then_inc(sem("p3T_ready"), 1)

            def invert(n):
                dve.wait_ge(sem("den3_mm"), n + 1)
                if n:
                    dve.wait_ge(sem("spread3_mm"), n)
                settle(nc.vector.reciprocal(rd3[:], bank[6][:, 0:16]))
                nc.vector.tensor_copy(rd3_wide[:].rearrange("p q j c -> p (q j) c"),
                                      rd3[:].unsqueeze(2).broadcast_to([128, 16, 32])).then_inc(sem("rd3_ready"), 1)

            def divide(n):
                dve.wait_ge(sem("spread3_mm"), n + 1)
                tt(ob3[:, n // 2, n % 2, :, :].rearrange("p h q -> p (h q)"), bank[6][:, :], o3[:, n % 2, :], ALU.mult)\
                    .then_inc(sem("ob3_ready"), 1)

            for u in range(len(UNITS) + 1):
                if u < len(UNITS):
                    largest(u)
                if u >= 1:
                    copy_turned(u - 1)
                for n, end in enumerate((UNITS_G, UNITS_B, UNITS_B + UNITS_G)):
                    if u == end + 3:
                        invert(n)
                    if u == end + 4:
                        divide(n)
            invert(3)
            divide(3)
            dve.wait_ge(sem("att3_mm"), B)
            settle(tt(flat(u3[:]), bank[7][:, :], flat(u3[:]), ALU.add))

            normalise(LN_MID3, u3, gain=row("ln1_g"), shift=lambda t: row("ln1_b"))
            dve.wait_ge(sem("y_ready"), NT * turn_of(LN_MID3) + NT)
            settle(tt(u3[:], y[LN_MID3][:], row("ffn_b2", NT), ALU.add))
            note(tt(t4[:], t4[:], row("ln2_b", NT), ALU.add))
            dve.wait_ge(sem("ffn3_mm"), 1)
            settle(tt(flat(u3[:]), bank[6][:, :], flat(u3[:]), ALU.add))
            normalise(LN_END3, u3, gain=row("ln2_g"), shift=lambda t: t4[:, t, :], out=t5)

            normalise(LN_FFN3, t5)
            dve.wait_ge(sem("route3_mm"), 1)
            logits(lg3, 4, E3, "routing_bias", m3).then_inc(sem("lg3_ready"), 1)
            dve.wait_ge(sem("lg3_ready"), 1)
            def shared(t):
                dve.wait_ge(sem("sb_mm"), t + 1)
                dve.wait_ge(sem("s_silu"), t + 1)
                if t >= 3:
                    dve.wait_ge(sem("shared_down"), t - 2)
                tt(hs[:, t % 3, :], bank[2 + t % 2][:, :], silu[:, t % 2, :], ALU.mult).then_inc(sem("hs_ready"), 1)

            def weigh():
                dve.wait_ge(sem("e3_ready"), 1)
                settle(tt(weight[:], e3[:], chosen[:], ALU.mult))
                settle(nc.vector.tensor_reduce(s3[:], weight[:], AX.X, ALU.add))
                settle(nc.vector.reciprocal(s3[:], s3[:]))
                settle(tt(weight[:], weight[:], s3[:].unsqueeze(2).broadcast_to([128, NT, E3]), ALU.mult))
                settle(nc.vector.tensor_copy(weight_bf[:, :, :, 0], weight[:]))
                settle(tt(left[:], weight[:], weight_bf[:, :, :, 0], ALU.subtract))
                settle(nc.vector.tensor_copy(weight_bf[:, :, :, 1], left[:]))
                note(tt(weight_bf[:, :, :, 2], left[:], weight_bf[:, :, :, 1], ALU.subtract))

            def split_tokens():
                tokens = y[LN_FFN3]
                dve.wait_ge(sem("y_ready"), NT * turn_of(LN_FFN3) + NT)
                settle(nc.vector.tensor_copy(y_bf[:, :, 0, :], tokens[:]))
                settle(tt(tokens_left[:], tokens[:], y_bf[:, :, 0, :], ALU.subtract))
                settle(nc.vector.tensor_copy(y_bf[:, :, 1, :], tokens_left[:]))
                note(tt(y_bf[:, :, 2, :], tokens_left[:], y_bf[:, :, 1, :], ALU.subtract))

            def find_places():
                dve.wait_ge(sem("places_mm"), 1)
                settle(stt(place[:], bank[6][:, 0:NT * E3].rearrange("p (t e) -> p t e", e=E3), 1.0, chosen[:],
                           ALU.add, ALU.mult))
                note(ts(place[:], place[:], -1.0, None, ALU.add))
                settle(nc.vector.tensor_copy(count[:], bank[6][:, E3 * NT:E3 * NT + E3]))
                settle(ts(chunks[:], count[:], 0.0, None, ALU.is_gt))
                for n in range(1, BLOCKS):
                    settle(stt(chunks[:], count[:], float(n * SLOTS), chunks[:], ALU.is_gt, ALU.add))
                settle(tt(cmp3[:, 0, 0:E3, :], before[:], chunks[:].unsqueeze(1).broadcast_to([128, E3, E3]), ALU.mult))
                settle(nc.vector.tensor_reduce(first[:], cmp3[:, 0, 0:E3, :], AX.X, ALU.add))

            def order_chunks():
                settle(tt(pairs[:, 0:1], first[:, E3 - 1:E3], chunks[:, E3 - 1:E3], ALU.add))
                settle(ts(pairs[:, 1:2], pairs[:, 0:1], 0.5, -0.25, ALU.mult, ALU.add))
                settle(ts(pairs[:, 2:3], pairs[:, 1:2], ROUND, ROUND, ALU.add, ALU.subtract))
                settle(stt(pairs[:, 3:4], pairs[:, 2:3], -2.0, pairs[:, 0:1], ALU.mult, ALU.add))
                note(nc.vector.tensor_copy(pairs_int[:], pairs[0:1, 2:4]))
                by_pair = plan[:, 4, :].rearrange("p (i l) -> p i l", l=2)
                settle(stt(by_pair, chunk_odd[:], pairs[:, 2:3], chunk_half[:], ALU.mult, ALU.add))
                settle(ts(pairs[:, 4:5], pairs[:, 2:3], 2.0, None, ALU.mult))
                settle(ts(plan[:, 0, :], chunk_no[:], pairs[:, 4:5], None, ALU.is_ge))
                settle(tt(plan[:, 1, :], chunk_no[:], plan[:, 4, :], ALU.subtract))
                settle(tt(plan[:, 1, :], plan[:, 1, :], plan[:, 0, :], ALU.mult))
                settle(tt(plan[:, 4, :], plan[:, 4, :], plan[:, 1, :], ALU.add))

            def make_plan():
                settle(tt(reach[:], plan[:, 4, :].unsqueeze(2).broadcast_to([128, NK, E3]),
                          first[:].unsqueeze(1).broadcast_to([128, NK, E3]), ALU.is_ge))
                settle(nc.vector.tensor_reduce(plan[:, 0, :], reach[:], AX.X, ALU.add))
                note(ts(plan[:, 0, :], plan[:, 0, :], -1.0, None, ALU.add))
                settle(tt(reach[:], reach[:], first[:].unsqueeze(1).broadcast_to([128, NK, E3]), ALU.mult))
                settle(nc.vector.tensor_reduce(plan[:, 3, :], reach[:], AX.X, ALU.max))
                note(tt(plan[:, 2, 2:NK], plan[:, 0, 2:NK], plan[:, 0, 0:NK - 2], ALU.not_equal))
                settle(tt(plan[:, 1, :], plan[:, 4, :], plan[:, 3, :], ALU.subtract))
                settle(ts(plan[:, 1, :], plan[:, 1, :], float(BLOCKS), float(SLOTS), ALU.min, ALU.mult))
                settle(nc.vector.tensor_copy(plan_int[:], plan[0:1, 0:3, :]))
                dve.sem_inc(sem("plan_ready"), 1)

            def choose(p, k):
                e = dve.value_load(plan_int[0:1, 0, bass.ds(k, 1)], min_val=0, max_val=E3 - 1)
                at = dve.value_load(plan_int[0:1, 1, bass.ds(k, 1)], min_val=0, max_val=BLOCKS * SLOTS)
                for t in range(NT):
                    last = ts(pick_bf[:, p, t, :], slot_no[:, bass.ds(at, SLOTS)], place[:, t, bass.ds(e, 1)], None,
                              ALU.is_equal)
                last.then_inc(sem("pick_ready"), 1)

            def copy_tokens(p, k, first=False):
                dve.wait_ge(sem("xe_mm"), k + 1)
                if not first:
                    dve.wait_ge(sem("ye_ready"), k)
                nc.vector.tensor_reduce(slot_weight[:, p:p + 1], bank[4][:, SLOTS:SLOTS + 3], AX.X, ALU.add)
                nc.vector.tensor_copy(xe[:, p, :], bank[4][:, 0:SLOTS]).then_inc(sem("xe_ready"), 1)

            def multiply(p, k):
                dve.wait_ge(sem("down_mm"), k + 1)
                for g, (t0, t1) in enumerate(GROUPS):
                    slot = (3 * (1 - p) + g) % 2
                    n = SLOTS * (t1 - t0)
                    dve.wait_ge(sem("b3_mm"), 3 * k + g + 1)
                    dve.wait_ge(sem("silu_ready"), 3 * k + g + 1)
                    tt(he[:, p, t0:t1, :].rearrange("p t s -> p (t s)"), bank[2 + slot][:, 0:n], silu[:, slot, 0:n],
                       ALU.mult).then_inc(sem("he_ready"), 1)
                    if g == 0:
                        dve.wait_ge(sem("spread_mm"), k + 1)
                        choose(1 - p, k + 1)
                copy_tokens(1 - p, k + 1)
                dve.wait_ge(sem("ye_hi_ready"), k + 1)
                stt(ye_lo[:, p, :], bank[5][:, 0:C], slot_weight[:, p:p + 1], ye_hi[:, p, :], ALU.mult, ALU.subtract)\
                    .then_inc(sem("ye_ready"), 1)

            for part in (spread, ye_hi, ye_lo):
                note(ts(part[:, 0, :], slot_no[:, 0:part.shape[2]], 0.0, None, ALU.mult))
            note(nc.vector.memset(plan[:, 2, 0:2], 0.0))
            compare(lg3, cmp3, E3)
            shared(0)
            rank(rank3, cmp3, before, E3)
            settle(ts(chosen[:], rank3[:], float(K3), None, ALU.is_lt))
            nc.vector.tensor_copy(chosen_bf[:], chosen[:]).then_inc(sem("chosen_ready"), 1)
            shared(1)
            weigh()
            shared(2)
            split_tokens()
            shared(3)
            find_places()
            shared(4)
            order_chunks()
            shared(5)
            make_plan()
            shared(6)
            choose(1, 0)
            for t in range(7, HT):
                shared(t)
            copy_tokens(1, 0, first=True)
            n_pairs = dve.value_load(pairs_int[0:1, 0:1], min_val=MIN_CHUNKS // 2, max_val=PAIRS)
            with dve.Fori(0, n_pairs) as i:
                multiply(1, 2 * i)
                multiply(0, 2 * i + 1)
            single = dve.value_load(pairs_int[0:1, 1:2], min_val=0, max_val=1)
            with dve.If(single > 0):
                multiply(1, 2 * n_pairs)
            dve.wait_ge(sem("out_mm"), 1)
            nc.vector.tensor_copy(flat(outT[:]), bank[7][:, :]).then_inc(sem("out_ready"), 1)


def launch_arrays(inputs):
    import numpy as np

    a = {k: np.asarray(v) for k, v in inputs.items()}

    def pack(at, n, parts):
        out = np.zeros((128, n), np.float32)
        for name, (first, count) in at.items():
            v = parts[name]
            out[0:v.shape[0], first:first + count] = v
        return out

    def col(v, n=1):
        return v.reshape(n, -1).T

    def scalar(v):
        return np.broadcast_to(v.reshape(1, 1), (128, 1))

    conv = pack(CONV_AT, CONV_N, {
        "wq": a["L0_conv_wq"].T, "wk": a["L0_conv_wk"].T, "wv": a["L0_conv_wv"].T,
        "bq": col(a["L0_conv_bq"]), "bk": col(a["L0_conv_bk"]),
        "gamma_pos": scalar(a["L0_conv_gamma_pos"]), "gamma_chan": scalar(a["L0_conv_gamma_chan"]),
        "alpha": scalar(a["L0_conv_alpha"]), "beta": scalar(a["L0_conv_beta"]),
        "conv_bias": col(a["L1_conv_bias"]), "mask_weight": col(a["L1_conv_mask_weight"]),
        "filter": a["L1_conv_filter"].reshape(C, 1)})
    att = pack(ATT_AT, ATT_N, {
        "WQ": a["L2_attn_W_Q"].T, "WK": a["L2_attn_W_K"].T, "WV": a["L2_attn_W_V"].T, "WO": a["L2_attn_W_O"].T,
        "bQ": col(a["L2_attn_b_Q"]), "bK": col(a["L2_attn_b_K"]), "Wr": a["L2_ffn_Wr"].T})
    experts2 = np.concatenate([
        a["L2_ffn_W1"], a["L2_ffn_W2"].reshape(E2, 2, 128, C).transpose(0, 2, 1, 3).reshape(E2, 128, 2 * C),
        a["L2_ffn_b1"].reshape(E2, 2, 128).transpose(0, 2, 1)], axis=2)

    def spread_heads(v):
        out = np.zeros((2, 4, 32, v.shape[1]), np.float32)
        out[:, :, 0:HD, :] = v.reshape(2, 4, HD, v.shape[1])
        return out.reshape(2, 128, v.shape[1]).transpose(1, 0, 2).reshape(128, 2 * v.shape[1])

    parts = {"ffn1": a["L3_attn_ffn_w1"].T,
             "ffn2": a["L3_attn_ffn_w2"].T.reshape(FT, 128, C).transpose(1, 0, 2).reshape(128, FT * C),
             "ffn_b1": col(a["L3_attn_ffn_b1"], FT), "gate": a["L3_ffn_gate_w"]}
    for s in "gl":
        w, b = a[f"L3_attn_{s}_in_w"], a[f"L3_attn_{s}_in_b"]
        parts |= {f"{s}_in": w.T, f"{s}_out": spread_heads(a[f"L3_attn_{s}_out_w"].T), f"{s}_bq": col(b[0:C]),
                  f"{s}_bk": col(b[C:2 * C])}
    l3 = pack(L3_AT, L3_N, parts)
    rows = {"bv": "L0_conv_bv", "bV": "L2_attn_b_V", "bO": "L2_attn_b_O", "br": "L2_ffn_br", "g_out_b": "L3_attn_g_out_b",
            "l_out_b": "L3_attn_l_out_b", "ffn_b2": "L3_attn_ffn_b2", "ln1_g": "L3_attn_ln1_g",
            "ln1_b": "L3_attn_ln1_b", "ln2_g": "L3_attn_ln2_g", "ln2_b": "L3_attn_ln2_b",
            "routing_bias": "L3_ffn_routing_bias"}
    return {
        "x": a["x"].reshape(B, C, PIX),
        "conv": conv,
        "taps": a["L1_conv_weight"].transpose(1, 2, 3, 0).reshape(C, 9, C),
        "att": att,
        "experts2": experts2,
        "b2": a["L2_ffn_b2"],
        "l3": l3,
        "rows": np.concatenate([a[f"L3_attn_{name[0]}_in_b"][2 * C:] if name in ("g_bv", "l_bv") else a[rows[name]]
                                for name, _ in ROWS]),
        "sw1": a["L3_ffn_sw1"], "sw2": a["L3_ffn_sw2"], "sw3": a["L3_ffn_sw3"],
        "w1": a["L3_ffn_w1"], "w2": a["L3_ffn_w2"], "w3": a["L3_ffn_w3"],
    }


def kernel(**inputs):
    import numpy as np
    import concourse.bacc as bacc
    from concourse.bass_utils import run_bass_kernel_spmd

    nc = bacc.Bacc("TRN2", target_bir_lowering=False, num_devices=1)
    arrays = {f"in_{k}": np.ascontiguousarray(v) for k, v in launch_arrays(inputs).items()}
    args = [nc.dram_tensor(k, v.shape, mybir.dt.from_np(v.dtype), kind="ExternalInput").ap() for k, v in arrays.items()]
    out = nc.dram_tensor("out", (B, C, PIX), F32, kind="ExternalOutput").ap()
    build(nc, *args, out)
    got = run_bass_kernel_spmd(nc, [arrays], core_ids=[0])
    return got.results[0]["out"].reshape(B, C, SIDE, SIDE)
```

```python
from contextlib import ExitStack

import concourse.bass as bass
from concourse import mybir

F32 = mybir.dt.float32
BF16 = mybir.dt.bfloat16
F32R = mybir.dt.float32r
ALU = mybir.AluOpType
ACT = mybir.ActivationFunctionType
AX = mybir.AxisListType

C = 128
B = 2
SIDE = 16
PIX = SIDE * SIDE
N = B * PIX
NT = N // 128
C8 = C // 8
GROUP = 4
HEADS, HD = 8, 16
E2, H2 = 8, 256
FF = 512
FT = FF // 128
E3, K3, H3 = 16, 4, 1365
HT = -(-H3 // 128)
H_LAST = H3 - (HT - 1) * 128
H_PAD = HT * 128
SLOTS = 128
MAX_CHUNKS = E3 + (K3 * N - E3) // SLOTS
MIN_CHUNKS = -(-K3 * N // SLOTS)
PAIRS = MAX_CHUNKS // 2
BLOCKS = -(-N // SLOTS)
GROUPS = [(0, 4), (4, 8), (8, HT)]
WINDOW = 5
CREDIT = 2
EPS = 1e-5
MASKED = -1e30
ROUND = 1.5 * 2.0 ** 23

CONV_COLS = [("wq", C8), ("wk", C8), ("wv", C), ("bq", 1), ("bk", 1), ("gamma_pos", 1), ("gamma_chan", 1), ("alpha", 1),
             ("beta", 1), ("conv_bias", 1), ("mask_weight", 1), ("filter", 1)]
ATT_COLS = [("WQ", C), ("WK", C), ("WV", C), ("WO", C), ("bQ", 1), ("bK", 1), ("Wr", E2)]
EXPERT2_N = 2 * C + 2 * C + 2
STEPS2 = 4
L3_COLS = [("g_in", 3 * C), ("l_in", 3 * C), ("g_out", 2 * C), ("l_out", 2 * C), ("ffn1", FF), ("ffn2", FT * C),
           ("g_bq", 1), ("l_bq", 1), ("g_bk", 1), ("l_bk", 1), ("ffn_b1", FT), ("gate", E3)]
ROWS = [("bv", C), ("bV", C), ("bO", C), ("br", E2), ("g_bv", C), ("l_bv", C), ("g_out_b", C), ("l_out_b", C), ("ffn_b2", C), ("ln1_g", C), ("ln1_b", C),
        ("ln2_g", C), ("ln2_b", C), ("routing_bias", E3)]


def columns(table):
    at, out = 0, {}
    for name, n in table:
        out[name] = (at, n)
        at += n
    return out, at


CONV_AT, CONV_N = columns(CONV_COLS)
ATT_AT, ATT_N = columns(ATT_COLS)
L3_AT, L3_N = columns(L3_COLS)
ROW_AT, ROW_N = columns(ROWS)

LN_ATT2, LN_FFN2, LN_ATT3, LN_MID3, LN_END3, LN_FFN3 = range(6)


WARM_MASK = 20
WARM_ATTEND0 = (6, 2, 3)
WARM_GROUP = (6, 7)
WARM_DIVIDE = 4
WARM_NORM = {LN_ATT2: 10, LN_FFN2: 18, LN_ATT3: 12, LN_MID3: 16, LN_FFN3: 30}
WARM_COPY = 1


def turn_of(k):
    return k - (k > LN_END3)


GLOBAL_HEADS, LOCAL_HEADS = 2, 4
WINDOWS = [(0, 0, 128 - WINDOW), (128 - 2 * WINDOW, 128 - WINDOW, 128 + WINDOW), (128, 128 + WINDOW, PIX)]
EDGE_Q, EDGE_K = 2 * WINDOW, 4 * WINDOW
EDGE = EDGE_Q * HEADS
UNITS = []
for _b in range(B):
    UNITS += [("g", _b, t, h) for t in range(2) for h in range(0, HEADS, GLOBAL_HEADS)]
    UNITS += [("e", _b, 1, 0)] + [("l", _b, w, h) for w in (0, 2) for h in range(0, HEADS, LOCAL_HEADS)]
UNITS_B = len(UNITS) // B
UNITS_G = 2 * HEADS // GLOBAL_HEADS


def build(nc, x_in, conv_w, taps_w, att_w, experts2_w, b2_w, l3_w, rows_w, sw1_in, sw2_in, sw3_in, w1_in, w2_in, w3_in, out):
    with ExitStack() as ctx:
        sems = {}

        def sem(name):
            if name not in sems:
                sems[name] = ctx.enter_context(nc.semaphore(name))
            return sems[name]

        def sb(name, shape, dt=F32):
            return ctx.enter_context(nc.sbuf_tensor(name, shape, dt))

        ROOM = 13312
        shared_room = sb("shared_room", [128, ROOM])
        used = {"experts2": ROOM - STEPS2 * EXPERT2_N}

        def room(phase, shape):
            parts, n = shape[0], 1
            for m in shape[1:]:
                n *= m
            at = used.get(phase, 0)
            used[phase] = at + n
            assert used[phase] <= ROOM, used
            view = shared_room[0:parts, at:at + n]
            letters = "abcd"[:len(shape) - 1]
            if len(letters) == 1:
                return view
            return view.rearrange(f"p ({' '.join(letters)}) -> p {' '.join(letters)}",
                                  **dict(zip(letters, shape[1:])))

        bank = [ctx.enter_context(nc.psum_tensor(f"bank{i}", [128, 512], F32)) for i in range(8)]

        conv = sb("conv", [128, CONV_N])
        taps = room("layers01", [128, 9, C])
        att = sb("att", [128, ATT_N])
        b2 = sb("b2", [E2, C])
        l3 = sb("l3", [128, L3_N])
        rows = sb("rows", [128, ROW_N])

        def cc(name):
            a, n = CONV_AT[name]
            return conv[:, a:a + n]

        def ca(name):
            a, n = ATT_AT[name]
            return att[:, a:a + n]

        def c3(name):
            a, n = L3_AT[name]
            return l3[:, a:a + n]

        def row(name, mid=None):
            a, n = ROW_AT[name]
            r = rows[:, a:a + n]
            return r if mid is None else r.unsqueeze(1).broadcast_to([128, mid, n])

        ident = sb("ident", [128, 128])
        ident_bf = sb("ident_bf", [128, 128], BF16)
        band = sb("band", [128, 128], BF16)
        edge_band = sb("edge_band", [128, EDGE_K], BF16)
        ones = sb("ones", [128, 128])
        group_mean = sb("group_mean", [128, 128])
        head_block = sb("head_block", [128, 128])
        head_mask = sb("head_mask", [128, HEADS])
        den_row = sb("den_row", [128, 4])
        ramp = sb("ramp", [128, SIDE])
        before = sb("before", [128, E3, E3])
        before2 = sb("before2", [128, E2, E2])
        earlier_bf = sb("earlier_bf", [128, 128], BF16)
        ones_bf = sb("ones_bf", [128, 128], BF16)
        slot_no = sb("slot_no", [128, (BLOCKS + 1) * SLOTS])
        chunk_no = sb("chunk_no", [128, 2 * PAIRS + 2])
        chunk_odd = sb("chunk_odd", [128, PAIRS + 1, 2])
        chunk_half = sb("chunk_half", [128, PAIRS + 1, 2])

        x0 = room("layers01", [128, B, PIX])
        q0 = room("layers01", [C8, N])
        k0 = room("layers01", [C8, N])
        v0T = room("layers01", [128, NT, C])
        x0T = room("layers01", [128, NT, C])
        p0 = room("layers01", [128, B, 2, PIX])
        p0T = room("layers01", [128, B, 2, PIX])
        pc = room("layers01", [128, B, C])
        pcT = room("layers01", [128, B, C])
        nmax0 = sb("nmax0", [128, B, 2])
        sum0 = sb("sum0", [128, B, 2])
        minc = sb("minc", [128, B])
        sumc = sb("sumc", [128, B])
        mix = sb("mix", [128, 4])
        x1 = sb("x1", [128, B, PIX])
        gst = sb("gst", [128, B, 6])
        gmv = sb("gmv", [128, B, 2])
        gdev = sb("gdev", [128, B])
        gm = sb("gm", [128, B])
        gvar = sb("gvar", [128, B])
        gr = sb("gr", [128, 4, B])
        gn = room("layers01", [128, B, SIDE, SIDE])
        sums = sb("sums", [128, 2, B, SIDE])
        weighted = sb("weighted", [128, 2, B, SIDE])
        moment = sb("moment", [128, 2, B])
        total = sb("total", [128, B])
        mu = sb("mu", [128, 2, B])
        mask_w = sb("mask_w", [128, 1])
        dist = sb("dist", [128, 2, B, SIDE])
        mask = room("layers01", [128, B, SIDE, SIDE])
        pad = room("layers01", [128, B, SIDE + 2, SIDE + 2])
        x2 = sb("x2", [128, B, PIX])

        t2 = room("layer2", [128, NT, C])
        t3 = sb("t3", [128, NT, C])
        t4 = sb("t4", [128, NT, C])
        u3 = sb("u3", [128, NT, C])
        z3 = sb("z3", [128, NT, C])
        t5 = sb("t5", [128, NT, C])
        y = [None if k == LN_END3 else sb(f"y{k}", [128, NT, C]) for k in range(6)]
        yT = [None if k == LN_END3 else sb(f"yT{k}", [128, N]) for k in range(6)]
        lst = sb("lst", [128, NT, 6])
        lmv = sb("lmv", [128, 6, NT, 2])
        lve = sb("lve", [128, 6, NT])
        lsd = sb("lsd", [128, 6, NT])
        lr0 = sb("lr0", [128, 6, NT])
        nothing = sb("nothing", [1, 1])
        eps = sb("eps", [128, 1])
        lra = sb("lra", [128, 2, NT])
        lr = sb("lr", [128, 6, NT])

        kmax = sb("kmax", [128, B])
        knmax = sb("knmax", [128, B])
        kq = sb("kq", [128, B])
        kqb = room("layer2", [128, B, 128])
        ek = room("layer2", [128, B, PIX])
        sek = sb("sek", [128, B])
        ekT = room("layer2", [128, NT, C])
        v2 = room("layer2", [128, NT, C])
        kv = room("layer2", [128, B, C])
        ksum = room("layer2", [128, B, HEADS])
        qmax = sb("qmax", [128, NT * HEADS])
        qs = room("layer2", [128, NT * HEADS, HD])
        eq = room("layer2", [128, NT, C])
        eqT = room("layer2", [128, N])
        rd2 = sb("rd2", [128, NT * HEADS])
        rden2 = room("layer2", [128, NT, HEADS, HD])
        num2 = room("layer2", [128, N])
        heads2 = room("layer2", [128, N])

        lg2 = sb("lg2", [128, NT, E2])
        m2 = sb("m2", [128, NT])
        e2 = sb("e2", [128, NT, E2])
        s2 = sb("s2", [128, NT])
        pr2 = sb("pr2", [128, NT, E2])
        cmp2 = room("route2", [128, 2, NT * E2, E2])
        rank2 = sb("rank2", [128, NT, E2])
        comb2 = sb("comb2", [128, NT, E2])
        comb2T = sb("comb2T", [E2, N])
        ew2 = [room("experts2", [128, EXPERT2_N]) for p in range(STEPS2)]
        h2 = sb("h2", [128, 4, N])

        q3 = [room("keys", [128, N]) for s in "gl"]
        k3 = [room("keys", [128, N]) for s in "gl"]
        km3 = [[room("keys", [128, HEADS, PIX]) for b in range(B)] for s in "gl"]
        vg = sb("vg", [128, NT, HEADS, 32])
        vl = sb("vl", [128, B * len(WINDOWS), HEADS, 32])
        q_edge = sb("q_edge", [128, B, EDGE_Q, HEADS])
        nmax3 = sb("nmax3", [128, len(UNITS), 4])
        p3 = sb("p3", [128, 2, 512])
        p3T = room("keys", [128, 2, 512])
        o3 = sb("o3", [128, 2, 512])
        rd3 = sb("rd3", [128, 16])
        rd3_wide = sb("rd3_wide", [128, 4, 4, 32])
        ob3 = sb("ob3", [128, B, 2, 2, PIX])
        hf3 = room("keys", [128, FT, N])

        lg3 = sb("lg3", [128, NT, E3])
        m3 = sb("m3", [128, NT])
        e3 = sb("e3", [128, NT, E3])
        s3 = sb("s3", [128, NT])
        cmp3 = room("mixture", [128, 2, NT * E3, E3])
        rank3 = sb("rank3", [128, NT, E3])
        chosen = sb("chosen", [128, NT, E3])
        chosen_bf = sb("chosen_bf", [128, NT, E3], BF16)
        weight = sb("weight", [128, NT, E3])
        left = sb("left", [128, NT, E3])
        place = sb("place", [128, NT, E3])
        count = sb("count", [128, E3])
        chunks = sb("chunks", [128, E3])
        first = sb("first", [128, E3])
        reach = room("mixture", [128, 2 * PAIRS + 2, E3])
        NK = 2 * PAIRS + 2
        plan = sb("plan", [128, 5, NK])
        plan_int = sb("plan_int", [1, 3, NK], mybir.dt.int32)
        pairs = sb("pairs", [128, 6])
        pairs_int = sb("pairs_int", [1, 2], mybir.dt.int32)
        w1 = [sb(f"w1_{p}", [128, H_PAD]) for p in range(2)]
        w2 = [sb(f"w2_{p}", [128, H_PAD]) for p in range(2)]
        w3 = [sb(f"w3_{p}", [128, HT, C]) for p in range(2)]
        tokens_left = room("mixture", [128, NT, C])
        silu = room("mixture", [128, 2, 512])
        hs = room("mixture", [128, 3, N])
        he = room("mixture", [128, 2, HT, SLOTS])
        xe = room("mixture", [128, 2, SLOTS])
        outT = room("mixture", [128, B, PIX])

        pick_bf = sb("pick_bf", [128, 2, NT, SLOTS], BF16)
        y_bf = sb("y_bf", [128, NT, 3, C], BF16)
        spread = sb("spread", [128, 2, N], F32R)
        ye_hi = sb("ye_hi", [128, 2, C], F32R)
        ye_lo = sb("ye_lo", [128, 2, C], F32R)
        slot_weight = sb("slot_weight", [128, 2])
        weight_bf = sb("weight_bf", [128, NT, E3, 3], BF16)

        block = ctx.enter_context(nc.Block())

        @block.sync
        def _(sp):
            sp.dma_start(x0[:], x_in.rearrange("b c n -> c b n")).then_inc(sem("x_in"), 16)
            sp.dma_start(conv[:], conv_w).then_inc(sem("conv_in"), 16)
            sp.dma_start(rows[:], rows_w.partition_broadcast(128)).then_inc(sem("rows_in"), 16)
            sp.dma_start(taps[:], taps_w).then_inc(sem("taps_in"), 16)
            sp.dma_start(att[:], att_w).then_inc(sem("att_in"), 16)
            sp.dma_start(b2[:], b2_w).then_inc(sem("b2_in"), 16)
            sp.dma_start(l3[:], l3_w).then_inc(sem("l3_in"), 16)
            for p in range(STEPS2):
                sp.dma_start(ew2[p][:], experts2_w[p, :, :]).then_inc(sem(f"ew2_in{p}"), 16)
            for e in range(STEPS2, E2):
                p = e % STEPS2
                sp.wait_ge(sem("expert2_mm"), CREDIT + e - STEPS2 + 1)
                sp.dma_start(ew2[p][:], experts2_w[e, :, :]).then_inc(sem(f"ew2_in{p}"), 16)

            def load(p, a1, a2, a3):
                full = (HT - 1) * 128
                sp.dma_start(w1[p][:, 0:H3], a1).then_inc(sem(f"w1_in{p}"), 16)
                sp.dma_start(w2[p][:, 0:H3], a2).then_inc(sem(f"w2_in{p}"), 16)
                sp.dma_start(w3[p][:, 0:HT - 1, :], a3[0:full, :].rearrange("(t p) d -> p t d", p=128))\
                    .then_inc(sem(f"w3_in{p}"), 16)
                sp.dma_start(w3[p][0:H_LAST, HT - 1, :], a3[full:H3, :]).then_inc(sem(f"w3_in{p}"), 16)

            load(0, sw1_in, sw2_in, sw3_in)
            sp.wait_ge(sem("plan_ready"), 1)
            n_pairs = sp.value_load(pairs_int[0:1, 0:1], min_val=MIN_CHUNKS // 2, max_val=PAIRS)

            def load_chunk(p, k, always=False):
                sp.wait_ge(sem("down_mm"), k + 1)
                e = sp.value_load(plan_int[0:1, 0, bass.ds(k, 1)], min_val=0, max_val=E3 - 1)
                weights = (w1_in[bass.ds(e, 1), :, :].rearrange("e c h -> c (e h)"),
                           w2_in[bass.ds(e, 1), :, :].rearrange("e c h -> c (e h)"),
                           w3_in[bass.ds(e, 1), :, :].rearrange("e h d -> (e h) d"))
                if always:
                    load(p, *weights)
                    return
                other = sp.value_load(plan_int[0:1, 2, bass.ds(k, 1)], min_val=0, max_val=1)
                with sp.If(other > 0):
                    load(p, *weights)
                with sp.If(other < 1):
                    sp.sem_inc(sem(f"w1_in{p}"), 16)
                    sp.sem_inc(sem(f"w2_in{p}"), 16)
                    sp.sem_inc(sem(f"w3_in{p}"), 32)

            load_chunk(1, 0, always=True)
            load_chunk(0, 1, always=True)
            with sp.Fori(1, n_pairs) as i:
                load_chunk(1, 2 * i)
                load_chunk(0, 2 * i + 1)
            single = sp.value_load(pairs_int[0:1, 1:2], min_val=0, max_val=1)
            with sp.If(single > 0):
                load_chunk(1, 2 * n_pairs)
            sp.wait_ge(sem("out_ready"), 1)
            sp.dma_start(out.rearrange("b c n -> c b n"), outT[:]).then_inc(sem("out_stored"), 16)
            sp.wait_ge(sem("out_stored"), 16)

        @block.gpsimd
        def _(pool):
            def select(out, pattern, base, mult, op, fill):
                return nc.gpsimd.affine_select(out=out, in_=out, compare_op=op, fill=fill, base=base, pattern=pattern,
                                               channel_multiplier=mult)

            made = [0]

            def make(ins):
                made[0] += 1
                ins.then_inc(sem("pool_step"), 1)
                pool.wait_ge(sem("pool_step"), made[0])

            nc.gpsimd.memset(ones_bf[:], 1.0)
            make(nc.gpsimd.memset(ident[:], 0.0))
            make(select(ident[:], [[-1, 128]], 0, 1, ALU.not_equal, 1.0))
            make(nc.gpsimd.memset(eps[:], EPS))
            nc.gpsimd.memset(ones[:], 1.0).then_inc(sem("ident_made"), 1)
            nc.gpsimd.memset(pad[:], 0.0).then_inc(sem("pad_made"), 1)
            g = group_mean[:].rearrange("p (g c) -> p g c", c=GROUP)
            make(nc.gpsimd.memset(group_mean[:], 1.0 / GROUP))
            make(select(g, [[-GROUP, C // GROUP], [0, GROUP]], 0, 1, ALU.is_ge, 0.0))
            make(select(g, [[GROUP, C // GROUP], [0, GROUP]], GROUP - 1, -1, ALU.is_ge, 0.0))
            nc.gpsimd.iota(ramp[:], pattern=[[1, SIDE]], base=1, channel_multiplier=0,
                           allow_small_or_imprecise_dtypes=True).then_inc(sem("group_made"), 1)
            g = head_block[:].rearrange("p (g c) -> p g c", c=HD)
            make(nc.gpsimd.memset(head_block[:], 1.0))
            make(select(g, [[-HD, HEADS], [0, HD]], 0, 1, ALU.is_ge, 0.0))
            make(select(g, [[HD, HEADS], [0, HD]], HD - 1, -1, ALU.is_ge, 0.0))
            make(nc.gpsimd.memset(head_mask[:], 1.0))
            make(select(head_mask[:], [[-HD, HEADS]], 0, 1, ALU.is_ge, 0.0))
            make(select(head_mask[:], [[HD, HEADS]], HD - 1, -1, ALU.is_ge, 0.0))
            make(nc.gpsimd.memset(before2[:], 1.0))
            make(select(before2[:], [[1, E2], [-1, E2]], -1, 0, ALU.is_ge, 0.0))
            make(nc.gpsimd.memset(before[:], 1.0))
            make(select(before[:], [[1, E3], [-1, E3]], -1, 0, ALU.is_ge, 0.0))
            make(nc.gpsimd.memset(den_row[:], 0.0))
            make(select(den_row[:], [[-32, 4]], -HD, 1, ALU.not_equal, 1.0))
            make(nc.gpsimd.memset(band[:], 0.0))
            make(select(band[:], [[-1, 128]], WINDOW, 1, ALU.is_ge, MASKED))
            make(select(band[:], [[1, 128]], WINDOW, -1, ALU.is_ge, MASKED))
            make(nc.gpsimd.memset(edge_band[:], 0.0))
            make(select(edge_band[:], [[HEADS, EDGE_K]], HEADS - 1, -1, ALU.is_ge, MASKED))
            make(select(edge_band[:], [[-HEADS, EDGE_K]], 2 * WINDOW * HEADS, 1, ALU.is_ge, MASKED))
            make(nc.gpsimd.tensor_copy(ident_bf[:], ident[:]))
            make(nc.gpsimd.memset(earlier_bf[:], 1.0))
            make(select(earlier_bf[:], [[1, 128]], -1, -1, ALU.is_ge, 0.0))
            make(nc.gpsimd.iota(slot_no[:], pattern=[[1, (BLOCKS + 1) * SLOTS]], base=0, channel_multiplier=0,
                                allow_small_or_imprecise_dtypes=True))
            for numbers, pattern in ((chunk_no, [[1, 2 * PAIRS + 2]]), (chunk_odd, [[0, PAIRS + 1], [1, 2]]),
                                     (chunk_half, [[1, PAIRS + 1], [0, 2]])):
                make(nc.gpsimd.iota(numbers[:], pattern=pattern, base=0, channel_multiplier=0,
                                    allow_small_or_imprecise_dtypes=True))
            for p in range(2):
                make(nc.gpsimd.memset(w1[p][:, H3:H_PAD], 0.0))
                make(nc.gpsimd.memset(w2[p][:, H3:H_PAD], 0.0))
            make(nc.gpsimd.memset(vg[:], 0.0))
            make(nc.gpsimd.memset(vl[:], 0.0))
            make(nc.gpsimd.memset(vg[:, :, :, HD:HD + 1], 1.0))
            nc.gpsimd.memset(vl[:, :, :, HD:HD + 1], 1.0).then_inc(sem("masks_made"), 1)
            for s in range(2):
                pool.wait_ge(sem("k3_ready"), s + 1)
                for h in range(HEADS):
                    last = nc.gpsimd.tensor_scalar(km3[s][1][:, h, :], k3[s][:, PIX:N], head_mask[:, h:h + 1], 0.0,
                                                   ALU.mult, ALU.add)
                last.then_inc(sem("km3_image1"), 1)

            pool.wait_ge(sem("y_ready"), NT * turn_of(LN_FFN3) + NT)
            tokens = y[LN_FFN3]
            make(nc.gpsimd.tensor_copy(y_bf[:, :, 0, :], tokens[:]))
            make(nc.gpsimd.tensor_tensor(tokens_left[:], tokens[:], y_bf[:, :, 0, :], ALU.subtract))
            make(nc.gpsimd.tensor_copy(y_bf[:, :, 1, :], tokens_left[:]))
            nc.gpsimd.tensor_tensor(y_bf[:, :, 2, :], tokens_left[:], y_bf[:, :, 1, :], ALU.subtract)\
                .then_inc(sem("y_bf_ready"), 1)

        @block.tensor
        def _(pe):
            mm = nc.tensor.matmul
            tr = nc.tensor.transpose

            def keep_warm(b, products):
                for _ in range(products):
                    mm(bank[b][:, :], ones_bf[:], ones_bf[:].unsqueeze(1).broadcast_to([128, 4, 128]),
                       start=True, stop=True)

            pe.sem_inc(sem("expert2_mm"), CREDIT)
            pe.sem_inc(sem("down_mm"), 1)
            pe.sem_inc(sem("scatter_mm"), 1)
            pe.sem_inc(sem("spread_mm"), 1)
            pe.wait_ge(sem("x_in"), 16)
            pe.wait_ge(sem("conv_in"), 16)
            pe.wait_ge(sem("ident_made"), 1)
            xf = x0[:].rearrange("p b n -> p (b n)")
            mm(bank[0][0:C8, :], cc("wq"), xf, start=True, stop=True).then_inc(sem("q0_mm"), 1)
            mm(bank[1][0:C8, :], cc("wk"), xf, start=True, stop=True).then_inc(sem("k0_mm"), 1)
            for t in range(NT):
                last = tr(bank[3][:, 128 * t:128 * t + 128], xf[:, 128 * t:128 * t + 128], ident[:])
            last.then_inc(sem("x0T_mm"), 1)
            for t in range(NT):
                last = mm(bank[2][:, 128 * t:128 * t + 128], xf[:, 128 * t:128 * t + 128], cc("wv"),
                          start=True, stop=True)
            last.then_inc(sem("v0_mm"), 1)
            pe.wait_ge(sem("q0_ready"), 1)
            pe.wait_ge(sem("k0_ready"), 1)
            for b in range(B):
                for t in range(2):
                    last = mm(bank[4 + b][:, PIX * t:PIX * t + PIX], q0[:, b * PIX + 128 * t:b * PIX + 128 * t + 128],
                              k0[:, b * PIX:b * PIX + PIX], start=True, stop=True)
                last.then_inc(sem("energy_mm"), 1)
            pe.wait_ge(sem("x0T_ready"), 1)
            for b in range(B):
                for t in range(2):
                    last = mm(bank[6][:, C * b:C * b + C], x0T[:, 2 * b + t, :], x0T[:, 2 * b + t, :],
                              start=(t == 0), stop=(t == 1))
            last.then_inc(sem("energyc_mm"), 1)
            pe.wait_ge(sem("v0_ready"), 1)
            for b in range(B):
                keep_warm(7, WARM_ATTEND0[b])
                pe.wait_ge(sem("p0_ready"), 4 * b + 4)
                for j in range(2):
                    for t in range(2):
                        last = tr(bank[b][:, j * PIX + 128 * t:j * PIX + 128 * t + 128],
                                  p0[:, b, t, 128 * j:128 * j + 128], ident[:])
                last.then_inc(sem("p0T_mm"), 1)
            pe.wait_ge(sem("pc_ready"), B)
            for b in range(B):
                last = tr(bank[2][:, C * b:C * b + C], pc[:, b, :], ident[:])
            last.then_inc(sem("pcT_mm"), 1)
            keep_warm(7, WARM_ATTEND0[2])
            pe.wait_ge(sem("pcT_ready"), 1)
            for b in range(B):
                pe.wait_ge(sem("p0T_ready"), b + 1)
                for j in range(2):
                    mm(bank[7 - 4 * b][:, 0:PIX], v0T[:, 2 * b + j, :], p0T[:, b, j, :],
                       start=(j == 0), stop=False)
                mm(bank[7 - 4 * b][:, 0:PIX], pcT[:, b, :], x0[:, b, :], start=False, stop=True)\
                    .then_inc(sem("layer0_mm"), 1)
            keep_warm(4, WARM_GROUP[0])
            pe.wait_ge(sem("group_made"), 1)
            pe.wait_ge(sem("gmv_ready"), 1)
            mm(bank[0][:, 0:B], group_mean[:], gmv[:, :, 0], start=True, stop=True).then_inc(sem("gmean_mm"), 1)
            keep_warm(4, WARM_GROUP[1])
            pe.wait_ge(sem("gdev_ready"), 1)
            mm(bank[1][:, 0:B], group_mean[:], gdev[:], start=True, stop=True).then_inc(sem("gvar_mm"), 1)
            keep_warm(5, WARM_MASK)
            pe.wait_ge(sem("taps_in"), 16)
            def turn_x2(b):
                pe.wait_ge(sem("x2_ready"), b + 1)
                for t in range(2):
                    last = tr(bank[7 if b else 3][:, 128 * t:128 * t + 128], x2[:, b, 128 * t:128 * t + 128], ident[:])
                last.then_inc(sem("t2_mm"), 1)

            for b in range(B):
                pe.wait_ge(sem("pad_ready"), b + 1)
                for k in range(9):
                    i, j = k // 3, k % 3
                    last = mm(bank[1 if b else 2][:, 0:PIX], taps[:, k, :], pad[:, b, i:i + SIDE, j:j + SIDE],
                              start=(k == 0), stop=(k == 8))
                    if b and k == 5:
                        turn_x2(0)
                last.then_inc(sem("conv_mm"), 1)
            turn_x2(1)

            def ln_transpose(k, b, spare):
                keep_warm(spare, WARM_NORM[k])
                for t in range(NT):
                    pe.wait_ge(sem("y_ready"), NT * turn_of(k) + t + 1)
                    tr(bank[b + t // 2][:, 128 * (t % 2):128 * (t % 2) + 128], y[k][:, t, :], ident[:]).then_inc(sem("yT_mm"), 1)
                keep_warm(spare, WARM_COPY)

            def wait_turned(k, image):
                pe.wait_ge(sem("yT_ready"), B * turn_of(k) + image + 1)

            def images_product(dst, w, k):
                for b in range(B):
                    wait_turned(k, b)
                    last = mm(dst[:, PIX * b:PIX * b + PIX], w, yT[k][:, PIX * b:PIX * b + PIX], start=True, stop=True)
                return last

            ln_transpose(LN_ATT2, 4, spare=6)
            pe.wait_ge(sem("att_in"), 16)
            yt = yT[LN_ATT2]
            images_product(bank[0], ca("WK"), LN_ATT2).then_inc(sem("k2_mm"), 1)
            for t in range(NT):
                mm(bank[1][:, 128 * t:128 * t + 128], yt[:, 128 * t:128 * t + 128], ca("WQ"), start=(t == 0),
                   stop=False, skip_group_check=True)
            for t in range(NT):
                last = mm(bank[2][:, 128 * t:128 * t + 128], yt[:, 128 * t:128 * t + 128], ca("WV"),
                          start=True, stop=True)
            last.then_inc(sem("v2_mm"), 1)
            for t in range(NT):
                pe.wait_ge(sem("kqb_ready"), t // 2 + 1)
                last = mm(bank[1][:, 128 * t:128 * t + 128], kqb[:, t // 2, :], ident[:], start=False,
                          stop=(t == NT - 1), skip_group_check=True)
            last.then_inc(sem("q2_mm"), 1)
            pe.wait_ge(sem("t2_ready"), 1)
            for b in range(B):
                pe.wait_ge(sem("ek_ready"), b + 1)
                for t in range(2):
                    last = tr(bank[3][:, (2 * b + t) * 128:(2 * b + t) * 128 + 128], ek[:, b, 128 * t:128 * t + 128],
                              ident[:])
            last.then_inc(sem("ekT_mm"), 1)
            pe.wait_ge(sem("ekT_ready"), 1)
            pe.wait_ge(sem("v2_ready"), 1)
            for b in range(B):
                for t in range(2):
                    last = mm(bank[5][:, C * b:C * b + C], ekT[:, 2 * b + t, :], v2[:, 2 * b + t, :],
                              start=(t == 0), stop=(t == 1))
            last.then_inc(sem("kv_mm"), 1)
            pe.wait_ge(sem("eq_ready"), 1)
            pe.wait_ge(sem("ekT_ready"), 1)
            for t in range(NT):
                last = tr(bank[3][:, 128 * t:128 * t + 128], eq[:, t, :], ident[:])
            last.then_inc(sem("eqT_mm"), 1)
            pe.wait_ge(sem("eqT_ready"), 1)
            pe.wait_ge(sem("kv_ready"), 2)
            for t in range(NT):
                last = mm(bank[4][:, HEADS * t:HEADS * t + HEADS], eqT[:, 128 * t:128 * t + 128], ksum[:, t // 2, :],
                          start=True, stop=True)
            last.then_inc(sem("den2_mm"), 1)
            for b in range(B):
                last = mm(bank[6][:, PIX * b:PIX * b + PIX], kv[:, b, :], eqT[:, PIX * b:PIX * b + PIX],
                          start=True, stop=True)
            last.then_inc(sem("num2_mm"), 1)
            pe.wait_ge(sem("rden2_ready"), 1)
            for t in range(NT):
                last = mm(bank[7][:, 128 * t:128 * t + 128],
                          rden2[:, t, :, :].rearrange("p h c -> p (h c)"), ident[:],
                          start=True, stop=True)
            last.then_inc(sem("spread2_mm"), 1)
            for t in range(NT):
                pe.wait_ge(sem("heads2_ready"), t // 2 + 1)
                last = mm(bank[0][:, 128 * t:128 * t + 128], heads2[:, 128 * t:128 * t + 128], ca("WO"),
                          start=True, stop=True)
            last.then_inc(sem("att2_mm"), 1)

            ln_transpose(LN_FFN2, 4, spare=2)
            yt = yT[LN_FFN2]
            for t in range(NT):
                wait_turned(LN_FFN2, t // 2)
                last = mm(bank[1][:, E2 * t:E2 * t + E2], yt[:, 128 * t:128 * t + 128], ca("Wr"), start=True, stop=True)
            last.then_inc(sem("route2_mm"), 1)
            pe.wait_ge(sem("heads2_ready"), B)
            wait_turned(LN_FFN2, B - 1)
            pe.wait_ge(sem("kv_ready"), 2)
            pe.wait_ge(sem("eqT_ready"), 1)

            def hidden2(i, p):
                e = STEPS2 * i + p
                pe.wait_ge(sem(f"ew2_in{p}"), 16 * i + 16)
                pe.wait_ge(sem("h2_ready"), 2 * e + 2)
                for half in range(2):
                    mm(bank[4 + 2 * (p % 2) + half][:, :], ew2[p][:, C * half:C * half + C], yt[:],
                       start=True, stop=True).then_inc(sem("hidden2_mm"), 1)

            def output2(i, p):
                e = STEPS2 * i + p
                pe.wait_ge(sem("y2_added"), e + 1)
                for half in range(2):
                    pe.wait_ge(sem("h2_ready"), 2 * CREDIT + 2 * e + half + 1)
                    for t in range(NT):
                        last = mm(bank[2 + p % 2][:, 128 * t:128 * t + 128],
                                  h2[:, 2 * (p % 2) + half, 128 * t:128 * t + 128],
                                  ew2[p][:, 2 * C + C * half:3 * C + C * half],
                                  start=(half == 0 and t == 0), stop=(half == 1 and t == NT - 1),
                                  skip_group_check=True)
                last.then_inc(sem("expert2_mm"), 1)

            with pe.Fori(0, E2 // STEPS2) as i:
                hidden2(i, 0)
                for p in range(1, STEPS2):
                    hidden2(i, p)
                    output2(i, p - 1)
                output2(i, STEPS2 - 1)
            pe.wait_ge(sem("comb2_ready"), 1)
            for t in range(NT):
                last = tr(bank[0][0:E2, 128 * t:128 * t + 128], comb2[:, t, :], ident[:])
            last.then_inc(sem("comb2T_mm"), 1)
            pe.wait_ge(sem("comb2T_ready"), 1)
            pe.wait_ge(sem("b2_in"), 16)
            for t in range(NT):
                last = mm(bank[1][:, 128 * t:128 * t + 128], comb2T[:, 128 * t:128 * t + 128], b2[:],
                          start=True, stop=True)
            last.then_inc(sem("bias2_mm"), 1)

            ln_transpose(LN_ATT3, 2, spare=0)
            pe.wait_ge(sem("l3_in"), 16)
            yt = yT[LN_ATT3]

            def queries_keys(s):
                w = c3(("g_in", "l_in")[s])
                images_product(bank[5 + 2 * s], w[:, C:2 * C], LN_ATT3).then_inc(sem("k3_mm"), 1)
                mm(bank[4 + 2 * s][:, :], w[:, 0:C], yt[:], start=True, stop=True).then_inc(sem("q3_mm"), 1)

            queries_keys(0)
            for t in range(NT):
                last = mm(bank[2][:, 128 * t:128 * t + 128], yt[:, 128 * t:128 * t + 128], c3("g_in")[:, 2 * C:3 * C],
                          start=True, stop=True)
            last.then_inc(sem("vg_mm"), 1)

            def local_values():
                pe.wait_ge(sem("q3_ready"), 1)
                pe.wait_ge(sem("k3_ready"), 1)
                for b in range(B):
                    for w, (start, _, _) in enumerate(WINDOWS):
                        last = mm(bank[4 + b][:, 128 * w:128 * w + 128], yt[:, b * PIX + start:b * PIX + start + 128],
                                  c3("l_in")[:, 2 * C:3 * C], start=True, stop=True)
                last.then_inc(sem("vl_mm"), 1)

            def scores(u):
                kind, b, t, h = UNITS[u]
                if u >= 2:
                    pe.wait_ge(sem("exp3"), u - 1)
                if kind == "g":
                    if b:
                        pe.wait_ge(sem("km3_image1"), 1)
                    else:
                        pe.wait_ge(sem("km3_global0"), h + GLOBAL_HEADS)
                    mm(bank[u % 2][:, :], q3[0][:, b * PIX + 128 * t:b * PIX + 128 * t + 128],
                       km3[0][b][:, h:h + GLOBAL_HEADS, :], start=True, stop=True).then_inc(sem("score3_mm"), 1)
                elif kind == "e":
                    start = b * PIX + WINDOWS[t][0]
                    pe.wait_ge(sem("q_edge_ready"), 1)
                    mm(bank[u % 2][0:EDGE, 0:EDGE_K], q_edge[:, b, :, :].rearrange("p q h -> p (q h)"),
                       k3[1][:, start:start + EDGE_K], start=True, stop=False)
                    mm(bank[u % 2][0:EDGE, 0:EDGE_K], ident_bf[:, 0:EDGE], edge_band[:], start=False, stop=True)\
                        .then_inc(sem("score3_mm"), 1)
                else:
                    start = WINDOWS[t][0]
                    if b == 0:
                        pe.wait_ge(sem("km3_local0"), HEADS)
                    else:
                        pe.wait_ge(sem("km3_image1"), 2)
                    mm(bank[u % 2][:, :], q3[1][:, b * PIX + start:b * PIX + start + 128],
                       km3[1][b][:, h:h + LOCAL_HEADS, start:start + 128], start=True, stop=False)
                    mm(bank[u % 2][:, :], ident_bf[:], band[:].unsqueeze(1).broadcast_to([128, LOCAL_HEADS, 128]),
                       start=False, stop=True).then_inc(sem("score3_mm"), 1)

            def turn(u):
                pe.wait_ge(sem("exp3"), u + 1)
                if u >= 2:
                    pe.wait_ge(sem("p3T_ready"), u - 1)
                if UNITS[u][0] == "e":
                    tr(bank[2 + u % 2][0:EDGE_K, 0:EDGE], p3[0:EDGE, u % 2, 0:EDGE_K], ident[0:EDGE, 0:EDGE])\
                        .then_inc(sem("p3T_mm"), 1)
                    return
                for n in range(4):
                    last = tr(bank[2 + u % 2][:, 128 * n:128 * n + 128], p3[:, u % 2, 128 * n:128 * n + 128], ident[:])
                last.then_inc(sem("p3T_mm"), 1)

            def attend(u):
                kind, b, t, h0 = UNITS[u]
                if u % UNITS_B == 0 and b:
                    pe.wait_ge(sem("o3_copied"), 1)
                if u % UNITS_B == UNITS_G and b:
                    pe.wait_ge(sem("o3_copied"), 2)
                pe.wait_ge(sem("p3T_ready"), u + 1)
                if kind == "g":
                    for n in range(GLOBAL_HEADS):
                        h = h0 + n
                        r = 32 * (h % 4)
                        for j in range(2):
                            last = mm(bank[4][r:r + 32, h // 4 * PIX + 128 * t:h // 4 * PIX + 128 * t + 128],
                                      vg[:, 2 * b + j, h, :], p3T[:, u % 2, (2 * n + j) * 128:(2 * n + j) * 128 + 128],
                                      start=(j == 0), stop=(j == 1), tile_position=(0, r))
                elif kind == "e":
                    _, first, end = WINDOWS[t]
                    turned = p3T[0:EDGE_K, u % 2, 0:EDGE].rearrange("p (q h) -> p q h", h=HEADS)
                    for h in range(HEADS):
                        r = 32 * (h % 4)
                        last = mm(bank[5][r:r + 32, h // 4 * PIX + first:h // 4 * PIX + end],
                                  vl[0:EDGE_K, b * len(WINDOWS) + t, h, :], turned[:, :, h],
                                  start=True, stop=True, tile_position=(0, r))
                else:
                    start, first, end = WINDOWS[t]
                    for n in range(LOCAL_HEADS):
                        h = h0 + n
                        r = 32 * (h % 4)
                        last = mm(bank[5][r:r + 32, h // 4 * PIX + first:h // 4 * PIX + end],
                                  vl[:, b * len(WINDOWS) + t, h, :],
                                  p3T[:, u % 2, 128 * n + first - start:128 * n + end - start],
                                  start=True, stop=True, tile_position=(0, r))
                last.then_inc(sem("attend3"), 1)

            def denominators(n):
                pe.wait_ge(sem("o3_copied"), n + 1)
                if n:
                    pe.wait_ge(sem("ob3_ready"), n)
                for q in range(4):
                    last = mm(bank[6][:, 4 * q:4 * q + 4], o3[:, n % 2, 128 * q:128 * q + 128], den_row[:],
                              start=True, stop=True)
                last.then_inc(sem("den3_mm"), 1)

            def spread_quotients(n):
                pe.wait_ge(sem("rd3_ready"), n + 1)
                for q in range(4):
                    last = mm(bank[6][:, 128 * q:128 * q + 128],
                              rd3_wide[:, q, :, :].rearrange("p j c -> p (j c)"), ident[:],
                              start=True, stop=True)
                last.then_inc(sem("spread3_mm"), 1)

            def project(b, s):
                if b and s == 0:
                    pe.wait_ge(sem("o3_copied"), 3)
                pe.wait_ge(sem("ob3_ready"), 2 * b + s + 1)
                for t in range(2):
                    for half in range(2):
                        last = mm(bank[4 if b else 7][:, 128 * t:128 * t + 128],
                                  ob3[:, b, s, half, 128 * t:128 * t + 128],
                                  c3(("g_out", "l_out")[s])[:, C * half:C * half + C],
                                  start=(s == 0 and t == 0 and half == 0), stop=(s == 1 and t == 1 and half == 1),
                                  skip_group_check=True)
                if s == 1:
                    last.then_inc(sem("att3_mm"), 1)

            pe.wait_ge(sem("masks_made"), 1)
            pe.wait_ge(sem("q3_ready"), 1)
            for u in range(len(UNITS) + 3):
                if u == UNITS_G:
                    pe.wait_ge(sem("q3_ready"), 2)
                    pe.wait_ge(sem("k3_ready"), 2)
                if u < len(UNITS):
                    scores(u)
                if u == 1:
                    queries_keys(1)
                    local_values()
                if u == 3:
                    pe.wait_ge(sem("v3_ready"), 2)
                if 2 <= u <= len(UNITS) + 1:
                    turn(u - 2)
                if u >= 3:
                    attend(u - 3)
                for n, end in enumerate((UNITS_G, UNITS_B, UNITS_B + UNITS_G)):
                    if u == end + 4:
                        denominators(n)
                    if u == end + 5:
                        spread_quotients(n)
                if u == UNITS_B + 6:
                    project(0, 0)
                    project(0, 1)
            keep_warm(0, WARM_DIVIDE)
            denominators(3)
            project(1, 0)
            keep_warm(0, 1)
            spread_quotients(3)
            keep_warm(0, WARM_DIVIDE)
            project(1, 1)

            ln_transpose(LN_MID3, 5, spare=0)
            for f in range(FT):
                images_product(bank[1 + f], c3("ffn1")[:, 128 * f:128 * f + 128], LN_MID3).then_inc(sem("ff3_mm"), 1)
            for b in range(B):
                for f in range(FT):
                    pe.wait_ge(sem("hf3_ready"), f + 1)
                    for t in range(2):
                        token = b * PIX + 128 * t
                        last = mm(bank[0 if b else 6][:, 128 * t:128 * t + 128], hf3[:, f, token:token + 128],
                                  c3("ffn2")[:, C * f:C * f + C], start=(f == 0 and t == 0),
                                  stop=(f == FT - 1 and t == 1), skip_group_check=True)
                last.then_inc(sem("ffn3_mm"), 1)

            ln_transpose(LN_FFN3, 5, spare=1)
            yt = yT[LN_FFN3]
            for t in range(NT):
                wait_turned(LN_FFN3, t // 2)
                last = mm(bank[4][:, E3 * t:E3 * t + E3], yt[:, 128 * t:128 * t + 128], c3("gate"), start=True, stop=True)
            last.then_inc(sem("route3_mm"), 1)

            def shared_up(t):
                if t >= 2:
                    pe.wait_ge(sem("hs_ready"), t - 1)
                if t == 0:
                    pe.wait_ge(sem("w1_in0"), 16)
                    pe.wait_ge(sem("w2_in0"), 16)
                mm(bank[t % 2][:, :], w1[0][:, 128 * t:128 * t + 128], yt[:], start=True, stop=True)\
                    .then_inc(sem("sa_mm"), 1)
                mm(bank[2 + t % 2][:, :], w2[0][:, 128 * t:128 * t + 128], yt[:], start=True, stop=True)\
                    .then_inc(sem("sb_mm"), 1)

            def shared_down(t):
                m = 128 if t < HT - 1 else H_LAST
                if t == 0:
                    pe.wait_ge(sem("w3_in0"), 32)
                pe.wait_ge(sem("hs_ready"), t + 1)
                return mm(bank[7][:, :], w3[0][0:m, t, :], hs[0:m, t % 3, :], start=False, stop=False,
                          skip_group_check=True)

            def places():
                pe.wait_ge(sem("chosen_ready"), 1)
                flat = chosen_bf[:].rearrange("p t e -> p (t e)")
                mm(bank[6][:, 0:NT * E3], earlier_bf[:], flat, start=True, stop=False, skip_group_check=True)
                for t in range(NT - 1):
                    mm(bank[6][:, E3 * (t + 1):E3 * NT].rearrange("p (t e) -> p t e", e=E3), ones_bf[:],
                       chosen_bf[:, t, :].unsqueeze(1).broadcast_to([128, NT - 1 - t, E3]),
                       start=False, stop=False, skip_group_check=True)
                for t in range(NT):
                    last = mm(bank[6][:, E3 * NT:E3 * NT + E3], ones_bf[:], chosen_bf[:, t, :],
                              start=False, stop=(t == NT - 1), skip_group_check=True)
                last.then_inc(sem("places_mm"), 1)

            def gather(p, k, first=False):
                e = pe.value_load(plan_int[0:1, 0, bass.ds(k, 1)], min_val=0, max_val=E3 - 1)
                pe.wait_ge(sem("pick_ready"), k + 1)
                if not first:
                    pe.wait_ge(sem("xe_ready"), k)
                for t in range(NT):
                    for part in range(3):
                        mm(bank[4][:, 0:SLOTS], y_bf[:, t, part, :], pick_bf[:, p, t, :],
                           start=(t == 0 and part == 0), stop=(t == NT - 1 and part == 2))
                for t in range(NT):
                    last = mm(bank[4][:, SLOTS:SLOTS + 3], pick_bf[:, p, t, :],
                              weight_bf[:, t, bass.ds(e, 1), :].rearrange("p e w -> p (e w)"),
                              start=(t == 0), stop=(t == NT - 1))
                last.then_inc(sem("xe_mm"), 1)
                if not first:
                    pe.wait_ge(sem("spread_ready"), k + 1)
                for t in range(NT):
                    last = mm(bank[6][:, 128 * t:128 * t + 128], pick_bf[:, p, t, :], ident_bf[:], start=True, stop=True)
                last.then_inc(sem("spread_mm"), 1)

            def scatter(p):
                mm(bank[7][:, :], ye_hi[:, p, :], spread[:, p, :], start=False, stop=False, skip_group_check=True)
                return mm(bank[7][:, :], ye_lo[:, p, :], spread[:, p, :], start=False, stop=False, skip_group_check=True)

            for t in range(HT):
                shared_up(t)
                if t == 1:
                    for q in range(NT):
                        mm(bank[7][:, 128 * q:128 * q + 128], t5[:, q, :], ident[:], start=(q == 0), stop=False,
                           skip_group_check=True)
                if t >= 1:
                    shared_down(t - 1).then_inc(sem("shared_down"), 1)
                if t == 3:
                    places()
            pe.wait_ge(sem("y_bf_ready"), 1)
            gather(1, 0, first=True)
            shared_down(HT - 1).then_inc(sem("down_mm"), 1)

            def compute(p, k, uses):
                pe.wait_ge(sem(f"w1_in{p}"), 16 * uses)
                pe.wait_ge(sem(f"w2_in{p}"), 16 * uses)
                pe.wait_ge(sem("xe_ready"), k + 1)
                for g, (t0, t1) in enumerate(GROUPS):
                    slot = (3 * (1 - p) + g) % 2
                    pe.wait_ge(sem("he_ready"), 3 * k + g + 1)
                    for w, b, name in ((w1, slot, "a3_mm"), (w2, 2 + slot, "b3_mm")):
                        for t in range(t0, t1):
                            last = mm(bank[b][:, SLOTS * (t - t0):SLOTS * (t - t0 + 1)],
                                      w[p][:, 128 * t:128 * t + 128], xe[:, p, :], start=True, stop=True)
                        last.then_inc(sem(name), 1)
                    if g == 0:
                        pe.wait_ge(sem("ye_ready"), k + 1)
                        pe.wait_ge(sem("spread_ready"), k + 1)
                        scatter(1 - p).then_inc(sem("scatter_mm"), 1)
                gather(1 - p, k + 1)
                pe.wait_ge(sem(f"w3_in{p}"), 32 * uses)
                for t in range(HT):
                    for g, (t0, _) in enumerate(GROUPS):
                        if t == t0:
                            pe.wait_ge(sem("he_ready"), CREDIT + 3 * k + g + 1)
                    m = 128 if t < HT - 1 else H_LAST
                    last = mm(bank[5][:, 0:C], he[0:m, p, t, :], w3[p][0:m, t, :], start=(t == 0), stop=(t == HT - 1))
                last.then_inc(sem("down_mm"), 1)

            n_pairs = pe.value_load(pairs_int[0:1, 0:1], min_val=MIN_CHUNKS // 2, max_val=PAIRS)
            with pe.Fori(0, n_pairs) as i:
                compute(1, 2 * i, i + 1)
                compute(0, 2 * i + 1, i + 2)
            single = pe.value_load(pairs_int[0:1, 1:2], min_val=0, max_val=1)
            with pe.If(single > 0):
                compute(1, 2 * n_pairs, n_pairs + 1)
                pe.wait_ge(sem("ye_ready"), 2 * n_pairs + 2)
                scatter(1).then_inc(sem("out_mm"), 1)
            with pe.If(single < 1):
                pe.wait_ge(sem("ye_ready"), 2 * n_pairs + 1)
                scatter(0).then_inc(sem("out_mm"), 1)

        @block.scalar
        def _(act):
            act.sem_inc(sem("h2_ready"), 2 * CREDIT)
            act.sem_inc(sem("spread_ready"), 1)

            def copy(dst, src):
                return nc.scalar.activation(dst, src, ACT.Copy)

            act.wait_ge(sem("conv_in"), 16)
            act.wait_ge(sem("q0_mm"), 1)
            nc.scalar.activation(q0[:], bank[0][0:C8, :], ACT.Identity, bias=cc("bq")[0:C8, :]).then_inc(sem("q0_ready"), 1)
            act.wait_ge(sem("x0T_mm"), 1)
            copy(x0T[:].rearrange("p t c -> p (t c)"), bank[3][:, :]).then_inc(sem("x0T_ready"), 1)
            for b in range(B):
                act.wait_ge(sem("nmax0_ready"), b + 1)
                for t in range(2):
                    nc.scalar.activation(p0[:, b, t, :], bank[4 + b][:, PIX * t:PIX * t + PIX], ACT.Exp,
                                         bias=nmax0[:, b, t:t + 1], accum_out=sum0[:, b, t:t + 1])\
                        .then_inc(sem("exp0"), 1)
            act.wait_ge(sem("minc_ready"), 1)
            for b in range(B):
                nc.scalar.activation(pc[:, b, :], bank[6][:, C * b:C * b + C], ACT.Exp, bias=minc[:, b:b + 1], scale=-1.0,
                                     accum_out=sumc[:, b:b + 1]).then_inc(sem("expc"), 1)
            for b in range(B):
                act.wait_ge(sem("p0T_mm"), b + 1)
                copy(p0T[:, b, :, :].rearrange("p t n -> p (t n)"), bank[b][:, :]).then_inc(sem("p0T_ready"), 1)
            nc.scalar.activation(nothing[:], ones[0:1, 0:1], ACT.Sqrt).then_inc(sem("act_prepared0"), 1)
            act.wait_ge(sem("act_prepared0"), 1)
            act.wait_ge(sem("gvar_ready"), 1)
            nc.scalar.activation(gr[:, 0, :], gvar[:], ACT.Sqrt).then_inc(sem("gsd_ready"), 1)

            def prepare(func):
                nc.scalar.activation(nothing[:], ones[0:1, 0:1], func).then_inc(sem("act_prepared"), 1)
                prepared[0] += 1
                act.wait_ge(sem("act_prepared"), prepared[0])

            prepared = [0]

            def deviation(k):
                prepare(ACT.Sqrt)
                act.wait_ge(sem("lmv_ready"), k + 1)
                nc.scalar.activation(lsd[:, k, :], lmv[:, k, :, 1], ACT.Sqrt, bias=eps[:]).then_inc(sem("lsd_ready"), 1)

            def ln_copy(k, b):
                for half in range(2):
                    act.wait_ge(sem("yT_mm"), NT * turn_of(k) + 2 * half + 2)
                    copy(yT[k][:, PIX * half:PIX * half + PIX], bank[b + half][:, 0:PIX])\
                        .then_inc(sem("yT_ready"), 1)

            deviation(LN_ATT2)
            ln_copy(LN_ATT2, 4)
            for b in range(B):
                last = copy(t2[:, 2 * b:2 * b + 2, :].rearrange("p t c -> p (t c)"), bank[7 if b else 3][:, 0:PIX])
            last.then_inc(sem("t2_ready"), 1)
            prepare(ACT.Exp)
            for b in range(B):
                act.wait_ge(sem("knmax_ready"), 1)
                nc.scalar.activation(ek[:, b, :], bank[0][:, PIX * b:PIX * b + PIX], ACT.Exp, bias=knmax[:, b:b + 1],
                                     accum_out=sek[:, b:b + 1]).then_inc(sem("ek_ready"), 1)
            act.wait_ge(sem("ekT_mm"), 1)
            copy(ekT[:].rearrange("p t c -> p (t c)"), bank[3][:, :]).then_inc(sem("ekT_ready"), 1)
            act.wait_ge(sem("qs_ready"), 1)
            nc.scalar.activation(eq[:].rearrange("p t c -> p (t c)"), qs[:].rearrange("p g c -> p (g c)"), ACT.Exp)\
                .then_inc(sem("eq_ready"), 1)
            act.wait_ge(sem("eqT_mm"), 1)
            copy(eqT[:], bank[3][:, :]).then_inc(sem("eqT_ready"), 1)
            act.wait_ge(sem("num2_mm"), 1)
            copy(num2[:], bank[6][:, :]).then_inc(sem("num2_ready"), 1)

            deviation(LN_FFN2)
            ln_copy(LN_FFN2, 4)
            act.wait_ge(sem("lg2_ready"), 1)
            nc.scalar.activation(e2[:], lg2[:], ACT.Exp).then_inc(sem("e2_ready"), 1)
            prepare(ACT.Gelu)
            with act.Fori(0, E2 // STEPS2) as i:
                for p in range(STEPS2):
                    e = STEPS2 * i + p
                    act.wait_ge(sem(f"ew2_in{p}"), 16 * i + 16)
                    act.wait_ge(sem("expert2_mm"), e + 1)
                    for half in range(2):
                        h = 2 * (p % 2) + half
                        act.wait_ge(sem("hidden2_mm"), 2 * e + half + 1)
                        nc.scalar.activation(h2[:, h, :], bank[4 + h][:, :], ACT.Gelu,
                                             bias=ew2[p][:, 4 * C + half:4 * C + half + 1]).then_inc(sem("h2_ready"), 1)
            act.wait_ge(sem("comb2T_mm"), 1)
            copy(comb2T[:], bank[0][0:E2, :]).then_inc(sem("comb2T_ready"), 1)

            deviation(LN_ATT3)
            ln_copy(LN_ATT3, 2)

            def queries(s):
                act.wait_ge(sem("q3_mm"), s + 1)
                nc.scalar.activation(q3[s][:], bank[4 + 2 * s][:, :], ACT.Identity, bias=c3("gl"[s] + "_bq"))\
                    .then_inc(sem("q3_ready"), 1)

            prepare(ACT.Exp)
            queries(0)
            act.wait_ge(sem("masks_made"), 1)

            def local_keys(heads):
                for h in heads:
                    nc.scalar.activation(km3[1][0][:, h, :], k3[1][:, 0:PIX], ACT.Copy, scale=head_mask[:, h:h + 1])\
                        .then_inc(sem("km3_local0"), 1)

            def exps(u):
                kind = UNITS[u][0]
                n = GLOBAL_HEADS if kind == "g" else LOCAL_HEADS
                m = 512 // n
                act.wait_ge(sem("nmax3_ready"), u + 1)
                if u >= 2:
                    act.wait_ge(sem("p3T_mm"), u - 1)
                if kind == "e":
                    nc.scalar.activation(p3[0:EDGE, u % 2, 0:EDGE_K], bank[u % 2][0:EDGE, 0:EDGE_K], ACT.Exp,
                                         bias=nmax3[0:EDGE, u, 0:1]).then_inc(sem("exp3"), 1)
                    return
                for h in range(n):
                    last = nc.scalar.activation(p3[:, u % 2, m * h:m * h + m], bank[u % 2][:, m * h:m * h + m], ACT.Exp,
                                                bias=nmax3[:, u, h:h + 1])
                last.then_inc(sem("exp3"), 1)

            def copy_out(n):
                act.wait_ge(sem("attend3"), (n // 2) * UNITS_B + (UNITS_B if n % 2 else UNITS_G))
                if n >= 2:
                    act.wait_ge(sem("ob3_ready"), n - 1)
                copy(o3[:, n % 2, :], bank[4 + n % 2][:, :]).then_inc(sem("o3_copied"), 1)

            for u in range(len(UNITS)):
                exps(u)
                if u == 1:
                    queries(1)
                    act.wait_ge(sem("k3_ready"), 2)
                if 2 <= u <= HEADS // 2 + 1:
                    local_keys(range(2 * u - 4, 2 * u - 2))
                for n, end in enumerate((UNITS_G, UNITS_B, UNITS_B + UNITS_G)):
                    if u == end + 2:
                        copy_out(n)
            copy_out(3)

            deviation(LN_MID3)
            ln_copy(LN_MID3, 5)
            for f in range(FT):
                act.wait_ge(sem("ff3_mm"), f + 1)
                nc.scalar.activation(hf3[:, f, :], bank[1 + f][:, :], ACT.Relu, bias=c3("ffn_b1")[:, f:f + 1])\
                    .then_inc(sem("hf3_ready"), 1)
            deviation(LN_END3)

            deviation(LN_FFN3)
            ln_copy(LN_FFN3, 5)
            act.wait_ge(sem("lg3_ready"), 1)
            nc.scalar.activation(e3[:], lg3[:], ACT.Exp).then_inc(sem("e3_ready"), 1)
            for t in range(HT):
                act.wait_ge(sem("sa_mm"), t + 1)
                if t >= 2:
                    act.wait_ge(sem("hs_ready"), t - 1)
                nc.scalar.activation(silu[:, t % 2, :], bank[t % 2][:, :], ACT.Silu).then_inc(sem("s_silu"), 1)

            def copy_turned_choice(p, k):
                act.wait_ge(sem("scatter_mm"), k + 1)
                act.wait_ge(sem("spread_mm"), k + 2)
                copy(spread[:, p, :], bank[6][:, :]).then_inc(sem("spread_ready"), 1)

            def activate(p, k):
                for g, (t0, t1) in enumerate(GROUPS):
                    slot = (3 * (1 - p) + g) % 2
                    n = SLOTS * (t1 - t0)
                    act.wait_ge(sem("a3_mm"), 3 * k + g + 1)
                    act.wait_ge(sem("he_ready"), 3 * k + g + 1)
                    nc.scalar.activation(silu[:, slot, 0:n], bank[slot][:, 0:n], ACT.Silu)\
                        .then_inc(sem("silu_ready"), 1)
                copy_turned_choice(1 - p, k + 1)
                act.wait_ge(sem("xe_ready"), k + 1)
                act.wait_ge(sem("down_mm"), k + 3)
                nc.scalar.activation(ye_hi[:, p, :], bank[5][:, 0:C], ACT.Copy, scale=slot_weight[:, p:p + 1])\
                    .then_inc(sem("ye_hi_ready"), 1)

            act.wait_ge(sem("plan_ready"), 1)
            copy_turned_choice(1, 0)
            n_pairs = act.value_load(pairs_int[0:1, 0:1], min_val=MIN_CHUNKS // 2, max_val=PAIRS)
            with act.Fori(0, n_pairs) as i:
                activate(1, 2 * i)
                activate(0, 2 * i + 1)
            single = act.value_load(pairs_int[0:1, 1:2], min_val=0, max_val=1)
            with act.If(single > 0):
                activate(1, 2 * n_pairs)

        @block.vector
        def _(dve):
            tt = nc.vector.tensor_tensor
            ts = nc.vector.tensor_scalar
            stt = nc.vector.scalar_tensor_tensor
            done = [0]

            def note(ins):
                done[0] += 1
                ins.then_inc(sem("dve_step"), 1)

            def settle(ins=None):
                if ins is not None:
                    note(ins)
                dve.wait_ge(sem("dve_step"), done[0])

            def flat(x):
                return x.rearrange("p a b -> p (a b)")

            dve.sem_inc(sem("y2_added"), CREDIT)
            dve.sem_inc(sem("he_ready"), CREDIT)
            dve.sem_inc(sem("ye_ready"), 1)
            dve.wait_ge(sem("conv_in"), 16)
            dve.wait_ge(sem("rows_in"), 16)
            note(tt(mix[:, 0:1], cc("alpha"), cc("gamma_pos"), ALU.mult))
            note(tt(mix[:, 1:2], cc("beta"), cc("gamma_chan"), ALU.mult))
            note(stt(mix[:, 2:3], cc("alpha"), 1.0, cc("beta"), ALU.add, ALU.add))
            settle(stt(mask_w[:], cc("filter"), 1.0, cc("mask_weight"), ALU.is_equal, ALU.mult))
            note(ts(mask_w[:], mask_w[:], -2.0 / (SIDE - 1), None, ALU.mult))
            dve.wait_ge(sem("k0_mm"), 1)
            ts(k0[:], bank[1][0:C8, :], cc("bk")[0:C8, :], None, ALU.add).then_inc(sem("k0_ready"), 1)
            dve.wait_ge(sem("v0_mm"), 1)
            tt(v0T[:], bank[2][:, :].rearrange("p (t c) -> p t c", t=NT), row("bv", NT), ALU.add)\
                .then_inc(sem("v0_ready"), 1)
            for b in range(B):
                dve.wait_ge(sem("energy_mm"), b + 1)
                nc.vector.tensor_reduce(nmax0[:, b, :], bank[4 + b][:, :].rearrange("p (t n) -> p t n", t=2), AX.X,
                                        ALU.max, negate=True).then_inc(sem("nmax0_ready"), 1)
            dve.wait_ge(sem("energyc_mm"), 1)
            nc.vector.tensor_reduce(minc[:], bank[6][:, 0:B * C].rearrange("p (b n) -> p b n", b=B), AX.X, ALU.min)\
                .then_inc(sem("minc_ready"), 1)
            for b in range(B):
                dve.wait_ge(sem("exp0"), 2 * b + 2)
                settle(nc.vector.reciprocal(sum0[:, b, :], sum0[:, b, :]))
                settle(ts(sum0[:, b, :], sum0[:, b, :], mix[:, 0:1], None, ALU.mult))
                for t in range(2):
                    ts(p0[:, b, t, :], p0[:, b, t, :], sum0[:, b, t:t + 1], None, ALU.mult).then_inc(sem("p0_ready"), 2)
            dve.wait_ge(sem("expc"), B)
            settle(nc.vector.reciprocal(sumc[:], sumc[:]))
            settle(ts(sumc[:], sumc[:], mix[:, 1:2], None, ALU.mult))
            for b in range(B):
                ts(pc[:, b, :], pc[:, b, :], sumc[:, b:b + 1], None, ALU.mult).then_inc(sem("pc_ready"), 1)
            dve.wait_ge(sem("pcT_mm"), 1)
            nc.vector.tensor_copy(flat(pcT[:]), bank[2][:, 0:B * C]).then_inc(sem("pcT_ready"), 1)
            for b in range(B):
                dve.wait_ge(sem("layer0_mm"), b + 1)
                settle(stt(x1[:, b, :], x0[:, b, :], mix[:, 2:3], bank[7 - 4 * b][:, 0:PIX], ALU.mult, ALU.add))
                settle(nc.vector.bn_stats(gst[:, b, :], x1[:, b, :]))
                note(nc.vector.bn_aggr(gmv[:, b, :], gst[:, b, :]))
            settle()
            dve.sem_inc(sem("gmv_ready"), 1)
            dve.wait_ge(sem("group_made"), 1)
            for b in range(B):
                grid = x1[:, b, :].rearrange("p (h w) -> p h w", h=SIDE)
                note(nc.vector.tensor_reduce(sums[:, 0, b, :], grid, AX.X, ALU.add))
                note(nc.vector.tensor_reduce(sums[:, 1, b, :], grid.rearrange("p h w -> p w h"), AX.X, ALU.add))
            dve.wait_ge(sem("gmean_mm"), 1)
            note(tt(gdev[:], gmv[:, :, 0], bank[0][:, 0:B], ALU.subtract))
            settle(nc.vector.tensor_copy(gm[:], bank[0][:, 0:B]))
            settle(tt(gdev[:], gdev[:], gdev[:], ALU.mult))
            tt(gdev[:], gdev[:], gmv[:, :, 1], ALU.add).then_inc(sem("gdev_ready"), 1)
            note(nc.vector.tensor_reduce(total[:], sums[:, 0, :, :], AX.X, ALU.add))
            settle(tt(weighted[:].rearrange("p k b h -> p (k b) h"), sums[:].rearrange("p k b h -> p (k b) h"),
                      ramp[:].unsqueeze(1).broadcast_to([128, 2 * B, SIDE]), ALU.mult))
            dve.wait_ge(sem("gvar_mm"), 1)
            ts(gvar[:], bank[1][:, 0:B], EPS, None, ALU.add).then_inc(sem("gvar_ready"), 1)
            settle(nc.vector.tensor_reduce(moment[:], weighted[:], AX.X, ALU.add))
            note(stt(total[:], gm[:], -float(PIX), total[:], ALU.mult, ALU.add))
            note(stt(moment[:], gm[:].unsqueeze(1).broadcast_to([128, 2, B]), -float(SIDE * sum(range(SIDE + 1))),
                     moment[:], ALU.mult, ALU.add))
            dve.wait_ge(sem("gsd_ready"), 1)

            def newton(r, r0, sd, v, tmp):
                settle(nc.vector.reciprocal(r0, sd))
                settle(tt(tmp, r0, r0, ALU.mult))
                settle(stt(tmp, tmp, -0.5, v, ALU.mult, ALU.mult))
                settle(stt(r, tmp, 1.5, r0, ALU.add, ALU.mult))

            dve.wait_ge(sem("gvar_ready"), 1)
            newton(gr[:, 2, :], gr[:, 1, :], gr[:, 0, :], gvar[:], gr[:, 3, :])
            for b in range(B):
                note(ts(gn[:, b, :, :].rearrange("p h w -> p (h w)"), x1[:, b, :], gm[:, b:b + 1], gr[:, 2, b:b + 1],
                        ALU.subtract, ALU.mult))
            r = gr[:, 2, :]
            note(tt(moment[:], moment[:], r.unsqueeze(1).broadcast_to([128, 2, B]), ALU.mult))
            settle(tt(total[:], total[:], r, ALU.mult))
            settle(ts(total[:], total[:], 1e-9, None, ALU.max))
            settle(nc.vector.reciprocal(total[:], total[:]))
            settle(tt(mu[:], moment[:], total[:].unsqueeze(1).broadcast_to([128, 2, B]), ALU.mult))
            settle(ts(mu[:], mu[:], 1.0, float(SIDE), ALU.max, ALU.min))
            settle(ts(mu[:], mu[:], ROUND, ROUND, ALU.add, ALU.subtract))
            d = dist[:].rearrange("p k b h -> p (k b) h")
            settle(tt(d, ramp[:].unsqueeze(1).broadcast_to([128, 2 * B, SIDE]),
                      mu[:].rearrange("p k b -> p (k b)").unsqueeze(2).broadcast_to([128, 2 * B, SIDE]), ALU.subtract))
            settle(stt(d, d, -1.0, d, ALU.mult, ALU.max))
            note(ts(dist[:, 0, :, :], dist[:, 0, :, :], mask_w[:], 1.0, ALU.mult, ALU.add))
            settle(ts(dist[:, 1, :, :], dist[:, 1, :, :], mask_w[:], None, ALU.mult))
            dve.wait_ge(sem("pad_made"), 1)
            for b in range(B):
                settle(tt(mask[:, b, :, :], dist[:, 0, b, :].unsqueeze(2).broadcast_to([128, SIDE, SIDE]),
                          dist[:, 1, b, :].unsqueeze(1).broadcast_to([128, SIDE, SIDE]), ALU.add))
                settle(stt(mask[:, b, :, :], mask[:, b, :, :], -1.0, gn[:, b, :, :], ALU.max, ALU.mult))
                ts(pad[:, b, 1:1 + SIDE, 1:1 + SIDE], mask[:, b, :, :], 0.0, None, ALU.max).then_inc(sem("pad_ready"), 1)

            def add_conv(b):
                dve.wait_ge(sem("conv_mm"), b + 1)
                stt(x2[:, b, :], bank[1 if b else 2][:, 0:PIX], cc("conv_bias"), x1[:, b, :], ALU.add, ALU.add)\
                    .then_inc(sem("x2_ready"), 1)

            def tiles_of(x):
                return lambda t: x[:, t, :]

            def measure(k, src, tiles, gain=None):
                for t in tiles:
                    note(nc.vector.bn_stats(lst[:, t, :], src(t)))
                settle()
                for t in tiles:
                    last = nc.vector.bn_aggr(lmv[:, k, t, :], lst[:, t, :])
                if tiles[-1] == NT - 1:
                    last.then_inc(sem("lmv_ready"), 1)
                    dve.wait_ge(sem("lmv_ready"), k + 1)
                    note(ts(lve[:, k, :], lmv[:, k, :, 1], EPS, None, ALU.add))
                else:
                    settle(last)
                if gain is not None:
                    for t in tiles:
                        note(stt(z3[:, t, :], src(t), lmv[:, k, t, 0:1], gain, ALU.subtract, ALU.mult))

            def normalise(k, src, gain=None, shift=None, out=None, measured=0):
                measure(k, src, range(measured, NT), gain)
                settle()
                dve.wait_ge(sem("lsd_ready"), k + 1)
                newton(lr[:, k, :], lr0[:, k, :], lsd[:, k, :], lve[:, k, :], lra[:, k % 2, :])
                for t in range(NT):
                    if gain is None:
                        ins = ts(y[k][:, t, :], src(t), lmv[:, k, t, 0:1], lr[:, k, t:t + 1], ALU.subtract, ALU.mult)
                    else:
                        ins = stt((y[k] if out is None else out)[:, t, :], z3[:, t, :], lr[:, k, t:t + 1], shift(t),
                                  ALU.mult, ALU.add)
                    if out is None:
                        ins.then_inc(sem("y_ready"), 1)
                    else:
                        note(ins)
                if out is not None:
                    settle()

            def turned_x2(t):
                return bank[7 if t >= 2 else 3][:, 128 * (t % 2):128 * (t % 2) + 128]

            add_conv(0)
            dve.wait_ge(sem("t2_mm"), 1)
            measure(LN_ATT2, turned_x2, range(NT // B))
            add_conv(1)
            dve.wait_ge(sem("t2_mm"), B)
            normalise(LN_ATT2, turned_x2, measured=NT // B)
            dve.wait_ge(sem("att_in"), 16)
            dve.wait_ge(sem("k2_mm"), 1)
            settle(nc.vector.tensor_reduce(kmax[:], bank[0][:, :].rearrange("p (b n) -> p b n", b=B), AX.X, ALU.max))
            ts(knmax[:], kmax[:], -1.0, None, ALU.mult).then_inc(sem("knmax_ready"), 1)
            settle(ts(kq[:], kmax[:], ca("bK"), ca("bQ"), ALU.add, ALU.add))
            dve.wait_ge(sem("ident_made"), 1)
            for b in range(B):
                ts(kqb[:, b, :], ones[:], kq[:, b:b + 1], None, ALU.mult).then_inc(sem("kqb_ready"), 1)
            dve.wait_ge(sem("v2_mm"), 1)
            tt(v2[:], bank[2][:, :].rearrange("p (t c) -> p t c", t=NT), row("bV", NT), ALU.add).then_inc(sem("v2_ready"), 1)
            dve.wait_ge(sem("q2_mm"), 1)
            settle(nc.vector.tensor_reduce(qmax[:], bank[1][:, :].rearrange("p (g c) -> p g c", c=HD), AX.X, ALU.max))
            tt(qs[:], bank[1][:, :].rearrange("p (g c) -> p g c", c=HD),
               qmax[:].unsqueeze(2).broadcast_to([128, NT * HEADS, HD]), ALU.subtract).then_inc(sem("qs_ready"), 1)
            dve.wait_ge(sem("masks_made"), 1)
            dve.wait_ge(sem("ek_ready"), B)
            for b in range(B):
                last = ts(ksum[:, b, :], head_mask[:], sek[:, b:b + 1], None, ALU.mult)
            last.then_inc(sem("kv_ready"), 1)
            dve.wait_ge(sem("kv_mm"), 1)
            tt(kv[:], bank[5][:, 0:B * C].rearrange("p (b c) -> p b c", b=B),
               head_block[:].unsqueeze(1).broadcast_to([128, B, C]), ALU.mult).then_inc(sem("kv_ready"), 1)
            dve.wait_ge(sem("t2_ready"), 1)
            note(tt(t2[:], t2[:], row("bO", NT), ALU.add))
            dve.wait_ge(sem("den2_mm"), 1)
            settle(nc.vector.reciprocal(rd2[:], bank[4][:, 0:NT * HEADS]))
            nc.vector.tensor_copy(rden2[:].rearrange("p t h c -> p (t h) c"),
                                  rd2[:].unsqueeze(2).broadcast_to([128, NT * HEADS, HD])).then_inc(sem("rden2_ready"), 1)
            dve.wait_ge(sem("spread2_mm"), 1)
            dve.wait_ge(sem("num2_ready"), 1)
            for b in range(B):
                part = slice(PIX * b, PIX * b + PIX)
                tt(heads2[:, part], bank[7][:, part], num2[:, part], ALU.mult).then_inc(sem("heads2_ready"), 1)
            dve.wait_ge(sem("att2_mm"), 1)
            settle(tt(flat(t3[:]), bank[0][:, :], flat(t2[:]), ALU.add))

            normalise(LN_FFN2, tiles_of(t3))

            def logits(lg, b, n, bias, m):
                settle(tt(lg[:], bank[b][:, 0:NT * n].rearrange("p (t e) -> p t e", e=n), row(bias, NT), ALU.add))
                settle(nc.vector.tensor_reduce(m[:], lg[:], AX.X, ALU.max))
                return tt(lg[:], lg[:], m[:].unsqueeze(2).broadcast_to([128, NT, n]), ALU.subtract)

            def tiles(x, n):
                return x.rearrange("p (t e) f -> p t e f", t=NT)

            def compare(x, cmp, n):
                other = x[:].unsqueeze(2).broadcast_to([128, NT, n, n])
                own = x[:].unsqueeze(3).broadcast_to([128, NT, n, n])
                note(tt(tiles(cmp[:, 0, :, :], n), other, own, ALU.is_gt))
                settle(tt(tiles(cmp[:, 1, :, :], n), other, own, ALU.is_equal))

            def precede(cmp, earlier, n):
                settle(tt(tiles(cmp[:, 1, :, :], n), tiles(cmp[:, 1, :, :], n),
                          earlier[:].unsqueeze(1).broadcast_to([128, NT, n, n]), ALU.mult))
                settle(tt(cmp[:, 0, :, :], cmp[:, 0, :, :], cmp[:, 1, :, :], ALU.add))

            def rank(out, cmp):
                settle(nc.vector.tensor_reduce(out[:].rearrange("p t e -> p (t e)"), cmp[:, 0, :, :], AX.X, ALU.add))

            dve.wait_ge(sem("route2_mm"), 1)
            logits(lg2, 1, E2, "br", m2).then_inc(sem("lg2_ready"), 1)
            dve.wait_ge(sem("e2_ready"), 1)
            settle(nc.vector.tensor_reduce(s2[:], e2[:], AX.X, ALU.add))
            settle(nc.vector.reciprocal(s2[:], s2[:]))
            settle(tt(pr2[:], e2[:], s2[:].unsqueeze(2).broadcast_to([128, NT, E2]), ALU.mult))
            compare(pr2, cmp2, E2)
            precede(cmp2, before2, E2)
            rank(rank2, cmp2)
            stt(comb2[:], rank2[:], 2.0, pr2[:], ALU.is_lt, ALU.mult).then_inc(sem("comb2_ready"), 1)
            dve.wait_ge(sem("comb2_ready"), 1)
            nc.vector.tensor_copy(t4[:], t3[:]).then_inc(sem("t4_added"), 1)
            with dve.Fori(0, E2 // STEPS2) as i:
                for p in range(STEPS2):
                    e = STEPS2 * i + p
                    dve.wait_ge(sem("expert2_mm"), CREDIT + e + 1)
                    dve.wait_ge(sem("t4_added"), e + 1)
                    for t in range(NT):
                        last = stt(t4[:, t, :], bank[2 + p % 2][:, 128 * t:128 * t + 128],
                                   comb2[:, t, bass.ds(e, 1)], t4[:, t, :], ALU.mult, ALU.add)
                    last.then_inc(sem("t4_added"), 1)
                    dve.wait_ge(sem("t4_added"), e + 2)
                    dve.sem_inc(sem("y2_added"), 1)
            dve.wait_ge(sem("bias2_mm"), 1)
            settle(tt(flat(t4[:]), bank[1][:, :], flat(t4[:]), ALU.add))

            normalise(LN_ATT3, tiles_of(t4))
            dve.wait_ge(sem("y_ready"), NT * turn_of(LN_ATT3) + NT)
            settle(tt(u3[:], y[LN_ATT3][:], row("g_out_b", NT), ALU.add))
            note(tt(u3[:], u3[:], row("l_out_b", NT), ALU.add))
            dve.wait_ge(sem("l3_in"), 16)

            def keys(s):
                dve.wait_ge(sem("k3_mm"), s + 1)
                ts(k3[s][:], bank[5 + 2 * s][:, :], c3("gl"[s] + "_bk"), HD ** -0.5, ALU.add, ALU.mult)\
                    .then_inc(sem("k3_ready"), 1)

            keys(0)
            dve.wait_ge(sem("k3_ready"), 1)

            def global_keys(heads):
                for h in heads:
                    ts(km3[0][0][:, h, :], k3[0][:, 0:PIX], head_mask[:, h:h + 1], None, ALU.mult)\
                        .then_inc(sem("km3_global0"), 1)

            global_keys(range(2 * GLOBAL_HEADS))

            def values(dst, src, side, n):
                bias = row(side + "_bv").rearrange("p (h c) -> p h c", h=HEADS)
                return tt(dst, src.rearrange("p (t h c) -> p t h c", t=n, h=HEADS),
                          bias.unsqueeze(1).broadcast_to([128, n, HEADS, HD]), ALU.add)

            dve.wait_ge(sem("vg_mm"), 1)
            values(vg[:, :, :, 0:HD], bank[2][:, :], "g", NT).then_inc(sem("v3_ready"), 1)

            def edge_queries():
                dve.wait_ge(sem("q3_ready"), 2)
                edge = WINDOWS[1][1]
                tt(q_edge[:], q3[1][:].rearrange("p (b n) -> p b n", b=B)[:, :, edge:edge + EDGE_Q].unsqueeze(3)
                   .broadcast_to([128, B, EDGE_Q, HEADS]),
                   head_mask[:].unsqueeze(1).unsqueeze(1).broadcast_to([128, B, EDGE_Q, HEADS]), ALU.mult)\
                    .then_inc(sem("q_edge_ready"), 1)

            def local_values():
                nw = len(WINDOWS)
                dve.wait_ge(sem("vl_mm"), 1)
                for b in range(B):
                    last = values(vl[:, nw * b:nw * b + nw, :, 0:HD], bank[4 + b][:, 0:nw * C], "l", nw)
                last.then_inc(sem("v3_ready"), 1)

            def largest(u):
                kind = UNITS[u][0]
                n = GLOBAL_HEADS if kind == "g" else LOCAL_HEADS
                dve.wait_ge(sem("score3_mm"), u + 1)
                if kind == "e":
                    nc.vector.tensor_reduce(nmax3[0:EDGE, u, 0:1], bank[u % 2][0:EDGE, 0:EDGE_K], AX.X, ALU.max,
                                            negate=True).then_inc(sem("nmax3_ready"), 1)
                    return
                nc.vector.tensor_reduce(nmax3[:, u, 0:n], bank[u % 2][:, :].rearrange("p (h n) -> p h n", h=n),
                                        AX.X, ALU.max, negate=True).then_inc(sem("nmax3_ready"), 1)

            def copy_turned(u):
                dve.wait_ge(sem("p3T_mm"), u + 1)
                if u >= 2:
                    dve.wait_ge(sem("attend3"), u - 1)
                if UNITS[u][0] == "e":
                    nc.vector.tensor_copy(p3T[0:EDGE_K, u % 2, 0:EDGE], bank[2 + u % 2][0:EDGE_K, 0:EDGE])\
                        .then_inc(sem("p3T_ready"), 1)
                    return
                nc.vector.tensor_copy(p3T[:, u % 2, :], bank[2 + u % 2][:, :]).then_inc(sem("p3T_ready"), 1)

            def invert(n):
                dve.wait_ge(sem("den3_mm"), n + 1)
                if n:
                    dve.wait_ge(sem("spread3_mm"), n)
                settle(nc.vector.reciprocal(rd3[:], bank[6][:, 0:16]))
                nc.vector.tensor_copy(rd3_wide[:].rearrange("p q j c -> p (q j) c"),
                                      rd3[:].unsqueeze(2).broadcast_to([128, 16, 32])).then_inc(sem("rd3_ready"), 1)

            def divide(n):
                dve.wait_ge(sem("spread3_mm"), n + 1)
                tt(ob3[:, n // 2, n % 2, :, :].rearrange("p h q -> p (h q)"), bank[6][:, :], o3[:, n % 2, :], ALU.mult)\
                    .then_inc(sem("ob3_ready"), 1)

            for u in range(len(UNITS) + 2):
                if u < len(UNITS):
                    largest(u)
                if u < HEADS // GLOBAL_HEADS - 2:
                    global_keys(range((u + 2) * GLOBAL_HEADS, (u + 3) * GLOBAL_HEADS))
                if u == 1:
                    keys(1)
                    local_values()
                if u == 4:
                    edge_queries()
                if u >= 2:
                    copy_turned(u - 2)
                for n, end in enumerate((UNITS_G, UNITS_B, UNITS_B + UNITS_G)):
                    if u == end + 4:
                        invert(n)
                    if u == end + 5:
                        divide(n)

            def add_attention(b):
                own = u3[:, 2 * b:2 * b + 2, :]
                dve.wait_ge(sem("att3_mm"), b + 1)
                settle(tt(flat(own), bank[4 if b else 7][:, 0:PIX], flat(own), ALU.add))

            add_attention(0)
            measure(LN_MID3, tiles_of(u3), range(NT // B), gain=row("ln1_g"))
            invert(3)
            divide(3)
            add_attention(1)

            normalise(LN_MID3, tiles_of(u3), gain=row("ln1_g"), shift=lambda t: row("ln1_b"), measured=NT // B)
            dve.wait_ge(sem("y_ready"), NT * turn_of(LN_MID3) + NT)
            settle(tt(u3[:], y[LN_MID3][:], row("ffn_b2", NT), ALU.add))
            note(tt(t4[:], t4[:], row("ln2_b", NT), ALU.add))
            for b in range(B):
                own = u3[:, 2 * b:2 * b + 2, :]
                dve.wait_ge(sem("ffn3_mm"), b + 1)
                settle(tt(flat(own), bank[0 if b else 6][:, 0:PIX], flat(own), ALU.add))
                if b == 0:
                    measure(LN_END3, tiles_of(u3), range(NT // B), gain=row("ln2_g"))
            normalise(LN_END3, tiles_of(u3), gain=row("ln2_g"), shift=lambda t: t4[:, t, :], out=t5, measured=NT // B)

            normalise(LN_FFN3, tiles_of(t5))
            dve.wait_ge(sem("route3_mm"), 1)
            logits(lg3, 4, E3, "routing_bias", m3).then_inc(sem("lg3_ready"), 1)
            dve.wait_ge(sem("lg3_ready"), 1)
            def shared(t):
                dve.wait_ge(sem("sb_mm"), t + 1)
                dve.wait_ge(sem("s_silu"), t + 1)
                if t >= 3:
                    dve.wait_ge(sem("shared_down"), t - 2)
                tt(hs[:, t % 3, :], bank[2 + t % 2][:, :], silu[:, t % 2, :], ALU.mult).then_inc(sem("hs_ready"), 1)

            def weigh():
                dve.wait_ge(sem("e3_ready"), 1)
                settle(tt(weight[:], e3[:], chosen[:], ALU.mult))
                settle(nc.vector.tensor_reduce(s3[:], weight[:], AX.X, ALU.add))
                settle(nc.vector.reciprocal(s3[:], s3[:]))
                settle(tt(weight[:], weight[:], s3[:].unsqueeze(2).broadcast_to([128, NT, E3]), ALU.mult))
                settle(nc.vector.tensor_copy(weight_bf[:, :, :, 0], weight[:]))
                settle(tt(left[:], weight[:], weight_bf[:, :, :, 0], ALU.subtract))
                settle(nc.vector.tensor_copy(weight_bf[:, :, :, 1], left[:]))
                note(tt(weight_bf[:, :, :, 2], left[:], weight_bf[:, :, :, 1], ALU.subtract))

            def find_places():
                dve.wait_ge(sem("places_mm"), 1)
                settle(stt(place[:], bank[6][:, 0:NT * E3].rearrange("p (t e) -> p t e", e=E3), 1.0, chosen[:],
                           ALU.add, ALU.mult))
                note(ts(place[:], place[:], -1.0, None, ALU.add))
                settle(nc.vector.tensor_copy(count[:], bank[6][:, E3 * NT:E3 * NT + E3]))
                settle(ts(chunks[:], count[:], 0.0, None, ALU.is_gt))
                for n in range(1, BLOCKS):
                    settle(stt(chunks[:], count[:], float(n * SLOTS), chunks[:], ALU.is_gt, ALU.add))
                settle(tt(cmp3[:, 0, 0:E3, :], before[:], chunks[:].unsqueeze(1).broadcast_to([128, E3, E3]), ALU.mult))
                settle(nc.vector.tensor_reduce(first[:], cmp3[:, 0, 0:E3, :], AX.X, ALU.add))

            def order_chunks():
                settle(tt(pairs[:, 0:1], first[:, E3 - 1:E3], chunks[:, E3 - 1:E3], ALU.add))
                settle(ts(pairs[:, 1:2], pairs[:, 0:1], 0.5, -0.25, ALU.mult, ALU.add))
                settle(ts(pairs[:, 2:3], pairs[:, 1:2], ROUND, ROUND, ALU.add, ALU.subtract))
                settle(stt(pairs[:, 3:4], pairs[:, 2:3], -2.0, pairs[:, 0:1], ALU.mult, ALU.add))
                note(nc.vector.tensor_copy(pairs_int[:], pairs[0:1, 2:4]))
                by_pair = plan[:, 4, :].rearrange("p (i l) -> p i l", l=2)
                settle(stt(by_pair, chunk_odd[:], pairs[:, 2:3], chunk_half[:], ALU.mult, ALU.add))
                settle(ts(pairs[:, 4:5], pairs[:, 2:3], 2.0, None, ALU.mult))
                settle(ts(plan[:, 0, :], chunk_no[:], pairs[:, 4:5], None, ALU.is_ge))
                settle(tt(plan[:, 1, :], chunk_no[:], plan[:, 4, :], ALU.subtract))
                settle(tt(plan[:, 1, :], plan[:, 1, :], plan[:, 0, :], ALU.mult))
                settle(tt(plan[:, 4, :], plan[:, 4, :], plan[:, 1, :], ALU.add))

            def plan_experts():
                settle(tt(reach[:], plan[:, 4, :].unsqueeze(2).broadcast_to([128, NK, E3]),
                          first[:].unsqueeze(1).broadcast_to([128, NK, E3]), ALU.is_ge))
                settle(nc.vector.tensor_reduce(plan[:, 0, :], reach[:], AX.X, ALU.add))
                note(ts(plan[:, 0, :], plan[:, 0, :], -1.0, None, ALU.add))

            def plan_blocks():
                settle(tt(reach[:], reach[:], first[:].unsqueeze(1).broadcast_to([128, NK, E3]), ALU.mult))
                settle(nc.vector.tensor_reduce(plan[:, 3, :], reach[:], AX.X, ALU.max))
                note(tt(plan[:, 2, 2:NK], plan[:, 0, 2:NK], plan[:, 0, 0:NK - 2], ALU.not_equal))
                settle(tt(plan[:, 1, :], plan[:, 4, :], plan[:, 3, :], ALU.subtract))
                settle(ts(plan[:, 1, :], plan[:, 1, :], float(BLOCKS), float(SLOTS), ALU.min, ALU.mult))
                settle(nc.vector.tensor_copy(plan_int[:], plan[0:1, 0:3, :]))
                dve.sem_inc(sem("plan_ready"), 1)

            def choose(p, k):
                e = dve.value_load(plan_int[0:1, 0, bass.ds(k, 1)], min_val=0, max_val=E3 - 1)
                at = dve.value_load(plan_int[0:1, 1, bass.ds(k, 1)], min_val=0, max_val=BLOCKS * SLOTS)
                for t in range(NT):
                    last = ts(pick_bf[:, p, t, :], slot_no[:, bass.ds(at, SLOTS)], place[:, t, bass.ds(e, 1)], None,
                              ALU.is_equal)
                last.then_inc(sem("pick_ready"), 1)

            def copy_tokens(p, k, first=False):
                dve.wait_ge(sem("xe_mm"), k + 1)
                if not first:
                    dve.wait_ge(sem("ye_ready"), k)
                nc.vector.tensor_reduce(slot_weight[:, p:p + 1], bank[4][:, SLOTS:SLOTS + 3], AX.X, ALU.add)
                nc.vector.tensor_copy(xe[:, p, :], bank[4][:, 0:SLOTS]).then_inc(sem("xe_ready"), 1)

            def multiply(p, k):
                dve.wait_ge(sem("down_mm"), k + 1)
                for g, (t0, t1) in enumerate(GROUPS):
                    slot = (3 * (1 - p) + g) % 2
                    n = SLOTS * (t1 - t0)
                    dve.wait_ge(sem("b3_mm"), 3 * k + g + 1)
                    dve.wait_ge(sem("silu_ready"), 3 * k + g + 1)
                    tt(he[:, p, t0:t1, :].rearrange("p t s -> p (t s)"), bank[2 + slot][:, 0:n], silu[:, slot, 0:n],
                       ALU.mult).then_inc(sem("he_ready"), 1)
                    if g == 0:
                        dve.wait_ge(sem("spread_mm"), k + 1)
                        choose(1 - p, k + 1)
                copy_tokens(1 - p, k + 1)
                dve.wait_ge(sem("ye_hi_ready"), k + 1)
                stt(ye_lo[:, p, :], bank[5][:, 0:C], slot_weight[:, p:p + 1], ye_hi[:, p, :], ALU.mult, ALU.subtract)\
                    .then_inc(sem("ye_ready"), 1)

            for part in (spread, ye_hi, ye_lo):
                note(ts(part[:, 0, :], slot_no[:, 0:part.shape[2]], 0.0, None, ALU.mult))
            note(nc.vector.memset(plan[:, 2, 0:2], 0.0))
            compare(lg3, cmp3, E3)
            shared(0)
            precede(cmp3, before, E3)
            shared(1)
            rank(rank3, cmp3)
            settle(ts(chosen[:], rank3[:], float(K3), None, ALU.is_lt))
            nc.vector.tensor_copy(chosen_bf[:], chosen[:]).then_inc(sem("chosen_ready"), 1)
            shared(2)
            weigh()
            shared(3)
            find_places()
            shared(4)
            order_chunks()
            shared(5)
            plan_experts()
            shared(6)
            plan_blocks()
            shared(7)
            choose(1, 0)
            for t in range(8, HT):
                shared(t)
            copy_tokens(1, 0, first=True)
            n_pairs = dve.value_load(pairs_int[0:1, 0:1], min_val=MIN_CHUNKS // 2, max_val=PAIRS)
            with dve.Fori(0, n_pairs) as i:
                multiply(1, 2 * i)
                multiply(0, 2 * i + 1)
            single = dve.value_load(pairs_int[0:1, 1:2], min_val=0, max_val=1)
            with dve.If(single > 0):
                multiply(1, 2 * n_pairs)
            dve.wait_ge(sem("out_mm"), 1)
            nc.vector.tensor_copy(flat(outT[:]), bank[7][:, :]).then_inc(sem("out_ready"), 1)


def launch_arrays(inputs):
    import numpy as np

    a = {k: np.asarray(v) for k, v in inputs.items()}

    def pack(at, n, parts):
        out = np.zeros((128, n), np.float32)
        for name, (first, count) in at.items():
            v = parts[name]
            out[0:v.shape[0], first:first + count] = v
        return out

    def col(v, n=1):
        return v.reshape(n, -1).T

    def scalar(v):
        return np.broadcast_to(v.reshape(1, 1), (128, 1))

    conv = pack(CONV_AT, CONV_N, {
        "wq": a["L0_conv_wq"].T, "wk": a["L0_conv_wk"].T, "wv": a["L0_conv_wv"].T,
        "bq": col(a["L0_conv_bq"]), "bk": col(a["L0_conv_bk"]),
        "gamma_pos": scalar(a["L0_conv_gamma_pos"]), "gamma_chan": scalar(a["L0_conv_gamma_chan"]),
        "alpha": scalar(a["L0_conv_alpha"]), "beta": scalar(a["L0_conv_beta"]),
        "conv_bias": col(a["L1_conv_bias"]), "mask_weight": col(a["L1_conv_mask_weight"]),
        "filter": a["L1_conv_filter"].reshape(C, 1)})
    att = pack(ATT_AT, ATT_N, {
        "WQ": a["L2_attn_W_Q"].T, "WK": a["L2_attn_W_K"].T, "WV": a["L2_attn_W_V"].T, "WO": a["L2_attn_W_O"].T,
        "bQ": col(a["L2_attn_b_Q"]), "bK": col(a["L2_attn_b_K"]), "Wr": a["L2_ffn_Wr"].T})
    experts2 = np.concatenate([
        a["L2_ffn_W1"], a["L2_ffn_W2"].reshape(E2, 2, 128, C).transpose(0, 2, 1, 3).reshape(E2, 128, 2 * C),
        a["L2_ffn_b1"].reshape(E2, 2, 128).transpose(0, 2, 1)], axis=2)

    def spread_heads(v):
        out = np.zeros((2, 4, 32, v.shape[1]), np.float32)
        out[:, :, 0:HD, :] = v.reshape(2, 4, HD, v.shape[1])
        return out.reshape(2, 128, v.shape[1]).transpose(1, 0, 2).reshape(128, 2 * v.shape[1])

    parts = {"ffn1": a["L3_attn_ffn_w1"].T,
             "ffn2": a["L3_attn_ffn_w2"].T.reshape(FT, 128, C).transpose(1, 0, 2).reshape(128, FT * C),
             "ffn_b1": col(a["L3_attn_ffn_b1"], FT), "gate": a["L3_ffn_gate_w"]}
    for s in "gl":
        w, b = a[f"L3_attn_{s}_in_w"], a[f"L3_attn_{s}_in_b"]
        parts |= {f"{s}_in": w.T, f"{s}_out": spread_heads(a[f"L3_attn_{s}_out_w"].T), f"{s}_bq": col(b[0:C]),
                  f"{s}_bk": col(b[C:2 * C])}
    l3 = pack(L3_AT, L3_N, parts)
    rows = {"bv": "L0_conv_bv", "bV": "L2_attn_b_V", "bO": "L2_attn_b_O", "br": "L2_ffn_br", "g_out_b": "L3_attn_g_out_b",
            "l_out_b": "L3_attn_l_out_b", "ffn_b2": "L3_attn_ffn_b2", "ln1_g": "L3_attn_ln1_g",
            "ln1_b": "L3_attn_ln1_b", "ln2_g": "L3_attn_ln2_g", "ln2_b": "L3_attn_ln2_b",
            "routing_bias": "L3_ffn_routing_bias"}
    return {
        "x": a["x"].reshape(B, C, PIX),
        "conv": conv,
        "taps": a["L1_conv_weight"].transpose(1, 2, 3, 0).reshape(C, 9, C),
        "att": att,
        "experts2": experts2,
        "b2": a["L2_ffn_b2"],
        "l3": l3,
        "rows": np.concatenate([a[f"L3_attn_{name[0]}_in_b"][2 * C:] if name in ("g_bv", "l_bv") else a[rows[name]]
                                for name, _ in ROWS]),
        "sw1": a["L3_ffn_sw1"], "sw2": a["L3_ffn_sw2"], "sw3": a["L3_ffn_sw3"],
        "w1": a["L3_ffn_w1"], "w2": a["L3_ffn_w2"], "w3": a["L3_ffn_w3"],
    }


def kernel(**inputs):
    import numpy as np
    import concourse.bacc as bacc
    from concourse.bass_utils import run_bass_kernel_spmd

    nc = bacc.Bacc("TRN2", target_bir_lowering=False, num_devices=1)
    arrays = {f"in_{k}": np.ascontiguousarray(v) for k, v in launch_arrays(inputs).items()}
    args = [nc.dram_tensor(k, v.shape, mybir.dt.from_np(v.dtype), kind="ExternalInput").ap() for k, v in arrays.items()]
    out = nc.dram_tensor("out", (B, C, PIX), F32, kind="ExternalOutput").ap()
    build(nc, *args, out)
    got = run_bass_kernel_spmd(nc, [arrays], core_ids=[0])
    return got.results[0]["out"].reshape(B, C, SIDE, SIDE)
```
